# Optimizing a Trainium2 kernel written in Bass

```python
import numpy as np
import jax
import jax.numpy as jnp

def _softmax(x, axis=-1):
    return jax.nn.softmax(x, axis=axis)

def _gelu(x):
    return jax.nn.gelu(x, approximate=True)

def _silu(x):
    return jax.nn.silu(x)

def _sigmoid(x):
    return jax.nn.sigmoid(x)

def _layernorm(x, axis=-1, eps=1e-05):
    m = jnp.mean(x, axis=axis, keepdims=True)
    v = jnp.var(x, axis=axis, keepdims=True)
    return (x - m) / jnp.sqrt(v + eps)

def _scatter_add(tgt, idx, src, axis=0):
    return tgt.at[idx].add(src)

def _segment_sum(src, seg, n):
    return jax.ops.segment_sum(src, seg, n)
kernel_name = 'mk_hybrid_d2_jaxref_r8_51fdc7'

def setup_inputs(seed: int=0):
    np.random.seed(seed)
    _w = jnp.asarray

    def _L0_attn_a_setup():
        import jax, jax.numpy as jnp
        import numpy as np
        LN_EPS = 1e-05
        NEG_INF = -1e+38

        def _layer_norm(x, g, b):
            mu = x.mean(-1, keepdims=True)
            var = ((x - mu) ** 2).mean(-1, keepdims=True)
            return (x - mu) * jax.lax.rsqrt(var + LN_EPS) * g + b

        def _wkv(w, u, k, v):
            B, T, C = k.shape
            kt = jnp.swapaxes(k, 0, 1)
            vt = jnp.swapaxes(v, 0, 1)
            aa0 = jnp.zeros((B, C), k.dtype)
            bb0 = jnp.zeros((B, C), k.dtype)
            pp0 = jnp.full((B, C), NEG_INF, k.dtype)

            def step(carry, inp):
                aa, bb, pp = carry
                kk, vv = inp
                p = jnp.maximum(pp, u + kk)
                e1 = jnp.exp(pp - p)
                e2 = jnp.exp(u + kk - p)
                y = (e1 * aa + e2 * vv) / (e1 + e2)
                p2 = jnp.maximum(pp + w, w + kk)
                e1u = jnp.exp(pp + w - p2)
                e2u = jnp.exp(w + kk - p2)
                aa2 = e1u * aa + e2u * vv
                bb2 = e1u + e2u
                pp2 = p2 + jnp.log(bb2)
                return ((aa2, bb2, pp2), y)
            _, ys = jax.lax.scan(step, (aa0, bb0, pp0), (kt, vt))
            return jnp.swapaxes(ys, 0, 1)

        def _shift(h):
            return jnp.pad(h[:, :-1, :], ((0, 0), (1, 0), (0, 0)))
        key = jax.random.key(seed)
        B, T, C = (8, 256, 128)
        ks = jax.random.split(key, 12)
        s = 0.02
        return {'x': jax.random.normal(ks[0], (B, T, C), jnp.float32), 'time_decay': jax.random.normal(ks[1], (C,), jnp.float32) * 0.01, 'time_first': jax.random.normal(ks[2], (C,), jnp.float32) * 0.01, 'w_tk': jax.random.normal(ks[3], (C, C), jnp.float32) * s, 'w_tv': jax.random.normal(ks[4], (C, C), jnp.float32) * s, 'w_tr': jax.random.normal(ks[5], (C, C), jnp.float32) * s, 'w_ck': jax.random.normal(ks[6], (C, 4 * C), jnp.float32) * s, 'w_cv': jax.random.normal(ks[7], (4 * C, C), jnp.float32) * s, 'w_cr': jax.random.normal(ks[8], (C, C), jnp.float32) * s, 'ln1_g': jnp.ones((C,), jnp.float32), 'ln1_b': jnp.zeros((C,), jnp.float32), 'ln2_g': jnp.ones((C,), jnp.float32), 'ln2_b': jnp.zeros((C,), jnp.float32), 'mix_k': jnp.ones((1, 1, C), jnp.float32), 'mix_v': jnp.ones((1, 1, C), jnp.float32), 'mix_r': jnp.ones((1, 1, C), jnp.float32), 'cmix_k': jnp.ones((1, 1, C), jnp.float32), 'cmix_r': jnp.ones((1, 1, C), jnp.float32)}
    _L0_attn_a_in = _L0_attn_a_setup()

    def _L0_attn_b_setup():
        import jax, jax.numpy as jnp
        import numpy as np
        B, S, D = (4, 256, 128)
        SCALE = 1.0 / np.sqrt(D)
        key = jax.random.key(seed)
        k1, k2, k3 = jax.random.split(key, 3)
        x = jax.random.normal(k1, (B, S, D), dtype=jnp.float32)
        bound = 1.0 / np.sqrt(D)
        W_qk = jax.random.uniform(k2, (D, D), minval=-bound, maxval=bound, dtype=jnp.float32)
        W_v = jax.random.uniform(k3, (D, D), minval=-bound, maxval=bound, dtype=jnp.float32)
        alibi_slope = jnp.full((1,), 0.5, dtype=jnp.float32)
        return {'x': x, 'W_qk': W_qk, 'W_v': W_v, 'alibi_slope': alibi_slope}
    _L0_attn_b_in = _L0_attn_b_setup()

    def _L0_ffn_setup():
        import jax, jax.numpy as jnp
        import numpy as np
        D_MODEL = 128
        NUM_HEADS = 4
        NUM_EXPERTS = 8
        TOP_K = 2
        D_FF = 128
        EPS = 1e-06

        def _rmsnorm(x, g):
            return x * jax.lax.rsqrt(jnp.mean(x * x, axis=-1, keepdims=True) + EPS) * g

        def _swiglu(x, w1, w2, w3):
            return jax.nn.silu(x @ w1.T) * (x @ w3.T) @ w2.T
        key = jax.random.key(seed)
        ks = jax.random.split(key, 16)
        d, e, f = (D_MODEL, NUM_EXPERTS, D_FF)
        dc = d // 4
        s = 0.02
        return {'X': jax.random.normal(ks[0], (2, 128, d), dtype=jnp.float32), 'g1': jnp.ones((d,), jnp.float32), 'g2': jnp.ones((d,), jnp.float32), 'Wq': jax.random.normal(ks[1], (d, d), jnp.float32) * s, 'Wkc': jax.random.normal(ks[2], (dc, d), jnp.float32) * s, 'Wvc': jax.random.normal(ks[3], (dc, d), jnp.float32) * s, 'Wo': jax.random.normal(ks[4], (d, d), jnp.float32) * s, 'Wr': jax.random.normal(ks[5], (e, d), jnp.float32) * s, 'expert_bias': jnp.zeros((e,), jnp.float32), 'sW1': jax.random.normal(ks[6], (f, d), jnp.float32) * s, 'sW2': jax.random.normal(ks[7], (d, f), jnp.float32) * s, 'sW3': jax.random.normal(ks[8], (f, d), jnp.float32) * s, 'eW1': jax.random.normal(ks[9], (e, f, d), jnp.float32) * s, 'eW2': jax.random.normal(ks[10], (e, d, f), jnp.float32) * s, 'eW3': jax.random.normal(ks[11], (e, f, d), jnp.float32) * s}
    _L0_ffn_in = _L0_ffn_setup()

    def _L1_attn_a_setup():
        import jax, jax.numpy as jnp
        import numpy as np
        B, S, DIM = (2, 1024, 128)
        NH, NKV, HD = (16, 4, 64)
        GROUPS = NH // NKV
        CHUNK = 128
        THETA = 10000.0

        def _slopes(h):
            return jnp.asarray([2.0 ** (-8.0 / h * (i + 1)) for i in range(h)], dtype=jnp.float32)

        def _rope_tables(s, d):
            inv = 1.0 / THETA ** (np.arange(0, d, 2, dtype=np.float64) / d)
            freqs = np.outer(np.arange(s, dtype=np.float64), inv)
            emb = np.concatenate([freqs, freqs], axis=-1)
            return (jnp.asarray(np.cos(emb), jnp.float32), jnp.asarray(np.sin(emb), jnp.float32))

        def _apply_rope(x, cos, sin):
            x1, x2 = jnp.split(x, 2, axis=-1)
            rot = jnp.concatenate([-x2, x1], axis=-1)
            return x * cos + rot * sin

        def _lightning_attn(q, k, v, slopes, chunk):
            b, h, s, d = q.shape
            nc = s // chunk
            t = jnp.arange(chunk, dtype=jnp.float32)
            sl = slopes[:, None, None]
            mask = jnp.where(t[:, None] >= t[None, :], jnp.exp(-sl * (t[:, None] - t[None, :])), 0.0)
            q_dec = jnp.exp(-slopes[:, None] * (t + 1.0))[..., None]
            k_dec = jnp.exp(-slopes[:, None] * (chunk - 1.0 - t))[..., None]
            blk_dec = jnp.exp(-slopes * chunk)[None, :, None, None]

            def to_chunks(x):
                return x.reshape(b, h, nc, chunk, d).transpose(2, 0, 1, 3, 4)
            qc, kc, vc = (to_chunks(q), to_chunks(k), to_chunks(v))

            def step(kv, inp):
                qi, ki, vi = inp
                scores = jnp.einsum('bhtd,bhsd->bhts', qi, ki) * mask
                o = jnp.einsum('bhts,bhsd->bhtd', scores, vi) + jnp.einsum('bhtd,bhde->bhte', qi * q_dec, kv)
                kv = blk_dec * kv + jnp.einsum('bhtd,bhte->bhde', ki * k_dec, vi)
                return (kv, o)
            kv0 = jnp.zeros((b, h, d, d), q.dtype)
            _, outs = jax.lax.scan(step, kv0, (qc, kc, vc))
            return outs.transpose(1, 2, 0, 3, 4).reshape(b, h, s, d)
        key = jax.random.key(seed)
        k0, k1, k2, k3, k4 = jax.random.split(key, 5)
        x = jax.random.normal(k0, (B, S, DIM), jnp.float32)
        Wq = jax.random.normal(k1, (NH * HD, DIM), jnp.float32) * 0.02
        Wk = jax.random.normal(k2, (NKV * HD, DIM), jnp.float32) * 0.02
        Wv = jax.random.normal(k3, (NKV * HD, DIM), jnp.float32) * 0.02
        Wo = jax.random.normal(k4, (DIM, NH * HD), jnp.float32) * 0.02
        return {'x': x, 'Wq': Wq, 'Wk': Wk, 'Wv': Wv, 'Wo': Wo}
    _L1_attn_a_in = _L1_attn_a_setup()

    def _L1_attn_b_setup():
        import jax, jax.numpy as jnp
        import numpy as np
        EMBED_DIM = 128
        NUM_HEADS = 16
        EFF_HEADS = NUM_HEADS // 2
        HEAD_DIM = EMBED_DIM // NUM_HEADS
        LAMBDA_INIT = 0.8
        B, N = (2, 256)
        key = jax.random.key(seed)
        ks = jax.random.split(key, 14)
        s = 0.02
        return {'x': jax.random.normal(ks[0], (B, N, EMBED_DIM), dtype=jnp.float32), 'Wq': jax.random.normal(ks[1], (EMBED_DIM, EMBED_DIM), dtype=jnp.float32) * s, 'bq': jnp.zeros((EMBED_DIM,), dtype=jnp.float32), 'Wk': jax.random.normal(ks[2], (EMBED_DIM, EMBED_DIM), dtype=jnp.float32) * s, 'bk': jnp.zeros((EMBED_DIM,), dtype=jnp.float32), 'Wv': jax.random.normal(ks[3], (EMBED_DIM, EMBED_DIM), dtype=jnp.float32) * s, 'bv': jnp.zeros((EMBED_DIM,), dtype=jnp.float32), 'Wp': jax.random.normal(ks[4], (EMBED_DIM, EMBED_DIM), dtype=jnp.float32) * s, 'bp': jnp.zeros((EMBED_DIM,), dtype=jnp.float32), 'lambda_q1': jax.random.normal(ks[5], (EFF_HEADS, 1, HEAD_DIM), dtype=jnp.float32) * s, 'lambda_k1': jax.random.normal(ks[6], (EFF_HEADS, 1, HEAD_DIM), dtype=jnp.float32) * s, 'lambda_q2': jax.random.normal(ks[7], (EFF_HEADS, 1, HEAD_DIM), dtype=jnp.float32) * s, 'lambda_k2': jax.random.normal(ks[8], (EFF_HEADS, 1, HEAD_DIM), dtype=jnp.float32) * s}
    _L1_attn_b_in = _L1_attn_b_setup()

    def _L1_ffn_setup():
        import jax, jax.numpy as jnp
        import numpy as np
        B, S, D = (4, 256, 128)
        E, H, TOP_K = (8, 256, 2)
        key = jax.random.key(seed)
        k_x, k_g, k_w1, k_w2, k_w3 = jax.random.split(key, 5)
        s_d = 1.0 / np.sqrt(D)
        s_h = 1.0 / np.sqrt(H)
        return {'x': jax.random.normal(k_x, (B, S, D), dtype=jnp.float32), 'w_gate': jax.random.normal(k_g, (D, E), dtype=jnp.float32) * s_d, 'w1': jax.random.normal(k_w1, (E, D, H), dtype=jnp.float32) * s_d, 'w3': jax.random.normal(k_w3, (E, D, H), dtype=jnp.float32) * s_d, 'w2': jax.random.normal(k_w2, (E, H, D), dtype=jnp.float32) * s_h}
    _L1_ffn_in = _L1_ffn_setup()
    _d = {'L0_attn_a_x': _L0_attn_a_in['x'], 'L0_attn_a_time_decay': _L0_attn_a_in['time_decay'], 'L0_attn_a_time_first': _L0_attn_a_in['time_first'], 'L0_attn_a_w_tk': _L0_attn_a_in['w_tk'], 'L0_attn_a_w_tv': _L0_attn_a_in['w_tv'], 'L0_attn_a_w_tr': _L0_attn_a_in['w_tr'], 'L0_attn_a_w_ck': _L0_attn_a_in['w_ck'], 'L0_attn_a_w_cv': _L0_attn_a_in['w_cv'], 'L0_attn_a_w_cr': _L0_attn_a_in['w_cr'], 'L0_attn_a_ln1_g': _L0_attn_a_in['ln1_g'], 'L0_attn_a_ln1_b': _L0_attn_a_in['ln1_b'], 'L0_attn_a_ln2_g': _L0_attn_a_in['ln2_g'], 'L0_attn_a_ln2_b': _L0_attn_a_in['ln2_b'], 'L0_attn_a_mix_k': _L0_attn_a_in['mix_k'], 'L0_attn_a_mix_v': _L0_attn_a_in['mix_v'], 'L0_attn_a_mix_r': _L0_attn_a_in['mix_r'], 'L0_attn_a_cmix_k': _L0_attn_a_in['cmix_k'], 'L0_attn_a_cmix_r': _L0_attn_a_in['cmix_r'], 'L0_attn_b_W_qk': _L0_attn_b_in['W_qk'], 'L0_attn_b_W_v': _L0_attn_b_in['W_v'], 'L0_attn_b_alibi_slope': _L0_attn_b_in['alibi_slope'], 'L0_ffn_g1': _L0_ffn_in['g1'], 'L0_ffn_g2': _L0_ffn_in['g2'], 'L0_ffn_Wq': _L0_ffn_in['Wq'], 'L0_ffn_Wkc': _L0_ffn_in['Wkc'], 'L0_ffn_Wvc': _L0_ffn_in['Wvc'], 'L0_ffn_Wo': _L0_ffn_in['Wo'], 'L0_ffn_Wr': _L0_ffn_in['Wr'], 'L0_ffn_expert_bias': _L0_ffn_in['expert_bias'], 'L0_ffn_sW1': _L0_ffn_in['sW1'], 'L0_ffn_sW2': _L0_ffn_in['sW2'], 'L0_ffn_sW3': _L0_ffn_in['sW3'], 'L0_ffn_eW1': _L0_ffn_in['eW1'], 'L0_ffn_eW2': _L0_ffn_in['eW2'], 'L0_ffn_eW3': _L0_ffn_in['eW3'], 'L1_attn_a_Wq': _L1_attn_a_in['Wq'], 'L1_attn_a_Wk': _L1_attn_a_in['Wk'], 'L1_attn_a_Wv': _L1_attn_a_in['Wv'], 'L1_attn_a_Wo': _L1_attn_a_in['Wo'], 'L1_attn_b_Wq': _L1_attn_b_in['Wq'], 'L1_attn_b_bq': _L1_attn_b_in['bq'], 'L1_attn_b_Wk': _L1_attn_b_in['Wk'], 'L1_attn_b_bk': _L1_attn_b_in['bk'], 'L1_attn_b_Wv': _L1_attn_b_in['Wv'], 'L1_attn_b_bv': _L1_attn_b_in['bv'], 'L1_attn_b_Wp': _L1_attn_b_in['Wp'], 'L1_attn_b_bp': _L1_attn_b_in['bp'], 'L1_attn_b_lambda_q1': _L1_attn_b_in['lambda_q1'], 'L1_attn_b_lambda_k1': _L1_attn_b_in['lambda_k1'], 'L1_attn_b_lambda_q2': _L1_attn_b_in['lambda_q2'], 'L1_attn_b_lambda_k2': _L1_attn_b_in['lambda_k2'], 'L1_ffn_w_gate': _L1_ffn_in['w_gate'], 'L1_ffn_w1': _L1_ffn_in['w1'], 'L1_ffn_w3': _L1_ffn_in['w3'], 'L1_ffn_w2': _L1_ffn_in['w2']}
    _x0 = _d['L0_attn_a_x']
    _d['L0_attn_a_x'] = jax.random.normal(jax.random.fold_in(jax.random.key(seed), 1), (8, 512, 128), dtype=_x0.dtype)
    del _x0
    return _d

def reference(L0_attn_a_x, L0_attn_a_time_decay, L0_attn_a_time_first, L0_attn_a_w_tk, L0_attn_a_w_tv, L0_attn_a_w_tr, L0_attn_a_w_ck, L0_attn_a_w_cv, L0_attn_a_w_cr, L0_attn_a_ln1_g, L0_attn_a_ln1_b, L0_attn_a_ln2_g, L0_attn_a_ln2_b, L0_attn_a_mix_k, L0_attn_a_mix_v, L0_attn_a_mix_r, L0_attn_a_cmix_k, L0_attn_a_cmix_r, L0_attn_b_W_qk, L0_attn_b_W_v, L0_attn_b_alibi_slope, L0_ffn_g1, L0_ffn_g2, L0_ffn_Wq, L0_ffn_Wkc, L0_ffn_Wvc, L0_ffn_Wo, L0_ffn_Wr, L0_ffn_expert_bias, L0_ffn_sW1, L0_ffn_sW2, L0_ffn_sW3, L0_ffn_eW1, L0_ffn_eW2, L0_ffn_eW3, L1_attn_a_Wq, L1_attn_a_Wk, L1_attn_a_Wv, L1_attn_a_Wo, L1_attn_b_Wq, L1_attn_b_bq, L1_attn_b_Wk, L1_attn_b_bk, L1_attn_b_Wv, L1_attn_b_bv, L1_attn_b_Wp, L1_attn_b_bp, L1_attn_b_lambda_q1, L1_attn_b_lambda_k1, L1_attn_b_lambda_q2, L1_attn_b_lambda_k2, L1_ffn_w_gate, L1_ffn_w1, L1_ffn_w3, L1_ffn_w2):

    def _L0_attn_a_ref(x, time_decay, time_first, w_tk, w_tv, w_tr, w_ck, w_cv, w_cr, ln1_g, ln1_b, ln2_g, ln2_b, mix_k, mix_v, mix_r, cmix_k, cmix_r):
        import jax, jax.numpy as jnp
        import numpy as np
        LN_EPS = 1e-05
        NEG_INF = -1e+38

        def _layer_norm(x, g, b):
            mu = x.mean(-1, keepdims=True)
            var = ((x - mu) ** 2).mean(-1, keepdims=True)
            return (x - mu) * jax.lax.rsqrt(var + LN_EPS) * g + b

        def _wkv(w, u, k, v):
            B, T, C = k.shape
            kt = jnp.swapaxes(k, 0, 1)
            vt = jnp.swapaxes(v, 0, 1)
            aa0 = jnp.zeros((B, C), k.dtype)
            bb0 = jnp.zeros((B, C), k.dtype)
            pp0 = jnp.full((B, C), NEG_INF, k.dtype)

            def step(carry, inp):
                aa, bb, pp = carry
                kk, vv = inp
                p = jnp.maximum(pp, u + kk)
                e1 = jnp.exp(pp - p)
                e2 = jnp.exp(u + kk - p)
                y = (e1 * aa + e2 * vv) / (e1 + e2)
                p2 = jnp.maximum(pp + w, w + kk)
                e1u = jnp.exp(pp + w - p2)
                e2u = jnp.exp(w + kk - p2)
                aa2 = e1u * aa + e2u * vv
                bb2 = e1u + e2u
                pp2 = p2 + jnp.log(bb2)
                return ((aa2, bb2, pp2), y)
            _, ys = jax.lax.scan(step, (aa0, bb0, pp0), (kt, vt))
            return jnp.swapaxes(ys, 0, 1)

        def _shift(h):
            return jnp.pad(h[:, :-1, :], ((0, 0), (1, 0), (0, 0)))
        h = _layer_norm(x, ln1_g, ln1_b)
        hp = _shift(h)
        xk = h * mix_k + hp * (1.0 - mix_k)
        xv = h * mix_v + hp * (1.0 - mix_v)
        xr = h * mix_r + hp * (1.0 - mix_r)
        k = xk @ w_tk
        v = xv @ w_tv
        r = jax.nn.sigmoid(xr @ w_tr)
        y = _wkv(time_decay, time_first, k, v)
        x = x + r * y
        h2 = _layer_norm(x, ln2_g, ln2_b)
        hp2 = _shift(h2)
        ck = h2 * cmix_k + hp2 * (1.0 - cmix_k)
        cr = h2 * cmix_r + hp2 * (1.0 - cmix_r)
        kk = jnp.square(jax.nn.relu(ck @ w_ck))
        x = x + jax.nn.sigmoid(cr @ w_cr) * (kk @ w_cv)
        return x

    def _L0_attn_b_ref(x, W_qk, W_v, alibi_slope):
        import jax, jax.numpy as jnp
        import numpy as np
        B, S, D = (4, 256, 128)
        SCALE = 1.0 / np.sqrt(D)
        seq_len = x.shape[1]
        scores = jnp.einsum('bqe,bke->bqk', x @ W_qk, x) * SCALE
        kpos = jnp.arange(seq_len, dtype=x.dtype)[None, :]
        qpos = jnp.arange(seq_len, dtype=x.dtype)[:, None]
        scores = scores + (kpos - qpos) * alibi_slope[0]
        causal = qpos >= kpos
        scores = jnp.where(causal, scores, -jnp.inf)
        attn = jax.nn.softmax(scores, axis=-1)
        v = x @ W_v.T
        return jnp.einsum('bqk,bkd->bqd', attn, v)

    def _L0_ffn_ref(X, g1, g2, Wq, Wkc, Wvc, Wo, Wr, expert_bias, sW1, sW2, sW3, eW1, eW2, eW3):
        import jax, jax.numpy as jnp
        import numpy as np
        D_MODEL = 128
        NUM_HEADS = 4
        NUM_EXPERTS = 8
        TOP_K = 2
        D_FF = 128
        EPS = 1e-06

        def _rmsnorm(x, g):
            return x * jax.lax.rsqrt(jnp.mean(x * x, axis=-1, keepdims=True) + EPS) * g

        def _swiglu(x, w1, w2, w3):
            return jax.nn.silu(x @ w1.T) * (x @ w3.T) @ w2.T
        B, S, d = X.shape
        H = NUM_HEADS
        dk = d // H
        scale = 1.0 / jnp.sqrt(jnp.float32(dk))
        nx = _rmsnorm(X, g1)
        Q = (nx @ Wq.T).reshape(B, S, H, dk).transpose(0, 2, 1, 3)
        Kc = nx @ Wkc.T
        Vc = nx @ Wvc.T
        scores = jnp.einsum('bhsd,btd->bhst', Q, Kc) * scale
        attn = jax.nn.softmax(scores, axis=-1)
        out = jnp.einsum('bhst,btd->bhsd', attn, Vc)
        out = out.transpose(0, 2, 1, 3).reshape(B, S, d) @ Wo.T
        X = X + out
        nx = _rmsnorm(X, g2)
        xf = nx.reshape(-1, d)
        logits = xf @ Wr.T + expert_bias
        rw = jax.nn.softmax(logits, axis=-1)
        topw, topi = jax.lax.top_k(rw, TOP_K)
        topw = jax.nn.softmax(topw, axis=-1)
        combine = jnp.sum(jax.nn.one_hot(topi, NUM_EXPERTS, dtype=xf.dtype) * topw[..., None], axis=1)
        shared = _swiglu(xf, sW1, sW2, sW3)
        h = jax.nn.silu(jnp.einsum('td,efd->etf', xf, eW1)) * jnp.einsum('td,efd->etf', xf, eW3)
        eo = jnp.einsum('etf,edf->etd', h, eW2)
        specialist = jnp.einsum('te,etd->td', combine, eo)
        moe_out = (shared + specialist).reshape(B, S, d)
        return X + moe_out

    def _L1_attn_a_ref(x, Wq, Wk, Wv, Wo):
        import jax, jax.numpy as jnp
        import numpy as np
        B, S, DIM = (2, 1024, 128)
        NH, NKV, HD = (16, 4, 64)
        GROUPS = NH // NKV
        CHUNK = 128
        THETA = 10000.0

        def _slopes(h):
            return jnp.asarray([2.0 ** (-8.0 / h * (i + 1)) for i in range(h)], dtype=jnp.float32)

        def _rope_tables(s, d):
            inv = 1.0 / THETA ** (np.arange(0, d, 2, dtype=np.float64) / d)
            freqs = np.outer(np.arange(s, dtype=np.float64), inv)
            emb = np.concatenate([freqs, freqs], axis=-1)
            return (jnp.asarray(np.cos(emb), jnp.float32), jnp.asarray(np.sin(emb), jnp.float32))

        def _apply_rope(x, cos, sin):
            x1, x2 = jnp.split(x, 2, axis=-1)
            rot = jnp.concatenate([-x2, x1], axis=-1)
            return x * cos + rot * sin

        def _lightning_attn(q, k, v, slopes, chunk):
            b, h, s, d = q.shape
            nc = s // chunk
            t = jnp.arange(chunk, dtype=jnp.float32)
            sl = slopes[:, None, None]
            mask = jnp.where(t[:, None] >= t[None, :], jnp.exp(-sl * (t[:, None] - t[None, :])), 0.0)
            q_dec = jnp.exp(-slopes[:, None] * (t + 1.0))[..., None]
            k_dec = jnp.exp(-slopes[:, None] * (chunk - 1.0 - t))[..., None]
            blk_dec = jnp.exp(-slopes * chunk)[None, :, None, None]

            def to_chunks(x):
                return x.reshape(b, h, nc, chunk, d).transpose(2, 0, 1, 3, 4)
            qc, kc, vc = (to_chunks(q), to_chunks(k), to_chunks(v))

            def step(kv, inp):
                qi, ki, vi = inp
                scores = jnp.einsum('bhtd,bhsd->bhts', qi, ki) * mask
                o = jnp.einsum('bhts,bhsd->bhtd', scores, vi) + jnp.einsum('bhtd,bhde->bhte', qi * q_dec, kv)
                kv = blk_dec * kv + jnp.einsum('bhtd,bhte->bhde', ki * k_dec, vi)
                return (kv, o)
            kv0 = jnp.zeros((b, h, d, d), q.dtype)
            _, outs = jax.lax.scan(step, kv0, (qc, kc, vc))
            return outs.transpose(1, 2, 0, 3, 4).reshape(b, h, s, d)
        b, s, _ = x.shape
        q = (x @ Wq.T).reshape(b, s, NH, HD).transpose(0, 2, 1, 3)
        k = (x @ Wk.T).reshape(b, s, NKV, HD).transpose(0, 2, 1, 3)
        v = (x @ Wv.T).reshape(b, s, NKV, HD).transpose(0, 2, 1, 3)
        cos, sin = _rope_tables(s, HD)
        q = _apply_rope(q, cos, sin)
        k = _apply_rope(k, cos, sin)
        k = jnp.repeat(k, GROUPS, axis=1)
        v = jnp.repeat(v, GROUPS, axis=1)
        out = _lightning_attn(q, k, v, _slopes(NH), CHUNK)
        out = out.transpose(0, 2, 1, 3).reshape(b, s, NH * HD)
        return out @ Wo.T

    def _L1_attn_b_ref(x, Wq, bq, Wk, bk, Wv, bv, Wp, bp, lambda_q1, lambda_k1, lambda_q2, lambda_k2):
        import jax, jax.numpy as jnp
        import numpy as np
        EMBED_DIM = 128
        NUM_HEADS = 16
        EFF_HEADS = NUM_HEADS // 2
        HEAD_DIM = EMBED_DIM // NUM_HEADS
        LAMBDA_INIT = 0.8
        B, N = (2, 256)
        Bb, Nn, C = x.shape
        H, H2, hd = (NUM_HEADS, EFF_HEADS, HEAD_DIM)
        scale = hd ** (-0.5)
        q = (x @ Wq.T + bq).reshape(Bb, Nn, H, hd).transpose(0, 2, 1, 3)
        k = (x @ Wk.T + bk).reshape(Bb, Nn, H, hd).transpose(0, 2, 1, 3)
        v = (x @ Wv.T + bv).reshape(Bb, Nn, H, hd).transpose(0, 2, 1, 3)
        q1, q2 = (q[:, :H2], q[:, H2:])
        k1, k2 = (k[:, :H2], k[:, H2:])
        v1, v2 = (v[:, :H2], v[:, H2:])
        l1 = jnp.exp(jnp.minimum((lambda_q1 * lambda_k1).sum((-1, -2)), 5.0))
        l2 = jnp.exp(jnp.minimum((lambda_q2 * lambda_k2).sum((-1, -2)), 5.0))
        lv = (l1 - l2 + LAMBDA_INIT).mean()
        a1 = jax.nn.softmax(jnp.einsum('bhnd,bhmd->bhnm', q1, k1) * scale, axis=-1)
        x1 = jnp.einsum('bhnm,bhmd->bhnd', a1, v1).transpose(0, 2, 1, 3).reshape(Bb, Nn, C // 2)
        a2 = jax.nn.softmax(jnp.einsum('bhnd,bhmd->bhnm', q2, k2) * scale, axis=-1)
        x2 = jnp.einsum('bhnm,bhmd->bhnd', a2, v2).transpose(0, 2, 1, 3).reshape(Bb, Nn, C // 2)
        out = jnp.concatenate([x1 - lv * x2, x2], axis=-1) @ Wp.T + bp
        return out

    def _L1_ffn_ref(x, w_gate, w1, w3, w2):
        import jax, jax.numpy as jnp
        import numpy as np
        B, S, D = (4, 256, 128)
        E, H, TOP_K = (8, 256, 2)
        bsz, seq_len, embed_dim = x.shape
        xt = x.reshape(-1, embed_dim)
        T = xt.shape[0]
        logits = xt @ w_gate
        top_logits, sel = jax.lax.top_k(logits, TOP_K)
        probs = jax.nn.softmax(top_logits, axis=-1).astype(x.dtype)
        h = jax.nn.silu(jnp.einsum('td,edh->eth', xt, w1)) * jnp.einsum('td,edh->eth', xt, w3)
        y = jnp.einsum('eth,ehd->etd', h, w2)
        t_idx = jnp.arange(T)
        yk = y[sel.T, t_idx[None, :], :]
        out = jnp.einsum('ktd,tk->td', yk, probs)
        return out.reshape(bsz, seq_len, embed_dim)
    x = L0_attn_a_x
    x = x + _L0_attn_a_ref(_layernorm(x, axis=-1), L0_attn_a_time_decay, L0_attn_a_time_first, L0_attn_a_w_tk, L0_attn_a_w_tv, L0_attn_a_w_tr, L0_attn_a_w_ck, L0_attn_a_w_cv, L0_attn_a_w_cr, L0_attn_a_ln1_g, L0_attn_a_ln1_b, L0_attn_a_ln2_g, L0_attn_a_ln2_b, L0_attn_a_mix_k, L0_attn_a_mix_v, L0_attn_a_mix_r, L0_attn_a_cmix_k, L0_attn_a_cmix_r)
    x = x + _L0_ffn_ref(_layernorm(x, axis=-1), L0_ffn_g1, L0_ffn_g2, L0_ffn_Wq, L0_ffn_Wkc, L0_ffn_Wvc, L0_ffn_Wo, L0_ffn_Wr, L0_ffn_expert_bias, L0_ffn_sW1, L0_ffn_sW2, L0_ffn_sW3, L0_ffn_eW1, L0_ffn_eW2, L0_ffn_eW3)
    x = x + _L0_attn_b_ref(_layernorm(x, axis=-1), L0_attn_b_W_qk, L0_attn_b_W_v, L0_attn_b_alibi_slope)
    x = x + _L0_ffn_ref(_layernorm(x, axis=-1), L0_ffn_g1, L0_ffn_g2, L0_ffn_Wq, L0_ffn_Wkc, L0_ffn_Wvc, L0_ffn_Wo, L0_ffn_Wr, L0_ffn_expert_bias, L0_ffn_sW1, L0_ffn_sW2, L0_ffn_sW3, L0_ffn_eW1, L0_ffn_eW2, L0_ffn_eW3)
    x = x + _L1_attn_a_ref(_layernorm(x, axis=-1), L1_attn_a_Wq, L1_attn_a_Wk, L1_attn_a_Wv, L1_attn_a_Wo)
    x = x + _L1_ffn_ref(_layernorm(x, axis=-1), L1_ffn_w_gate, L1_ffn_w1, L1_ffn_w3, L1_ffn_w2)
    x = x + _L1_attn_b_ref(_layernorm(x, axis=-1), L1_attn_b_Wq, L1_attn_b_bq, L1_attn_b_Wk, L1_attn_b_bk, L1_attn_b_Wv, L1_attn_b_bv, L1_attn_b_Wp, L1_attn_b_bp, L1_attn_b_lambda_q1, L1_attn_b_lambda_k1, L1_attn_b_lambda_q2, L1_attn_b_lambda_k2)
    x = x + _L1_ffn_ref(_layernorm(x, axis=-1), L1_ffn_w_gate, L1_ffn_w1, L1_ffn_w3, L1_ffn_w2)
    return x

_drawn_inputs = setup_inputs


def setup_inputs(seed=0):
    import zlib

    import numpy as np

    out = dict(_drawn_inputs(seed))
    spreads = {'L0_attn_a_ln1_g': (1.0, 0.577),
     'L0_attn_a_ln1_b': (0.0, 0.1),
     'L0_attn_a_ln2_g': (1.0, 0.6),
     'L0_attn_a_ln2_b': (0.0, 0.8),
     'L0_attn_a_mix_k': (1.0, 0.6),
     'L0_attn_a_mix_v': (1.0, 0.6),
     'L0_attn_a_mix_r': (1.0, 0.6),
     'L0_attn_a_cmix_k': (1.0, 0.6),
     'L0_attn_a_cmix_r': (1.0, 0.6),
     'L0_ffn_g1': (1.0, 0.6),
     'L0_ffn_g2': (1.0, 0.6),
     'L0_ffn_expert_bias': (0.0, 0.8),
     'L1_attn_b_bq': (0.0, 0.8),
     'L1_attn_b_bk': (0.0, 2.0),
     'L1_attn_b_bv': (0.0, 0.8),
     'L1_attn_b_bp': (0.0, 1.418)}
    factors = {'L0_attn_a_time_decay': 3.443,
     'L0_attn_a_time_first': 8.0,
     'L0_attn_a_w_tr': 3.19,
     'L0_attn_a_w_ck': 4.566,
     'L0_attn_a_w_cv': 3.853,
     'L0_attn_a_w_cr': 8.0,
     'L0_ffn_Wq': 8.0,
     'L0_ffn_Wkc': 8.0,
     'L0_ffn_Wvc': 8.0,
     'L0_ffn_Wo': 8.0,
     'L0_ffn_Wr': 8.0,
     'L0_ffn_sW1': 7.624,
     'L0_ffn_sW2': 7.16,
     'L0_ffn_sW3': 7.592,
     'L0_ffn_eW1': 8.0,
     'L0_ffn_eW2': 8.0,
     'L0_ffn_eW3': 8.0,
     'L1_attn_b_Wq': 8.0,
     'L1_attn_b_Wk': 8.0,
     'L1_attn_b_Wv': 8.0,
     'L1_attn_b_Wp': 7.209,
     'L1_attn_b_lambda_q1': 64.0,
     'L1_attn_b_lambda_k1': 64.0,
     'L1_attn_b_lambda_q2': 64.0,
     'L1_attn_b_lambda_k2': 64.0}
    for name, (base, spread) in spreads.items():
        noise = np.random.default_rng([zlib.crc32(name.encode()), seed]).standard_normal(out[name].shape)
        drawn = base * np.exp(spread * noise) if base else spread * noise
        out[name] = jnp.asarray(drawn.astype(out[name].dtype))
    for name, factor in factors.items():
        out[name] = (out[name] * factor).astype(out[name].dtype)
    return out
```

```python
from contextlib import ExitStack
import math
import concourse.bass as bass
from concourse import mybir

F32 = mybir.dt.float32
F32R = mybir.dt.float32r
BF16 = mybir.dt.bfloat16
U32 = mybir.dt.uint32
ALU = mybir.AluOpType
ACT = mybir.ActivationFunctionType
AXX = mybir.AxisListType.X

P = 128
NSEQ = 8
T = 512
NQ = T // P
PAIRS = NSEQ // 2
LN_EPS = 1e-5
RMS_EPS = 1e-6
LOG2E = math.log2(math.e)


IN_USE = []


def core_semaphore(nc, name):
    handle = nc.alloc_semaphore(name=name)
    IN_USE.append(handle)
    return handle


def clear_semaphores(nc):
    nc.clear_and_free_semaphores(IN_USE)
    IN_USE.clear()
    nc.all_engine_barrier()


class Steps:

    def __init__(self, nc, ctx, plan, name):
        self.sem = core_semaphore(nc, name)
        self.known = plan.setdefault(name, {})
        self.at = 0

    def start(self):
        self.at = 0

    def step(self, *name):
        place = self.known.setdefault(name, self.at)
        assert place == self.at, (name, place, self.at)
        self.at += 1
        return 1

    def per(self):
        return max(len(self.known), 1)

    def done(self, rep, *name, back=0):
        if name not in self.known:
            return 1
        return (rep + (1 - back)) * self.per() + (self.known[name] + 1)

    def credit(self, engine):
        engine.sem_inc(self.sem, self.per())


def cut(start, size):
    return bass.ds(start, size)


class Core:

    def __init__(self, nc, ctx, plan, dram):
        self.nc, self.plan, self.dram = nc, plan, dram
        self.x = ctx.enter_context(nc.sbuf_tensor("x", [P, NSEQ * T], F32))
        self.x2 = ctx.enter_context(nc.sbuf_tensor("x2", [P, NSEQ * T], F32))
        self.ident = ctx.enter_context(nc.sbuf_tensor("ident", [P, P], F32))
        self.iota = ctx.enter_context(nc.sbuf_tensor("iota", [P, 8], F32))
        self.powers = ctx.enter_context(nc.sbuf_tensor("powers", [P, 2 * 32 + NQ], F32))
        self.psum = ctx.enter_context(nc.psum_tensor("psum", [P, 8, 512], F32))
        self.settled = ctx.enter_context(nc.sbuf_tensor("settled", [P, 2], F32))
        self.eps = self.powers[:, 64:64 + NQ]
        self.half = self.powers[:, 0:NQ]
        self.two = self.powers[:, 32:64]


def load_block(core):
    nc, d = core.nc, core.dram
    with ExitStack() as ctx:
        loaded = core_semaphore(nc, "x_loaded")
        block = ctx.enter_context(nc.Block())

        @block.sync
        def _(sp):
            for b in range(NSEQ):
                sp.dma_start(core.x[:, b * T:(b + 1) * T].rearrange("p (q d) -> p q d", d=P),
                             d["x"][b, :, :].rearrange("(q p) d -> p q d", p=P)).then_inc(loaded, 16)
            sp.dma_start(core.ident[:, :], d["ident"]).then_inc(loaded, 16)
            sp.dma_start(core.iota[:, :], d["iota"]).then_inc(loaded, 16)
            sp.wait_ge(loaded, 16 * (NSEQ + 2))

        @block.gpsimd
        def _(pool):
            pool.memset(core.powers[:, 0:32], -0.5)
            pool.memset(core.powers[:, 32:64], 2.0)
            pool.memset(core.powers[:, 64:64 + NQ], LN_EPS)


def store_block(core):
    nc, d = core.nc, core.dram
    with ExitStack() as ctx:
        stored = core_semaphore(nc, "x_stored")
        block = ctx.enter_context(nc.Block())

        @block.sync
        def _(sp):
            for b in range(NSEQ):
                sp.dma_start(d["out"][b, :, :].rearrange("(q p) d -> p q d", p=P),
                             core.x[:, b * T:(b + 1) * T].rearrange("p (q d) -> p q d", d=P)).then_inc(stored, 16)
            sp.wait_ge(stored, 16 * NSEQ)


def settle(core, engine):
    if engine.engine == core.nc.gpsimd.engine:
        core.nc.gpsimd.tensor_tensor(core.settled[:, 0:1], core.half[:, 0:1], core.half[:, 0:1], ALU.add)
    else:
        core.nc.vector.memset(core.settled[:, 1:2], 0.0)


class Head:

    def __init__(self, core, ctx, name, kind, src, bank, affine=None):
        nc, plan = core.nc, core.plan
        self.core, self.kind, self.src, self.bank = core, kind, src, bank
        self.affine = affine
        self.vec = Steps(nc, ctx, plan, name + "_head_vector")
        self.pool = Steps(nc, ctx, plan, name + "_head_pool")
        self.pe = Steps(nc, ctx, plan, name + "_head_tensor")
        self.act = Steps(nc, ctx, plan, name + "_head_scalar")
        self.low = Steps(nc, ctx, plan, name + "_head_low")
        self.kept = Steps(nc, ctx, plan, name + "_head_kept")
        sb = lambda n, s, t=F32: ctx.enter_context(nc.sbuf_tensor(name + n, s, t))
        self.stats = sb("stats", [P, NQ, 6])
        self.mv = sb("mv", [P, 2, NQ, 2])
        self.var = sb("var", [P, NQ])
        self.rstd = sb("rstd", [P, NQ])
        self.var2 = sb("var2", [P, NQ])
        self.scale = sb("scale", [P, NQ])
        self.z = sb("z", [P, NQ, P])
        self.pad = 1 if affine else 0
        self.hi = sb("hi", [P, 2, self.pad + T], F32R)
        self.lo = sb("lo", [P, 2, self.pad + T], F32R)
        self.full = sb("full", [P, T]) if affine else None
        self.keep = sb("keep", [P, 2, T]) if kind in ("ln2", "lnr") else None

    def start(self):
        for s in (self.vec, self.pool, self.pe, self.act, self.kept, self.low):
            s.start()


    def vector_stats(self, dve, k, par, seq):
        nc, v = self.core.nc, self.vec
        if self.keep is not None and not (isinstance(k, int) and k == 0):
            dve.wait_ge(self.kept.sem, self.kept.done(k - 1, "keep", back=1))
        dve.wait_ge(self.pool.sem, self.pool.done(k, "scale", back=1))
        for q in range(NQ):
            nc.vector.bn_stats(self.stats[:, q, :], self.src[:, cut(seq * T + q * P, P)]).then_inc(v.sem, v.step("stats", q))
        dve.wait_ge(v.sem, v.done(k, "stats", NQ - 1))
        settle(self.core, dve)
        for q in range(NQ):
            nc.vector.bn_aggr(self.mv[:, par, q, :], self.stats[:, q, :]).then_inc(v.sem, v.step("mv", q))

    def pool_scale(self, pool, k, par):
        nc, g, v = self.core.nc, self.pool, self.vec
        pool.wait_ge(v.sem, v.done(k, "mv", NQ - 1))
        settle(self.core, pool)
        var, mean = self.mv[:, par, :, 1], self.mv[:, par, :, 0]
        if self.kind == "rms":
            nc.gpsimd.tensor_tensor(self.var[:, :], mean, mean, ALU.mult).then_inc(g.sem, g.step("sq"))
            pool.wait_ge(g.sem, g.done(k, "sq"))
            nc.gpsimd.tensor_tensor(self.rstd[:, :], self.var[:, :], var, ALU.add).then_inc(g.sem, g.step("ms"))
            pool.wait_ge(g.sem, g.done(k, "ms"))
            settle(self.core, pool)
            nc.gpsimd.tensor_scalar(self.var2[:, :], self.rstd[:, :], RMS_EPS, None, ALU.add).then_inc(g.sem, g.step("var2"))
        elif self.kind == "ln":
            nc.gpsimd.tensor_scalar(self.var2[:, :], var, LN_EPS, None, ALU.add).then_inc(g.sem, g.step("var2"))
        else:
            e2 = LN_EPS if self.kind == "ln2" else RMS_EPS
            nc.gpsimd.tensor_scalar(self.var2[:, :], var, 1.0 + e2, LN_EPS * e2, ALU.mult, ALU.add).then_inc(g.sem, g.step("var2"))
        pool.wait_ge(g.sem, g.done(k, "var2"))
        nc.gpsimd.tensor_tensor(self.scale[:, :], self.var2[:, :], self.core.half, ALU.pow).then_inc(g.sem, g.step("scale"))

    def pool_keep(self, pool, k, par, seq):
        nc, g, v = self.core.nc, self.kept, self.vec
        mean = self.mv[:, par, :, 0]
        nc.gpsimd.tensor_tensor(self.var[:, :], self.mv[:, par, :, 1], self.core.eps, ALU.add).then_inc(g.sem, g.step("var"))
        pool.wait_ge(g.sem, g.done(k, "var"))
        nc.gpsimd.tensor_tensor(self.rstd[:, :], self.var[:, :], self.core.half, ALU.pow).then_inc(g.sem, g.step("rstd"))
        pool.wait_ge(g.sem, g.done(k, "rstd"))
        wide = lambda m: m.unsqueeze(2).to_broadcast([P, NQ, P])
        kept = self.keep[:, par, :].rearrange("p (q d) -> p q d", d=P)
        tokens = self.src[:, cut(seq * T, T)].rearrange("p (q d) -> p q d", d=P)
        nc.gpsimd.tensor_tensor(kept, tokens, wide(mean), ALU.subtract).then_inc(g.sem, g.step("centred"))
        pool.wait_ge(g.sem, g.done(k, "centred"))
        nc.gpsimd.tensor_tensor(kept, kept, wide(self.rstd[:, :]), ALU.mult).then_inc(g.sem, g.step("keep"))

    def vector_z(self, dve, k, par, seq):
        nc, v = self.core.nc, self.vec
        dve.wait_ge(self.pool.sem, self.pool.done(k, "scale"))
        dve.wait_ge(self.pe.sem, self.pe.done(k, "tr", back=1))
        for q in range(NQ):
            src = self.src[:, cut(seq * T + q * P, P)]
            if self.kind == "rms":
                ins = nc.vector.tensor_scalar(self.z[:, q, :], src, self.scale[:, q:q + 1], None, ALU.mult)
            else:
                ins = nc.vector.tensor_scalar(self.z[:, q, :], src, self.mv[:, par, q, 0:1], self.scale[:, q:q + 1],
                                              ALU.subtract, ALU.mult)
            ins.then_inc(v.sem, v.step(*(("z",) if q == NQ - 1 else ("z", q))))

    def tensor_tr(self, pe, k):
        nc = self.core.nc
        pe.wait_ge(self.vec.sem, self.vec.done(k, "z"))
        pe.wait_ge(self.low.sem, self.low.done(k, "lo", back=1))
        pe.wait_ge(self.act.sem, self.act.done(k, "hi", back=1))
        for q in range(NQ):
            ins = nc.tensor.transpose(self.core.psum[:, self.bank, q * P:(q + 1) * P], self.z[:, q, :], self.core.ident[:, :])
        ins.then_inc(self.pe.sem, self.pe.step("tr"))

    def scalar_hi(self, act, k, par):
        nc = self.core.nc
        act.wait_ge(self.pe.sem, self.pe.done(k, "tr"))
        bank, to = self.core.psum[:, self.bank, :], self.hi[:, par, self.pad:self.pad + T]
        if self.affine:
            act.wait_ge(self.low.sem, self.low.done(k, "lo", back=1))
            gain, bias = self.affine
            nc.scalar.activation(self.full[:, :], bank, ACT.Identity, bias=bias, scale=gain).then_inc(self.act.sem, self.act.step("full"))
            act.wait_ge(self.act.sem, self.act.done(k, "full"))
            bank = self.full[:, :]
        nc.scalar.activation(to, bank, ACT.Copy).then_inc(self.act.sem, self.act.step("hi"))

    def vector_lo(self, dve, k, par):
        nc = self.core.nc
        dve.wait_ge(self.act.sem, self.act.done(k, "hi"))
        part = slice(self.pad, self.pad + T)
        whole = self.full[:, :] if self.affine else self.core.psum[:, self.bank, :]
        nc.vector.tensor_tensor(self.lo[:, par, part], whole, self.hi[:, par, part],
                                ALU.subtract).then_inc(self.low.sem, self.low.step("lo"))


def split_weights(core, ctx, name, raw, cols, chunks=()):
    nc = core.nc
    hi = ctx.enter_context(nc.sbuf_tensor(name + "_hi", [P, cols], F32R))
    lo = ctx.enter_context(nc.sbuf_tensor(name + "_lo", [P, cols], F32R))
    return hi, lo


def weights_block(core, name, source, hi, lo, scales=()):
    nc, cols = core.nc, hi.shape[1]
    CH = 2048
    n = (cols + CH - 1) // CH
    with ExitStack() as ctx:
        raw = ctx.enter_context(nc.sbuf_tensor(name + "_raw", [P, cols], F32))
        gain = ctx.enter_context(nc.sbuf_tensor(name + "_gain", [P, max(len(scales), 1)], F32))
        loaded = [core_semaphore(nc, f"{name}_loaded{c}") for c in range(n)]
        gains = core_semaphore(nc, name + "_gains")
        scaled = core_semaphore(nc, name + "_scaled")
        rounded = core_semaphore(nc, name + "_rounded")
        block = ctx.enter_context(nc.Block())
        span = lambda c: slice(c * CH, min((c + 1) * CH, cols))

        @block.sync
        def _(sp):
            for s, (_, _, g, *_) in enumerate(scales):
                sp.dma_start(gain[:, s:s + 1], g).then_inc(gains, 16)
            for c in range(n):
                sp.dma_start(raw[:, span(c)], core.dram[source][:, span(c)]).then_inc(loaded[c], 16)

        @block.gpsimd
        def _(pool):
            if scales:
                made = 0
                pool.wait_ge(gains, 16 * len(scales))
                for c in range(n):
                    pool.wait_ge(loaded[c], 16)
                for s, (a, b, _, *one_minus) in enumerate(scales):
                    if one_minus:
                        nc.gpsimd.tensor_scalar(gain[:, s:s + 1], gain[:, s:s + 1], -1.0, 1.0, ALU.mult, ALU.add).then_inc(scaled, 1)
                        made += 1
                        pool.wait_ge(scaled, made)
                    made += 1
                    nc.gpsimd.tensor_scalar(raw[:, a:b], raw[:, a:b], gain[:, s:s + 1], None, ALU.mult).then_inc(scaled, 1)

        @block.scalar
        def _(act):
            if scales:
                act.wait_ge(scaled, sum(len(s) - 2 for s in scales))
            for c in range(n):
                act.wait_ge(loaded[c], 16)
                nc.scalar.activation(hi[:, span(c)], raw[:, span(c)], ACT.Copy).then_inc(rounded, 1)

        @block.vector
        def _(dve):
            for c in range(n):
                dve.wait_ge(loaded[c], 16)
                dve.wait_ge(rounded, c + 1)
                nc.vector.tensor_tensor(lo[:, span(c)], raw[:, span(c)], hi[:, span(c)], ALU.subtract)


def product(nc, out, w_hi, w_lo, x_hi, x_lo, start=True, stop=True):
    nc.tensor.matmul(out, w_hi, x_hi, start=start, stop=False)
    nc.tensor.matmul(out, w_lo, x_hi, start=False, stop=False)
    return nc.tensor.matmul(out, w_hi, x_lo, start=False, stop=stop)


AL_QK, AL_V = 0, P
AL_COLS = 2 * P


def alibi_block(core, name, w_hi, w_lo):
    nc, plan, ps, d_ = core.nc, core.plan, core.psum, core.dram
    TR, Y, VB, S, W, O = 0, 1, 2, (3, 4), 5, (6, 7)
    SCALE = P ** -0.5
    U = 2 * NQ
    with ExitStack() as ctx:
        sb = lambda n, s, t=F32: ctx.enter_context(nc.sbuf_tensor(name + n, s, t))
        head = Head(core, ctx, name, "ln", core.x, TR)
        vec, act = Steps(nc, ctx, plan, name + "_vector"), Steps(nc, ctx, plan, name + "_scalar")
        pe = Steps(nc, ctx, plan, name + "_tensor")
        loaded = core_semaphore(nc, name + "_tables_loaded")
        made = core_semaphore(nc, name + "_bias_made")
        slope = sb("slope", [P, 1])
        bias = sb("bias", [P, NQ, T])
        y_hi, y_lo = sb("y_hi", [P, 2, T], F32R), sb("y_lo", [P, 2, T], F32R)
        V = sb("V", [P, 2, NQ, P])
        sc = sb("sc", [P, 2, T])
        neg_max, sums, rec = sb("neg_max", [P, U]), sb("sums", [P, U]), sb("rec", [P, U])
        w, wT = sb("w", [P, 2, T]), sb("wT", [P, 2, T])
        block = ctx.enter_context(nc.Block())
        keys = lambda u: (u % NQ + 1) * P

        @block.sync
        def _(sp):
            sp.dma_start(slope[:, :], d_["L0_attn_b_alibi_slope"].unsqueeze(0).to_broadcast([P, 1])).then_inc(loaded, 16)
            sp.dma_start(bias[:, :, :], d_["distance"].rearrange("p (q t) -> p q t", t=T)).then_inc(loaded, 16)
            sp.dma_start(sc[:, 0, 0:P], d_["causal"]).then_inc(loaded, 16)

        @block.tensor
        def _(t):
            pe.credit(t)
            head.pe.credit(t)
            head.start()
            head.tensor_tr(t, 0)

            def project(i, j):
                hi, lo = head.hi[:, j, :], head.lo[:, j, :]
                t.wait_ge(head.low.sem, head.low.done(2 * i + j, "lo"))
                back, m = earlier(j, 1, 2)
                t.wait_ge(vec.sem, vec.done(i, "y_lo", m, back=back))
                product(nc, ps[:, Y, :], w_hi[:, AL_QK:AL_QK + P], w_lo[:, AL_QK:AL_QK + P], hi, lo).then_inc(pe.sem, pe.step("y", j))
                t.wait_ge(act.sem, act.done(i, "V", m, back=back))
                for q in range(NQ):
                    c = slice(q * P, (q + 1) * P)
                    ins = product3(nc, ps[:, VB, c], head.hi[:, j, c], head.lo[:, j, c], w_hi[:, AL_V:AL_V + P], w_lo[:, AL_V:AL_V + P])
                ins.then_inc(pe.sem, pe.step("V", j))

            def scores(i, u):
                j, q = divmod(u, NQ)
                c, n = slice(q * P, (q + 1) * P), keys(u)
                t.wait_ge(vec.sem, vec.done(i, "y_lo", j))
                back, m = earlier(u, 2, U)
                t.wait_ge(vec.sem, vec.done(i, "sc", m, back=back))
                out = ps[:, S[u % 2], 0:n]
                nc.tensor.matmul(out, y_hi[:, j, c], head.hi[:, j, 0:n], start=True, stop=False)
                nc.tensor.matmul(out, y_lo[:, j, c], head.hi[:, j, 0:n], start=False, stop=False)
                nc.tensor.matmul(out, y_hi[:, j, c], head.lo[:, j, 0:n], start=False, stop=True).then_inc(pe.sem, pe.step("s", u))

            def turn(i, u):
                t.wait_ge(act.sem, act.done(i, "w", u))
                back, m = earlier(u, 1, U)
                t.wait_ge(act.sem, act.done(i, "wT", m, back=back))
                for k in range(u % NQ + 1):
                    ins = nc.tensor.transpose(ps[:, W, k * P:(k + 1) * P], w[:, u % 2, k * P:(k + 1) * P], core.ident[:, :])
                ins.then_inc(pe.sem, pe.step("turned", u))

            def attend(i, u):
                j, q = divmod(u, NQ)
                t.wait_ge(act.sem, act.done(i, "V", j))
                t.wait_ge(act.sem, act.done(i, "wT", u))
                if q == 0:
                    t.wait_ge(vec.sem, vec.done(i, "tail", j, back=1))
                for k in range(q + 1):
                    ins = nc.tensor.matmul(ps[:, O[j], q * P:(q + 1) * P], wT[:, u % 2, k * P:(k + 1) * P], V[:, j, k, :],
                                           start=(k == 0), stop=(k == q))
                ins.then_inc(pe.sem, pe.step("o", u))

            with t.Fori(0, PAIRS) as i:
                pe.start()
                project(i, 0)
                for n in range(U + 3):
                    if n < U:
                        scores(i, n)
                    if n == 1:
                        head.start()
                        head.tensor_tr(t, 2 * i + 1)
                    if n == 3:
                        project(i, 1)
                    if n == 7:
                        head.start()
                        head.tensor_tr(t, 2 * i + 2)
                    if 2 <= n < U + 2:
                        turn(i, n - 2)
                    if n >= 3:
                        attend(i, n - 3)

        @block.scalar
        def _(a):
            act.credit(a)
            head.act.credit(a)
            head.start()
            head.scalar_hi(a, 0, 0)

            def projected(i, j):
                a.wait_ge(pe.sem, pe.done(i, "o", j * NQ + NQ - 1, back=1))
                a.wait_ge(pe.sem, pe.done(i, "y", j))
                nc.scalar.activation(y_hi[:, j, :], ps[:, Y, :], ACT.Copy).then_inc(act.sem, act.step("y_hi", j))
                a.wait_ge(pe.sem, pe.done(i, "V", j))
                nc.scalar.activation(V[:, j, :, :], ps[:, VB, :].rearrange("p (q d) -> p q d", d=P), ACT.Copy).then_inc(act.sem, act.step("V", j))

            with a.Fori(0, PAIRS) as i:
                act.start()
                projected(i, 0)
                for n in range(U + 1):
                    if n < U:
                        a.wait_ge(vec.sem, vec.done(i, "max", n))
                        back, m = earlier(n, 2, U)
                        a.wait_ge(pe.sem, pe.done(i, "turned", m, back=back))
                        a.wait_ge(vec.sem, vec.done(i, "rec", n // NQ, back=1))
                        nc.scalar.activation(w[:, n % 2, 0:keys(n)], sc[:, n % 2, 0:keys(n)], ACT.Exp, bias=neg_max[:, n:n + 1],
                                             accum_out=sums[:, n:n + 1]).then_inc(act.sem, act.step("w", n))
                    if n == 1:
                        head.start()
                        head.scalar_hi(a, 2 * i + 1, 1)
                    if n == 2:
                        projected(i, 1)
                    if n >= 1:
                        u = n - 1
                        back, m = earlier(u, 2, U)
                        a.wait_ge(pe.sem, pe.done(i, "o", m, back=back))
                        a.wait_ge(pe.sem, pe.done(i, "turned", u))
                        nc.scalar.activation(wT[:, u % 2, 0:keys(u)], ps[:, W, 0:keys(u)], ACT.Copy).then_inc(act.sem, act.step("wT", u))
                head.start()
                head.scalar_hi(a, 2 * i + 2, 0)

        @block.vector
        def _(d):
            vec.credit(d)
            head.vec.credit(d)
            head.low.credit(d)

            def before(k, par, seq):
                head.start()
                head.vector_stats(d, k, par, seq)
                head.vector_z(d, k, par, seq)

            before(0, 0, 0)
            head.vector_lo(d, 0, 0)
            d.wait_ge(made, 1 + NQ)

            def projected(i, j):
                d.wait_ge(act.sem, act.done(i, "y_hi", j))
                nc.vector.tensor_tensor(y_lo[:, j, :], ps[:, Y, :], y_hi[:, j, :], ALU.subtract).then_inc(vec.sem, vec.step("y_lo", j))

            def tail(i, j):
                d.wait_ge(act.sem, act.done(i, "w", j * NQ + NQ - 1))
                us = slice(j * NQ, (j + 1) * NQ)
                d.wait_ge(vec.sem, vec.done(i, "tail", j, back=1))
                nc.vector.reciprocal(rec[:, us], sums[:, us]).then_inc(vec.sem, vec.step("rec", j))
                d.wait_ge(vec.sem, vec.done(i, "rec", j))
                d.wait_ge(pe.sem, pe.done(i, "o", j * NQ + NQ - 1))
                for q in range(NQ):
                    at = cut((2 * i + j) * T + q * P, P)
                    ins = nc.vector.scalar_tensor_tensor(core.x[:, at], ps[:, O[j], q * P:(q + 1) * P], rec[:, j * NQ + q:j * NQ + q + 1],
                                                         core.x[:, at], ALU.mult, ALU.add)
                ins.then_inc(vec.sem, vec.step("tail", j))

            with d.Fori(0, PAIRS) as i:
                vec.start()
                projected(i, 0)
                for n in range(U):
                    d.wait_ge(pe.sem, pe.done(i, "s", n))
                    back, m = earlier(n, 2, U)
                    d.wait_ge(act.sem, act.done(i, "w", m, back=back))
                    nc.vector.scalar_tensor_tensor(sc[:, n % 2, 0:keys(n)], ps[:, S[n % 2], 0:keys(n)], SCALE, bias[:, n % NQ, 0:keys(n)],
                                                   ALU.mult, ALU.add).then_inc(vec.sem, vec.step("sc", n))
                    d.wait_ge(vec.sem, vec.done(i, "sc", n))
                    nc.vector.tensor_reduce(neg_max[:, n:n + 1], sc[:, n % 2, 0:keys(n)], AXX, ALU.max,
                                            negate=True).then_inc(vec.sem, vec.step("max", n))
                    if n == 0:
                        before(2 * i + 1, 1, 2 * i + 1)
                    if n == 1:
                        head.vector_lo(d, 2 * i + 1, 1)
                    if n == 2:
                        projected(i, 1)
                    if n == 6:
                        before(2 * i + 2, 0, (2 * i + 2) % NSEQ)
                    if n == 7:
                        tail(i, 0)
                head.vector_lo(d, 2 * i + 2, 0)
                tail(i, 1)

        @block.gpsimd
        def _(p):
            head.pool.credit(p)
            p.wait_ge(loaded, 16 * 3)
            nc.gpsimd.tensor_scalar(bias[:, :, :], bias[:, :, :], slope[:, 0:1], None, ALU.mult).then_inc(made, 1)
            p.wait_ge(made, 1)
            for q in range(NQ):
                c = slice(q * P, (q + 1) * P)
                nc.gpsimd.tensor_tensor(bias[:, q, c], bias[:, q, c], sc[:, 0, 0:P], ALU.add).then_inc(made, 1)
            head.pool_scale(p, 0, 0)
            with p.Fori(0, PAIRS) as i:
                head.start()
                head.pool_scale(p, 2 * i + 1, 1)
                head.start()
                head.pool_scale(p, 2 * i + 2, 0)


def alibi_layer(core, ctx, name):
    hi, lo = split_weights(core, ctx, name + "w", None, AL_COLS)
    weights_block(core, name + "w", "alibi_w", hi, lo)
    alibi_block(core, name, hi, lo)


DK = 32
A0_HEADS = 4
A0_Q, A0_K = 0, A0_HEADS * 3 * DK
A0_V = A0_K + 3 * DK
A0_O = A0_V + DK
A0_COLS = A0_O + P


def attn0_block(core, name, w_hi, w_lo):
    nc, plan, ps = core.nc, core.plan, core.psum
    TR, R, S, O = 0, (1, 2, 3), (4, 5), (6, 7)
    ROWS = 3 * DK
    SCALE = DK ** -0.5
    U = 4
    with ExitStack() as ctx:
        sb = lambda n, s, t=F32: ctx.enter_context(nc.sbuf_tensor(name + n, s, t))
        head = Head(core, ctx, name, "lnr", core.x, TR)
        vec, act = Steps(nc, ctx, plan, name + "_vector"), Steps(nc, ctx, plan, name + "_scalar")
        pe = Steps(nc, ctx, plan, name + "_tensor")
        ready = core_semaphore(nc, name + "_fixed_ready")
        Q = sb("Q", [P, A0_HEADS, 2, T], F32R)
        K = sb("K", [P, 2, T], F32R)
        V = sb("V", [P, 2, NQ, DK])
        q_hi = Q
        ones = sb("ones", [P, DK])
        neg_max = sb("neg_max", [P, NQ, A0_HEADS, 97])
        weights = sb("weights", [P, 2, 4, T])
        rec = sb("rec", [P, T])
        att, att_hi, att_lo = sb("att", [P, T]), sb("att_hi", [P, T], F32R), sb("att_lo", [P, T], F32R)
        out_sb = sb("out_sb", [P, T])
        block = ctx.enter_context(nc.Block())

        proj = lambda j: [("k", j), ("v", j)] + [("q", j, h) for h in range(A0_HEADS)]
        maxes = lambda u: [("max", u, hh, st) for hh in range(2) for st in range(NQ)]
        rows = lambda u: [("nm", u, hh) for hh in range(2)]
        users = (proj(0) + maxes(0) + maxes(1) + rows(0) + proj(1) + maxes(2) + rows(1) + maxes(3)
                 + [("o", 0)] + rows(2) + rows(3) + [("o", 1)])

        def freed(i, user, back):
            if user[0] in ("k", "q"):
                return vec.sem, vec.done(i, "lo", *user, back=back)
            if user[0] == "max":
                return vec.sem, vec.done(i, *user, back=back)
            return act.sem, act.done(i, *user, back=back)

        def bank_of(user):
            return R[users.index(user) % len(R)]

        @block.tensor
        def _(t):
            pe.credit(t)
            head.pe.credit(t)
            head.pe.start()
            head.tensor_tr(t, 0)
            t.wait_ge(ready, 3)

            def ring(i, user):
                back, m = earlier(users.index(user), len(R), len(users))
                t.wait_ge(*freed(i, users[m], back))
                return bank_of(user)

            def project(i, j):
                k = 2 * i + j
                hi, lo = head.hi[:, j, :], head.lo[:, j, :]
                t.wait_ge(head.low.sem, head.low.done(k, "lo"))
                for user, c in [(("k", j), A0_K)]:
                    b = ring(i, user)
                    product(nc, ps[0:ROWS, b, :], w_hi[:, c:c + ROWS], w_lo[:, c:c + ROWS], hi, lo).then_inc(pe.sem, pe.step(*user))
                b = ring(i, ("v", j))
                for q in range(NQ):
                    c = slice(q * P, (q + 1) * P)
                    ins = product3(nc, ps[:, b, q * DK:(q + 1) * DK], head.hi[:, j, c], head.lo[:, j, c],
                                   w_hi[:, A0_V:A0_V + DK], w_lo[:, A0_V:A0_V + DK])
                ins.then_inc(pe.sem, pe.step("v", j))
                for h in range(A0_HEADS):
                    b, c = ring(i, ("q", j, h)), A0_Q + h * ROWS
                    product(nc, ps[0:ROWS, b, :], w_hi[:, c:c + ROWS], w_lo[:, c:c + ROWS], hi, lo).then_inc(pe.sem, pe.step("q", j, h))

            def scores_for_max(i, u):
                j, pr = divmod(u, 2)
                for hh in range(2):
                    h = 2 * pr + hh
                    t.wait_ge(vec.sem, vec.done(i, "lo", "q", j, h))
                    for st in range(NQ):
                        b = ring(i, ("max", u, hh, st))
                        nc.tensor.matmul(ps[:, b, :], Q[0:ROWS, h, j, st * P:(st + 1) * P], K[0:ROWS, j, :],
                                         start=True, stop=True).then_inc(pe.sem, pe.step("max", u, hh, st))

            def max_rows(i, u):
                for hh in range(2):
                    h = 2 * (u % 2) + hh
                    t.wait_ge(vec.sem, vec.done(i, "max", u, hh, NQ - 1))
                    b = ring(i, ("nm", u, hh))
                    for st in range(NQ):
                        ins = nc.tensor.transpose(ps[0:97, b, st * P:(st + 1) * P], neg_max[:, st, h, :], core.ident[:, :])
                    ins.then_inc(pe.sem, pe.step("nm", u, hh))

            def attend(i, u):
                j, pr = divmod(u, 2)
                t.wait_ge(act.sem, act.done(i, "nm", u, 1))
                back, m = earlier(u, 2, U)
                t.wait_ge(vec.sem, vec.done(i, "att", m, back=back))
                for tt in range(NQ + 1):
                    for hh in range(2):
                        if tt < NQ:
                            n = (u * NQ + tt) * 2 + hh
                            back, m = earlier(n, 2, U * NQ * 2)
                            t.wait_ge(act.sem, act.done(i, "exp", m, back=back))
                            nc.tensor.matmul(ps[:, S[n % 2], :], K[0:97, j, tt * P:(tt + 1) * P], Q[0:97, 2 * pr + hh, j, :],
                                             start=True, stop=True).then_inc(pe.sem, pe.step("st", n))
                    if tt > 0:
                        n = (u * NQ + tt - 1)
                        t.wait_ge(act.sem, act.done(i, "exp", 2 * n + 1))
                        for strip in range(4):
                            hh = strip % 2
                            left = V[:, j, tt - 1, :] if strip < 2 else ones[:, :]
                            ins = nc.tensor.matmul(ps[strip * 32:strip * 32 + 32, O[u % 2], :], left, weights[:, hh, n % 4, :],
                                                   start=(tt == 1), stop=(tt == NQ))
                        ins.then_inc(pe.sem, pe.step("pv", n))

            def output(i, j):
                t.wait_ge(vec.sem, vec.done(i, "att_lo", j))
                b = ring(i, ("o", j))
                product(nc, ps[:, b, :], w_hi[:, A0_O:A0_O + P], w_lo[:, A0_O:A0_O + P], att_hi[:, :], att_lo[:, :]).then_inc(pe.sem, pe.step("o", j))

            def tail(i, j, k_next):
                t.wait_ge(act.sem, act.done(i, "o", j))
                t.wait_ge(head.low.sem, head.low.done(k_next, "lo"))
                for q in range(NQ):
                    ins = nc.tensor.transpose(ps[:, TR, q * P:(q + 1) * P], out_sb[:, q * P:(q + 1) * P], core.ident[:, :])
                ins.then_inc(pe.sem, pe.step("tail", j))

            with t.Fori(0, PAIRS) as i:
                pe.start()
                project(i, 0)
                scores_for_max(i, 0)
                scores_for_max(i, 1)
                max_rows(i, 0)
                head.pe.start()
                t.wait_ge(vec.sem, vec.done(i, "tail", 1, back=1))
                head.tensor_tr(t, 2 * i + 1)
                attend(i, 0)
                project(i, 1)
                scores_for_max(i, 2)
                max_rows(i, 1)
                attend(i, 1)
                scores_for_max(i, 3)
                output(i, 0)
                max_rows(i, 2)
                attend(i, 2)
                tail(i, 0, 2 * i + 1)
                max_rows(i, 3)
                attend(i, 3)
                head.pe.start()
                t.wait_ge(vec.sem, vec.done(i, "tail", 0))
                head.tensor_tr(t, 2 * i + 2)
                output(i, 1)
                tail(i, 1, 2 * i + 2)

        @block.scalar
        def _(a):
            act.credit(a)
            head.act.credit(a)
            head.act.start()
            head.scalar_hi(a, 0, 0)
            copy = lambda out, in_: nc.scalar.activation(out, in_, ACT.Copy)

            def projected(i, j):
                for user in proj(j):
                    a.wait_ge(pe.sem, pe.done(i, *user))
                    b = bank_of(user)
                    if user[0] == "v":
                        copy(V[:, j, :, :], ps[:, b, 0:NQ * DK].rearrange("p (q d) -> p q d", d=DK)).then_inc(act.sem, act.step("v", j))
                    else:
                        to = K[0:ROWS, j, :] if user[0] == "k" else Q[0:ROWS, user[2], j, :]
                        copy(to, ps[0:ROWS, b, :]).then_inc(act.sem, act.step("hi", *user))

            def max_rows(i, u):
                j, pr = divmod(u, 2)
                for hh in range(2):
                    a.wait_ge(pe.sem, pe.done(i, "nm", u, hh))
                    copy(Q[96:97, 2 * pr + hh, j, :], ps[96:97, bank_of(("nm", u, hh)), :]).then_inc(act.sem, act.step("nm", u, hh))

            def exps(i, u):
                for tt in range(NQ):
                    for hh in range(2):
                        n = (u * NQ + tt) * 2 + hh
                        back, m = earlier(n // 2, 4, U * NQ)
                        a.wait_ge(pe.sem, pe.done(i, "pv", m, back=back))
                        a.wait_ge(pe.sem, pe.done(i, "st", n))
                        nc.scalar.activation(weights[:, hh, (n // 2) % 4, :], ps[:, S[n % 2], :], ACT.Exp,
                                             scale=SCALE).then_inc(act.sem, act.step("exp", n))

            def output(i, j):
                back, m = earlier(j, 1, 2)
                a.wait_ge(pe.sem, pe.done(i, "o", m, back=back))
                a.wait_ge(vec.sem, vec.done(i, "att", 2 * j + 1))
                copy(att_hi[:, :], att[:, :]).then_inc(act.sem, act.step("att_hi", j))
                a.wait_ge(pe.sem, pe.done(i, "tail", m, back=back))
                a.wait_ge(pe.sem, pe.done(i, "o", j))
                copy(out_sb[:, :], ps[:, bank_of(("o", j)), :]).then_inc(act.sem, act.step("o", j))

            with a.Fori(0, PAIRS) as i:
                act.start()
                projected(i, 0)
                max_rows(i, 0)
                head.act.start()
                head.scalar_hi(a, 2 * i + 1, 1)
                exps(i, 0)
                projected(i, 1)
                max_rows(i, 1)
                exps(i, 1)
                output(i, 0)
                max_rows(i, 2)
                exps(i, 2)
                max_rows(i, 3)
                exps(i, 3)
                head.act.start()
                head.scalar_hi(a, 2 * i + 2, 0)
                output(i, 1)

        @block.vector
        def _(d):
            vec.credit(d)
            head.vec.credit(d)
            head.low.credit(d)

            def head_before(k, par, seq):
                head.start()
                head.vector_stats(d, k, par, seq)
                head.vector_z(d, k, par, seq)

            head_before(0, 0, 0)
            head.vector_lo(d, 0, 0)

            def projected(i, j):
                for user in proj(j):
                    if user[0] == "v":
                        continue
                    d.wait_ge(act.sem, act.done(i, "hi", *user))
                    to = K[32:64, j, :] if user[0] == "k" else Q[64:96, user[2], j, :]
                    frm = ps[32:64, bank_of(user), :] if user[0] == "k" else ps[64:96, bank_of(user), :]
                    nc.vector.tensor_tensor(to, frm, to, ALU.subtract).then_inc(vec.sem, vec.step("lo", *user))

            def maxes_of(i, u):
                for hh in range(2):
                    h = 2 * (u % 2) + hh
                    back, m = earlier(u, 2, U)
                    d.wait_ge(pe.sem, pe.done(i, "nm", m, hh, back=back))
                    for st in range(NQ):
                        d.wait_ge(pe.sem, pe.done(i, "max", u, hh, st))
                        nc.vector.tensor_reduce(neg_max[:, st, h, 96:97], ps[:, bank_of(("max", u, hh, st)), :], AXX, ALU.max,
                                                negate=True).then_inc(vec.sem, vec.step("max", u, hh, st))

            def normalise(i, u):
                j, pr = divmod(u, 2)
                d.wait_ge(pe.sem, pe.done(i, "pv", u * NQ + NQ - 1))
                nc.vector.reciprocal(rec[0:64, :], ps[64:128, O[u % 2], :]).then_inc(vec.sem, vec.step("rec", u))
                d.wait_ge(vec.sem, vec.done(i, "rec", u))
                back, m = earlier(j, 1, 2)
                d.wait_ge(act.sem, act.done(i, "att_hi", m, back=back))
                d.wait_ge(vec.sem, vec.done(i, "att_lo", m, back=back))
                nc.vector.tensor_tensor(att[pr * 64:pr * 64 + 64, :], ps[0:64, O[u % 2], :], rec[0:64, :],
                                        ALU.mult).then_inc(vec.sem, vec.step("att", u))

            def att_lo_of(i, j):
                d.wait_ge(act.sem, act.done(i, "att_hi", j))
                nc.vector.tensor_tensor(att_lo[:, :], att[:, :], att_hi[:, :], ALU.subtract).then_inc(vec.sem, vec.step("att_lo", j))

            def tail(i, j):
                d.wait_ge(head.kept.sem, head.kept.done(2 * i + j, "keep"))
                d.wait_ge(pe.sem, pe.done(i, "tail", j))
                nc.vector.tensor_tensor(core.x2[:, cut((2 * i + j) * T, T)], head.keep[:, j, :], ps[:, TR, :],
                                        ALU.add).then_inc(vec.sem, vec.step("tail", j))

            with d.Fori(0, PAIRS) as i:
                vec.start()
                projected(i, 0)
                maxes_of(i, 0)
                head_before(2 * i + 1, 1, 2 * i + 1)
                maxes_of(i, 1)
                head.vector_lo(d, 2 * i + 1, 1)
                projected(i, 1)
                maxes_of(i, 2)
                normalise(i, 0)
                maxes_of(i, 3)
                normalise(i, 1)
                att_lo_of(i, 0)
                tail(i, 0)
                normalise(i, 2)
                head_before(2 * i + 2, 0, (2 * i + 2) % NSEQ)
                normalise(i, 3)
                head.vector_lo(d, 2 * i + 2, 0)
                att_lo_of(i, 1)
                tail(i, 1)

        @block.gpsimd
        def _(p):
            head.pool.credit(p)
            p.memset(K[96:97, :, :].bitcast(F32), 1.0).then_inc(ready, 1)
            p.wait_ge(ready, 1)
            p.memset(ones[:, :], 1.0).then_inc(ready, 1)
            p.wait_ge(ready, 2)
            p.memset(neg_max[:, :, :, :], 0.0).then_inc(ready, 1)

            def head_pool(k, par, seq):
                head.pool_scale(p, k, par)
                head.pool_keep(p, k, par, seq)

            head.kept.credit(p)
            head.start()
            head_pool(0, 0, 0)
            with p.Fori(0, PAIRS) as i:
                head.start()
                p.wait_ge(vec.sem, vec.done(i, "tail", 1, back=1))
                head_pool(2 * i + 1, 1, 2 * i + 1)
                head.start()
                p.wait_ge(vec.sem, vec.done(i, "tail", 0))
                head_pool(2 * i + 2, 0, (2 * i + 2) % NSEQ)


def attn0_layer(core, ctx, name):
    hi, lo = split_weights(core, ctx, name + "w", None, A0_COLS)
    weights_block(core, name + "w", "attn0_w", hi, lo, [(0, A0_O, core.dram["L0_ffn_g1"].unsqueeze(1))])
    attn0_block(core, name, hi, lo)


DH = 8
D_GROUPS = 4
PER_GROUP = 4
D_ROWS = 3 * PER_GROUP * DH
DF_Q = 0
DF_K = DF_Q + D_GROUPS * D_ROWS
DF_V = DF_K + D_GROUPS * D_ROWS
DF_P = DF_V + P
DF_COLS = DF_P + P


def diff_block(core, name, w_hi, w_lo):
    nc, plan, ps, dram = core.nc, core.plan, core.psum, core.dram
    O, R, S = 0, (1, 2, 3), (4, 6)
    SCALE = DH ** -0.5
    GROUPS = 2 * D_GROUPS
    BLOCKS = PER_GROUP * NQ
    NEG = D_ROWS + PER_GROUP
    with ExitStack() as ctx:
        sb = lambda n, s, t=F32: ctx.enter_context(nc.sbuf_tensor(name + n, s, t))
        head = Head(core, ctx, name, "ln", core.x, R[0])
        steps = lambda n: Steps(nc, ctx, plan, name + n)
        pe_proj, act_proj, vec_proj, pool_proj = (steps("_proj_" + e) for e in ("tensor", "scalar", "vector", "pool"))
        pe_max, act_max, vec_max = (steps("_max_" + e) for e in ("tensor", "scalar", "vector"))
        pe_att, act_att = (steps("_att_" + e) for e in ("tensor", "scalar"))
        pe_out, act_out, vec_out = (steps("_out_" + e) for e in ("tensor", "scalar", "vector"))
        pe_val, vec_val = (steps("_values_" + e) for e in ("tensor", "vector"))
        pe_end, act_end, vec_end, pool_end = (steps("_end_" + e) for e in ("tensor", "scalar", "vector", "pool"))
        loaded = core_semaphore(nc, name + "_rows_loaded")
        ready = core_semaphore(nc, name + "_fixed_ready")
        mixed = core_semaphore(nc, name + "_lambda_ready")
        Q, K = sb("Q", [P, 4, T], F32R), sb("K", [P, 2, T], F32R)
        kz = sb("kz", [P, 4, PER_GROUP, T], F32R)
        head_rows = sb("head_rows", [P, PER_GROUP])
        q_bias, k_bias = sb("q_bias", [D_ROWS, D_GROUPS]), sb("k_bias", [D_ROWS, D_GROUPS])
        v_bias, p_bias = sb("v_bias", [P, P]), sb("p_bias", [P, P])
        V = core.x2[:, :].rearrange("p (j t h e) -> p j t h e", j=2, t=NQ, h=16)
        neg_max = sb("neg_max", [P, NQ, NEG])
        weights = sb("weights", [P, NQ, PER_GROUP, T])
        o_sb = sb("o_sb", [P, T])
        rec = sb("rec", [P, NQ, PER_GROUP])
        on = sb("on", [P, NQ, P])
        f_hi, f_lo = sb("f_hi", [P, T], F32R), sb("f_lo", [P, T], F32R)
        lam = sb("lambdas", [P, 4, 8, DH])
        prod, sums, ex = sb("lambda_prod", [P, 2, 8, DH]), sb("lambda_sums", [P, 2, 8]), sb("lambda_exp", [P, 2, 8])
        gap, neg_lv = sb("lambda_gap", [P, 8]), sb("neg_lv", [P, 2])
        block = ctx.enter_context(nc.Block())

        AHEAD = (range(0, 6), range(6, 11), range(11, 16))

        proj = lambda n: [("q", n), ("k", n)] + ([("v", n)] if n % D_GROUPS == 0 else [])

        def slot_users(G):
            maxes = lambda part: [("max", G + 1, b) for b in AHEAD[part]]
            u = maxes(0)
            if G > 0:
                u += [("o", G - 1)]
            u += maxes(1) + proj(G + 2)
            if G == D_GROUPS:
                u += [("turned", 0)]
            u += maxes(2)
            if G == D_GROUPS:
                u += [("end", 0)]
            u += [("nm", G + 1)]
            if G in (0, 4):
                u += [("head", G // 4 + 1)]
            return u

        users = [u for G in range(GROUPS) for u in slot_users(G)] + [("o", GROUPS - 1), ("turned", 1), ("end", 1)]
        bank_of = lambda user: R[users.index(user) % len(R)]

        def freed(i, user, back):
            what, n = user[0], user[1]
            group = (n if i is None else GROUPS * i + n) - GROUPS * back
            seq = (n // D_GROUPS if what == "v" else n) - 2 * back if i is None else 2 * i + (n // D_GROUPS if what == "v" else n) - 2 * back
            if what in ("q", "k"):
                return vec_proj.sem, vec_proj.done(group, "lo", what)
            if what == "v":
                return vec_val.sem, vec_val.done(seq, "v")
            if what == "max":
                return vec_max.sem, vec_max.done(group, "max", user[2])
            if what == "nm":
                return act_max.sem, act_max.done(group, "nm")
            if what == "o":
                return vec_out.sem, vec_out.done(group, "on")
            if what == "turned":
                return vec_end.sem, vec_end.done(seq, "lo")
            if what == "end":
                return vec_end.sem, vec_end.done(seq, "tail")
            return head.low.sem, head.low.done(seq, "lo")

        before_loop = proj(8) + proj(9) + [("max", 8, b) for b in range(BLOCKS)] + [("nm", 8)]

        def ring(t, i, user):
            if i is None:
                at = before_loop.index(user)
                same = [u for u in before_loop[:at] if bank_of(u) == bank_of(user)]
                if same:
                    t.wait_ge(*freed(None, same[-1], 1))
            else:
                back, m = earlier(users.index(user), len(R), len(users))
                t.wait_ge(*freed(i, users[m], back))
            return bank_of(user)

        group_of = lambda i, n: n - GROUPS if i is None else GROUPS * i + n
        seq_of = lambda i, j: j - 2 if i is None else 2 * i + j

        @block.sync
        def _(sp):
            rows = [(head_rows[:, :], "diff_head_rows"), (q_bias[:, :], "diff_bq"), (k_bias[:, :], "diff_bk")]
            for to, frm in rows:
                sp.dma_start(to, dram[frm]).then_inc(loaded, 16)
            for to, frm in ((v_bias, "L1_attn_b_bv"), (p_bias, "L1_attn_b_bp")):
                sp.dma_start(to[:, :], dram[frm].unsqueeze(0).to_broadcast([P, P])).then_inc(loaded, 16)
            for m, n in enumerate(("q1", "q2", "k1", "k2")):
                sp.dma_start(lam[:, m, :, :].rearrange("p h d -> p (h d)"),
                             dram["L1_attn_b_lambda_" + n].unsqueeze(0).to_broadcast([P, 8 * DH])).then_inc(loaded, 16)

        @block.tensor
        def _(t):
            for s in (pe_proj, pe_max, pe_att, pe_out, pe_val, pe_end, head.pe):
                s.credit(t)

            def project(i, n):
                j = n // D_GROUPS
                hi, lo = head.hi[:, j % 2, :], head.lo[:, j % 2, :]
                pe_proj.start()
                if n % D_GROUPS == 0:
                    t.wait_ge(head.low.sem, head.low.done(seq_of(i, j), "lo"))
                for user, c in ((("q", n), DF_Q), (("k", n), DF_K)):
                    c += (n % D_GROUPS) * D_ROWS
                    b = ring(t, i, user)
                    product(nc, ps[0:D_ROWS, b, :], w_hi[:, c:c + D_ROWS], w_lo[:, c:c + D_ROWS], hi, lo
                            ).then_inc(pe_proj.sem, pe_proj.step(user[0]))
                if n % D_GROUPS == 0:
                    pe_val.start()
                    b = ring(t, i, ("v", n))
                    for q in range(NQ):
                        c = slice(q * P, (q + 1) * P)
                        ins = product3(nc, ps[:, b, c], head.hi[:, j % 2, c], head.lo[:, j % 2, c],
                                       w_hi[:, DF_V:DF_V + P], w_lo[:, DF_V:DF_V + P])
                    ins.then_inc(pe_val.sem, pe_val.step("v"))

            def scores_for_max(i, n, part):
                for b in part:
                    hh, st = divmod(b, NQ)
                    if b == 0:
                        pe_max.start()
                        t.wait_ge(vec_proj.sem, vec_proj.done(group_of(i, n), "lo", "q"))
                    if st == 0:
                        t.wait_ge(pool_proj.sem, pool_proj.done(group_of(i, n), "kz", hh))
                    bank = ring(t, i, ("max", n, b))
                    nc.tensor.matmul(ps[:, bank, :], Q[0:D_ROWS, n % 4, st * P:(st + 1) * P], kz[0:D_ROWS, n % 4, hh, :],
                                     start=True, stop=True).then_inc(pe_max.sem, pe_max.step("max", b))

            def max_rows(i, n):
                t.wait_ge(vec_max.sem, vec_max.done(group_of(i, n), "max", BLOCKS - 1))
                bank = ring(t, i, ("nm", n))
                for st in range(NQ):
                    ins = nc.tensor.transpose(ps[0:NEG, bank, st * P:(st + 1) * P], neg_max[:, st, :], core.ident[:, :])
                ins.then_inc(pe_max.sem, pe_max.step("nm"))

            def scores(i, n, tt):
                for pair in range(2):
                    m = 2 * tt + pair
                    g = group_of(i, n)
                    if m == 0:
                        pe_att.start()
                        t.wait_ge(act_max.sem, act_max.done(g, "nm"))
                    if m < 2:
                        t.wait_ge(act_att.sem, act_att.done(g, "exp", 6 + m, back=1))
                    else:
                        t.wait_ge(act_att.sem, act_att.done(g, "exp", m - 2))
                    for h in range(2):
                        ins = nc.tensor.matmul(ps[:, S[m % 2] + h, :], kz[0:NEG, n % 4, 2 * pair + h, tt * P:(tt + 1) * P],
                                               Q[0:NEG, n % 4, :], start=True, stop=True)
                    ins.then_inc(pe_att.sem, pe_att.step("scores", m))

            def attend(i, n, tt):
                j, g = divmod(n, D_GROUPS)
                if tt == 0:
                    if g == 0:
                        t.wait_ge(vec_val.sem, vec_val.done(seq_of(i, j), "v"))
                    t.wait_ge(act_out.sem, act_out.done(group_of(i, n), "o", back=1))
                t.wait_ge(act_att.sem, act_att.done(group_of(i, n), "exp", 2 * tt + 1))
                for hh in range(PER_GROUP):
                    ins = nc.tensor.matmul(ps[32 * hh:32 * hh + 32, O, :], V[:, j, tt, g * PER_GROUP + hh, :], weights[:, tt, hh, :],
                                           start=(tt == 0), stop=(tt == NQ - 1))
                ins.then_inc(pe_att.sem, pe_att.step("pv", tt))

            def turn_output(i, n):
                pe_out.start()
                t.wait_ge(act_out.sem, act_out.done(group_of(i, n), "o"))
                bank = ring(t, i, ("o", n))
                for q in range(NQ):
                    ins = nc.tensor.transpose(ps[:, bank, q * P:(q + 1) * P], o_sb[:, q * P:(q + 1) * P], core.ident[:, :])
                ins.then_inc(pe_out.sem, pe_out.step("o"))

            def turn_heads(i, j):
                pe_end.start()
                t.wait_ge(vec_end.sem, vec_end.done(seq_of(i, j), "mixed"))
                bank = ring(t, i, ("turned", j))
                for q in range(NQ):
                    ins = nc.tensor.transpose(ps[:, bank, q * P:(q + 1) * P], on[:, q, :], core.ident[:, :])
                ins.then_inc(pe_end.sem, pe_end.step("turned"))

            def end(i, j):
                t.wait_ge(vec_end.sem, vec_end.done(seq_of(i, j), "lo"))
                bank = ring(t, i, ("end", j))
                for q in range(NQ):
                    c = slice(q * P, (q + 1) * P)
                    ins = product3(nc, ps[:, bank, c], f_hi[:, c], f_lo[:, c], w_hi[:, DF_P:DF_P + P], w_lo[:, DF_P:DF_P + P])
                ins.then_inc(pe_end.sem, pe_end.step("end"))

            head.start()
            head.bank = R[0]
            head.tensor_tr(t, 0)
            t.wait_ge(ready, 4)
            t.wait_ge(head.low.sem, head.low.done(0, "lo"))
            project(None, 8)
            project(None, 9)
            scores_for_max(None, 8, range(BLOCKS))
            max_rows(None, 8)
            for u in before_loop[-3:]:
                t.wait_ge(*freed(None, u, 1))
            with t.Fori(0, PAIRS) as i:
                for G in range(GROUPS):
                    scores(i, G, 0)
                    scores_for_max(i, G + 1, AHEAD[0])
                    if G > 0:
                        turn_output(i, G - 1)
                    scores(i, G, 1)
                    attend(i, G, 0)
                    scores_for_max(i, G + 1, AHEAD[1])
                    project(i, G + 2)
                    if G == D_GROUPS:
                        turn_heads(i, 0)
                    scores(i, G, 2)
                    attend(i, G, 1)
                    scores_for_max(i, G + 1, AHEAD[2])
                    if G == D_GROUPS:
                        end(i, 0)
                    scores(i, G, 3)
                    attend(i, G, 2)
                    max_rows(i, G + 1)
                    if G in (0, 4):
                        head.start()
                        head.bank = ring(t, i, ("head", G // 4 + 1))
                        head.tensor_tr(t, 2 * i + G // 4 + 1)
                    attend(i, G, 3)
                turn_output(i, GROUPS - 1)
                turn_heads(i, 1)
                end(i, 1)

        @block.scalar
        def _(a):
            for s in (act_proj, act_max, act_att, act_out, act_end, head.act):
                s.credit(a)
            copy = lambda to, frm: nc.scalar.activation(to, frm, ACT.Copy)

            def projected(i, n):
                act_proj.start()
                if i is not None:
                    a.wait_ge(pe_att.sem, pe_att.done(group_of(i, n - 2), "pv", NQ - 1, back=1))
                for what, to, bias in (("q", Q[0:D_ROWS, n % 4, :], q_bias), ("k", K[0:D_ROWS, n % 2, :], k_bias)):
                    if what == "k" and i is not None:
                        a.wait_ge(pool_proj.sem, pool_proj.done(group_of(i, n - 1), "kz", PER_GROUP - 1, back=1))
                    a.wait_ge(pe_proj.sem, pe_proj.done(group_of(i, n), what))
                    nc.scalar.activation(to, ps[0:D_ROWS, bank_of((what, n)), :], ACT.Identity,
                                         bias=bias[:, n % D_GROUPS:n % D_GROUPS + 1]).then_inc(act_proj.sem, act_proj.step("hi", what))

            def max_rows(i, n):
                act_max.start()
                a.wait_ge(pe_max.sem, pe_max.done(group_of(i, n), "nm"))
                copy(Q[D_ROWS:NEG, n % 4, :], ps[D_ROWS:NEG, bank_of(("nm", n)), :]).then_inc(act_max.sem, act_max.step("nm"))

            def exps(i, n, tt):
                for pair in range(2):
                    m = 2 * tt + pair
                    g = group_of(i, n)
                    if m == 0:
                        act_att.start()
                    if pair == 0:
                        a.wait_ge(pe_att.sem, pe_att.done(g, "pv", tt, back=1))
                    a.wait_ge(pe_att.sem, pe_att.done(g, "scores", m))
                    nc.scalar.activation(weights[:, tt, 2 * pair:2 * pair + 2, :], ps[:, S[m % 2]:S[m % 2] + 2, :], ACT.Exp,
                                         scale=SCALE).then_inc(act_att.sem, act_att.step("exp", m))

            def output(i, n):
                act_out.start()
                g = group_of(i, n)
                a.wait_ge(pe_out.sem, pe_out.done(g, "o", back=1))
                a.wait_ge(pe_att.sem, pe_att.done(g, "pv", NQ - 1))
                copy(o_sb[:, :], ps[:, O, :]).then_inc(act_out.sem, act_out.step("o"))

            def end(i, j):
                act_end.start()
                k = seq_of(i, j)
                a.wait_ge(pe_end.sem, pe_end.done(k, "end", back=1))
                a.wait_ge(pe_end.sem, pe_end.done(k, "turned"))
                copy(f_hi[:, :], ps[:, bank_of(("turned", j)), :]).then_inc(act_end.sem, act_end.step("hi"))

            head.start()
            head.bank = R[0]
            head.scalar_hi(a, 0, 0)
            a.wait_ge(loaded, 16 * 9)
            a.wait_ge(ready, 4)
            a.wait_ge(mixed, 3)
            nc.scalar.activation(ex[:, :, :], sums[:, :, :], ACT.Exp).then_inc(mixed, 1)
            projected(None, 8)
            projected(None, 9)
            max_rows(None, 8)
            with a.Fori(0, PAIRS) as i:
                for G in range(GROUPS):
                    if G > 0:
                        output(i, G - 1)
                    exps(i, G, 0)
                    exps(i, G, 1)
                    projected(i, G + 2)
                    if G == D_GROUPS:
                        end(i, 0)
                    exps(i, G, 2)
                    exps(i, G, 3)
                    max_rows(i, G + 1)
                    if G in (0, 4):
                        head.start()
                        head.bank = bank_of(("head", G // 4 + 1))
                        head.scalar_hi(a, 2 * i + G // 4 + 1, (G // 4 + 1) % 2)
                output(i, GROUPS - 1)
                end(i, 1)

        @block.vector
        def _(d):
            for s in (vec_proj, vec_max, vec_out, vec_val, vec_end, head.vec, head.low):
                s.credit(d)

            def head_before(k, par, seq):
                head.start()
                head.vector_stats(d, k, par, seq)
                head.vector_z(d, k, par, seq)

            def projected(i, n):
                vec_proj.start()
                for what, to, bias in (("q", Q, q_bias), ("k", K, k_bias)):
                    rows = slice(64, 96) if what == "q" else slice(32, 64)
                    part = to[rows, n % (4 if what == "q" else 2), :]
                    d.wait_ge(act_proj.sem, act_proj.done(group_of(i, n), "hi", what))
                    nc.vector.scalar_tensor_tensor(part, ps[rows, bank_of((what, n)), :], bias[rows, n % D_GROUPS:n % D_GROUPS + 1], part,
                                                   ALU.add, ALU.subtract).then_inc(vec_proj.sem, vec_proj.step("lo", what))
                if n % D_GROUPS == 0:
                    j = n // D_GROUPS
                    vec_val.start()
                    if i is not None:
                        d.wait_ge(pe_att.sem, pe_att.done(group_of(i, n - 2), "pv", NQ - 1, back=1))
                    d.wait_ge(pe_val.sem, pe_val.done(seq_of(i, j), "v"))
                    view = lambda m: m.rearrange("p (t h e) -> p t h e", t=NQ, e=DH)
                    nc.vector.tensor_tensor(V[:, j % 2, :, :, 0:DH], view(ps[:, bank_of(("v", n)), :]),
                                            v_bias[:, :].rearrange("p (h e) -> p h e", e=DH).unsqueeze(1).to_broadcast([P, NQ, 16, DH]),
                                            ALU.add).then_inc(vec_val.sem, vec_val.step("v"))

            def maxes(i, n, part):
                for b in part:
                    hh, st = divmod(b, NQ)
                    if b == 0:
                        vec_max.start()
                        d.wait_ge(pe_max.sem, pe_max.done(group_of(i, n), "nm", back=1))
                    d.wait_ge(pe_max.sem, pe_max.done(group_of(i, n), "max", b))
                    nc.vector.tensor_reduce(neg_max[:, st, D_ROWS + hh:D_ROWS + hh + 1], ps[:, bank_of(("max", n, b)), :], AXX, ALU.max,
                                            negate=True).then_inc(vec_max.sem, vec_max.step("max", b))

            def normalise(i, n):
                j, g = divmod(n, D_GROUPS)
                vec_out.start()
                n_ = group_of(i, n)
                turned = ps[:, bank_of(("o", n)), :].rearrange("p (t h e) -> p t h e", t=NQ, e=32)
                d.wait_ge(vec_out.sem, vec_out.done(n_, "on", back=1))
                d.wait_ge(pe_out.sem, pe_out.done(n_, "o"))
                nc.vector.reciprocal(rec[:, :, :], turned[:, :, :, DH]).then_inc(vec_out.sem, vec_out.step("rec"))
                d.wait_ge(vec_out.sem, vec_out.done(n_, "rec"))
                if g == 0:
                    d.wait_ge(pe_end.sem, pe_end.done(seq_of(i, j), "turned", back=1))
                for st in range(NQ):
                    ins = nc.vector.tensor_tensor(on[:, st, 32 * g:32 * g + 32].rearrange("p (h e) -> p h e", e=DH), turned[:, st, :, 0:DH],
                                                  rec[:, st, :].unsqueeze(2).to_broadcast([P, PER_GROUP, DH]), ALU.mult)
                ins.then_inc(vec_out.sem, vec_out.step("on"))

            def mix(i, j):
                vec_end.start()
                d.wait_ge(vec_out.sem, vec_out.done(group_of(i, j * D_GROUPS + 3), "on"))
                nc.vector.scalar_tensor_tensor(on[:, :, 0:64], on[:, :, 64:P], neg_lv[:, 1:2], on[:, :, 0:64], ALU.mult, ALU.add
                                               ).then_inc(vec_end.sem, vec_end.step("mixed"))

            def end_lo(i, j):
                d.wait_ge(act_end.sem, act_end.done(seq_of(i, j), "hi"))
                nc.vector.tensor_tensor(f_lo[:, :], ps[:, bank_of(("turned", j)), :], f_hi[:, :], ALU.subtract
                                        ).then_inc(vec_end.sem, vec_end.step("lo"))

            def tail(i, j):
                k = seq_of(i, j)
                d.wait_ge(pool_end.sem, pool_end.done(k, "bias"))
                d.wait_ge(pe_end.sem, pe_end.done(k, "end"))
                at = cut(k * T, T)
                nc.vector.tensor_tensor(core.x[:, at], core.x[:, at], ps[:, bank_of(("end", j)), :], ALU.add
                                        ).then_inc(vec_end.sem, vec_end.step("tail"))

            head_before(0, 0, 0)
            head.bank = R[0]
            head.vector_lo(d, 0, 0)
            d.wait_ge(loaded, 16 * 9)
            d.wait_ge(ready, 4)
            nc.vector.tensor_tensor(prod[:, :, :, :], lam[:, 0:2, :, :], lam[:, 2:4, :, :], ALU.mult).then_inc(mixed, 1)
            d.wait_ge(mixed, 1)
            nc.vector.tensor_reduce(sums[:, :, :], prod[:, :, :, :], AXX, ALU.add).then_inc(mixed, 1)
            d.wait_ge(mixed, 2)
            nc.vector.tensor_scalar(sums[:, :, :], sums[:, :, :], 5.0, None, ALU.min).then_inc(mixed, 1)
            d.wait_ge(mixed, 4)
            nc.vector.tensor_tensor(gap[:, :], ex[:, 0, :], ex[:, 1, :], ALU.subtract).then_inc(mixed, 1)
            d.wait_ge(mixed, 5)
            nc.vector.tensor_scalar(gap[:, :], gap[:, :], 0.8, None, ALU.add).then_inc(mixed, 1)
            d.wait_ge(mixed, 6)
            nc.vector.tensor_reduce(neg_lv[:, 0:1], gap[:, :], AXX, ALU.add).then_inc(mixed, 1)
            d.wait_ge(mixed, 7)
            nc.vector.tensor_scalar(neg_lv[:, 1:2], neg_lv[:, 0:1], -0.125, None, ALU.mult).then_inc(mixed, 1)
            d.wait_ge(mixed, 8)
            projected(None, 8)
            projected(None, 9)
            maxes(None, 8, range(BLOCKS))
            with d.Fori(0, PAIRS) as i:
                for G in range(GROUPS):
                    maxes(i, G + 1, AHEAD[0])
                    if G > 0:
                        normalise(i, G - 1)
                    if G == D_GROUPS:
                        mix(i, 0)
                    maxes(i, G + 1, AHEAD[1])
                    projected(i, G + 2)
                    if G == D_GROUPS:
                        end_lo(i, 0)
                    if G in (0, 4):
                        head_before(2 * i + G // 4 + 1, (G // 4 + 1) % 2, (2 * i + G // 4 + 1) % NSEQ if G else 2 * i + 1)
                    maxes(i, G + 1, AHEAD[2])
                    if G == D_GROUPS:
                        tail(i, 0)
                    if G in (0, 4):
                        head.bank = bank_of(("head", G // 4 + 1))
                        head.vector_lo(d, 2 * i + G // 4 + 1, (G // 4 + 1) % 2)
                normalise(i, GROUPS - 1)
                mix(i, 1)
                end_lo(i, 1)
                tail(i, 1)

        @block.gpsimd
        def _(p):
            for s in (pool_proj, pool_end, head.pool):
                s.credit(p)

            def keys(i, n):
                pool_proj.start()
                if i is not None:
                    p.wait_ge(pe_att.sem, pe_att.done(group_of(i, n - 2), "pv", NQ - 1, back=1))
                p.wait_ge(vec_proj.sem, vec_proj.done(group_of(i, n), "lo", "k"))
                for hh in range(PER_GROUP):
                    nc.gpsimd.tensor_tensor(kz[:, n % 4, hh, :], K[:, n % 2, :], head_rows[:, hh:hh + 1].to_broadcast([P, T]), ALU.mult
                                            ).then_inc(pool_proj.sem, pool_proj.step("kz", hh))

            def bias(i, j):
                k = 2 * i + j
                pool_end.start()
                p.wait_ge(head.vec.sem, head.vec.done(k, "z"))
                tokens = core.x[:, cut(k * T, T)].rearrange("p (q d) -> p q d", d=P)
                nc.gpsimd.tensor_tensor(tokens, tokens, p_bias[:, :].unsqueeze(1).to_broadcast([P, NQ, P]), ALU.add
                                        ).then_inc(pool_end.sem, pool_end.step("bias"))

            p.memset(K[:, :, :].bitcast(F32), 0.0).then_inc(ready, 1)
            p.memset(neg_max[:, :, :], 0.0)
            p.memset(V[:, :, :, :, :], 0.0).then_inc(ready, 1)
            p.wait_ge(ready, 2)
            p.memset(V[:, :, :, :, DH:DH + 1], 1.0).then_inc(ready, 1)
            p.wait_ge(ready, 3)
            p.memset(K[D_ROWS:NEG, :, :].bitcast(F32), 1.0).then_inc(ready, 1)
            p.wait_ge(ready, 4)
            head.start()
            head.pool_scale(p, 0, 0)
            p.wait_ge(loaded, 16 * 9)
            keys(None, 8)
            keys(None, 9)
            with p.Fori(0, PAIRS) as i:
                for G in range(GROUPS):
                    if G in (0, 4):
                        head.start()
                        head.pool_scale(p, 2 * i + G // 4 + 1, (G // 4 + 1) % 2)
                    keys(i, G + 2)
                    if G in (1, 3):
                        bias(i, G // 2)


def diff_layer(core, ctx, name):
    hi, lo = split_weights(core, ctx, name + "w", None, DF_COLS)
    weights_block(core, name + "w", "diff_w", hi, lo)
    diff_block(core, name, hi, lo)


HD, KV_TILES, PER_KV = 64, 2, 4
Q_TILES = KV_TILES * PER_KV
LI_Q, LI_QS = 0, Q_TILES * P
LI_K = LI_QS + Q_TILES * P
LI_KS = LI_K + KV_TILES * P
LI_V = LI_KS + KV_TILES * P
LI_O = LI_V + KV_TILES * P
LI_COLS = LI_O + Q_TILES * P


def light_block(core, name, w_hi, w_lo):
    nc, plan, ps, dram = core.nc, core.plan, core.psum, core.dram
    TR, R, S, O = 0, (1, 2, 3), (4, 5), (6, 7)
    GROUPS = 2 * KV_TILES
    SLOTS = GROUPS * NQ
    with ExitStack() as ctx:
        sb = lambda n, s, t=F32: ctx.enter_context(nc.sbuf_tensor(name + n, s, t))
        head = Head(core, ctx, name, "ln", core.x, TR)
        steps = lambda n: Steps(nc, ctx, plan, name + n)
        pe, act, vec, pool = steps("_tensor"), steps("_scalar"), steps("_vector"), steps("_pool")
        pe_seq, act_seq, vec_seq, pool_seq = (steps("_seq_tensor"), steps("_seq_scalar"), steps("_seq_vector"),
                                              steps("_seq_pool"))
        loaded = core_semaphore(nc, name + "_tables_loaded")
        ready = core_semaphore(nc, name + "_zeros_ready")
        cos, sin = sb("cos", [P, T]), sb("sin", [P, T])
        mask = sb("mask", [P, KV_TILES * 2, PER_KV * P])
        q_dec = sb("q_dec", [P, Q_TILES, 1, P])
        k_dec = sb("k_dec", [P, 4 * PER_KV])
        blk_dec = sb("blk_dec", [P, Q_TILES])
        turned = sb("turned", [P, 2, 2, T])
        qf = core.x2[:, :].rearrange("p (n t) -> p n t", t=T)
        q_hi, q_lo = sb("q_hi", [P, Q_TILES, T], F32R), sb("q_lo", [P, Q_TILES, T], F32R)
        kf = sb("kf", [P, KV_TILES, T])
        kz_hi = sb("kz_hi", [P, KV_TILES, 2, T], F32R)
        kz_lo = sb("kz_lo", [P, KV_TILES, 2, T], F32R)
        kt = sb("kt", [P, KV_TILES, 3, P])
        V = sb("V", [P, 2, NQ, KV_TILES * P])
        v_dec = sb("v_dec", [P, 2, 2, PER_KV, HD])
        state = sb("state", [P, NQ, PER_KV, P])
        decayed = sb("decayed", [P, PER_KV, P])
        A = sb("A", [P, 2, 2, T])
        o_hi, o_lo = sb("o_hi", [P, PER_KV, T], F32R), sb("o_lo", [P, PER_KV, T], F32R)
        out_sb = sb("out_sb", [P, T])
        block = ctx.enter_context(nc.Block())

        units = {0: ["k", "q0"], 1: ["q1", "q2"], 2: ["q3"], 3: []}
        order = ["k", "q0", "q1", "q2", "q3"]
        banks_of_unit = lambda n, gp, unit: [("proj", n, gp, unit, half) for half in range(2)]

        def slot_users(s):
            G, c = divmod(s, NQ)
            n, gp = divmod(G + 1, 2)
            users = [u for unit in units[c] for u in banks_of_unit(n, gp, unit)]
            if c == 2:
                users += [("v", n, gp, b) for b in range(2) if gp == 0] + [("kt", n, gp)]
            if c == 0 and G > 0:
                users += [("wo", G - 1)]
            if c < 3:
                users += [("kv", s)]
            return users

        users = [u for s in range(SLOTS) for u in slot_users(s)] + [("wo", GROUPS - 1)]
        bank_of = lambda user: R[users.index(user) % len(R)]

        def freed(i, user, back):
            if user[0] == "proj":
                return vec_seq.sem, vec_seq.done(2 * i + user[1] - 2 * back, "term", *user[2:])
            if user[0] in ("v", "kt"):
                return act_seq.sem, act_seq.done(2 * i + user[1] - 2 * back, user[0], *user[2:])
            if user[0] == "wo":
                eng = vec if user[1] % 2 else act
                return eng.sem, eng.done(i, *user, back=back)
            return vec.sem, vec.done(i, *user, back=back)

        def ring(t, i, user):
            at = users.index(user)
            if i is None:
                before = [m for m in range(at) if m % len(R) == at % len(R) and users[m][1:3] == user[1:3]
                          and users[m][0] in ("proj", "v", "kt")]
                if before:
                    t.wait_ge(*freed(-1, users[before[-1]], 0))
            else:
                back, m = earlier(at, len(R), len(users))
                t.wait_ge(*freed(i, users[m], back))
            return bank_of(user)

        def group_before(G):
            return (0, G - 2) if G >= 2 else (1, G + 2)

        def kv_place(s):
            return (s // NQ * 3 + s % NQ) % 2

        @block.sync
        def _(sp):
            for to, frm in ((cos[:, :], "rope_cos"), (sin[:, :], "rope_sin"), (mask[:, :, :], "light_mask"),
                            (q_dec[:, :, :, :], "light_q_dec"), (k_dec[:, :], "light_k_dec"), (blk_dec[:, :], "light_blk_dec")):
                sp.dma_start(to, dram[frm]).then_inc(loaded, 16)

        def seq_of(i, n):
            return 0 if i is None else 2 * i + n

        @block.tensor
        def _(t):
            pe.credit(t)
            pe_seq.credit(t)
            head.pe.credit(t)

            def project_unit(i, n, gp, unit):
                k, par = seq_of(i, n), n % 2
                if unit == "k" and gp == 0:
                    pe_seq.start()
                    t.wait_ge(head.low.sem, head.low.done(k, "lo"))
                cols = (LI_K + gp * P, LI_KS + gp * P) if unit == "k" else [c + (gp * 4 + int(unit[1])) * P for c in (LI_Q, LI_QS)]
                for user, c in zip(banks_of_unit(n, gp, unit), cols):
                    b = ring(t, i, user)
                    product(nc, ps[:, b, :], w_hi[:, c:c + P], w_lo[:, c:c + P], head.hi[:, par, :], head.lo[:, par, :]
                            ).then_inc(pe_seq.sem, pe_seq.step("proj", *user[2:]))

            def project_rest(i, n, gp):
                k, par = seq_of(i, n), n % 2
                if gp == 0:
                    for b2 in range(2):
                        b = ring(t, i, ("v", n, gp, b2))
                        for h in range(2):
                            c = slice((2 * b2 + h) * P, (2 * b2 + h + 1) * P)
                            ins = product3(nc, ps[:, b, h * 256:h * 256 + 256], head.hi[:, par, c], head.lo[:, par, c],
                                           w_hi[:, LI_V:LI_V + 256], w_lo[:, LI_V:LI_V + 256])
                        ins.then_inc(pe_seq.sem, pe_seq.step("v", gp, b2))
                t.wait_ge(pool_seq.sem, pool_seq.done(k, "sum", gp, "k"))
                b = ring(t, i, ("kt", n, gp))
                for c in range(3):
                    ins = nc.tensor.transpose(ps[:, b, c * P:(c + 1) * P], kf[:, gp, c * P:(c + 1) * P], core.ident[:, :])
                ins.then_inc(pe_seq.sem, pe_seq.step("kt", gp))

            def scores(i, s):
                G, c = divmod(s, NQ)
                n, gp = divmod(G, 2)
                if c == 0:
                    t.wait_ge(vec_seq.sem, vec_seq.done(2 * i + n, "lo", gp, "q3"))
                for r in range(2):
                    back, m = earlier(s, 1, SLOTS)
                    t.wait_ge(vec.sem, vec.done(i, "masked", m, r, back=back))
                    cc = slice(c * P, (c + 1) * P)
                    q = lambda part: part[:, gp * 4:gp * 4 + 4, cc]
                    product(nc, ps[:, S[r], :].rearrange("p (u t) -> p u t", t=P), kz_hi[:, gp, r, cc], kz_lo[:, gp, r, cc],
                            q(q_hi), q(q_lo)).then_inc(pe.sem, pe.step("scores", s, r))

            def attend(i, s):
                G, c = divmod(s, NQ)
                n, gp = divmod(G, 2)
                bank = O[s % 2]
                back, m = earlier(s, 2, SLOTS)
                t.wait_ge(vec.sem, vec.done(i, "o_lo", m, back=back))
                t.wait_ge(act_seq.sem, act_seq.done(2 * i + n, "v", 0, 1))
                for r in range(2):
                    g = 2 * gp + r
                    t.wait_ge(vec.sem, vec.done(i, "masked", s, r))
                    ins = nc.tensor.matmul(ps[64 * r:64 * r + 64, bank, :], V[:, n, c, g * HD:(g + 1) * HD], A[:, s % 2, r, :],
                                           start=True, stop=(c == 0), skip_group_check=True)
                if c > 0:
                    t.wait_ge(vec.sem, vec.done(i, "kv", s - 1))
                    t.wait_ge(pool_seq.sem, pool_seq.done(2 * i + n, "decay", gp, 3))
                    for u in range(PER_KV):
                        ins = nc.tensor.matmul(ps[:, bank, u * P:(u + 1) * P], state[:, c, u, :], qf[:, gp * 4 + u, c * P:(c + 1) * P],
                                               start=False, stop=True, skip_group_check=True)
                ins.then_inc(pe.sem, pe.step("o", s))
                if c < 3:
                    t.wait_ge(act_seq.sem, act_seq.done(2 * i + n, "kt", gp))
                    t.wait_ge(pool.sem, pool.done(i, "v_dec", s))
                    b = ring(t, i, ("kv", s))
                    vs = v_dec[:, kv_place(s), :, :, :].rearrange("p r u e -> p (r u e)")
                    nc.tensor.matmul(ps[:, b, :], kt[:, gp, c, :], vs, start=True, stop=True).then_inc(pe.sem, pe.step("kv", s))

            def output(i, G):
                t.wait_ge(vec.sem, vec.done(i, "o_lo", G * NQ + NQ - 1))
                b = ring(t, i, ("wo", G))
                for u in range(PER_KV):
                    c = LI_O + ((G % 2) * 4 + u) * P
                    ins = product(nc, ps[:, b, :], w_hi[:, c:c + P], w_lo[:, c:c + P], o_hi[:, u, :], o_lo[:, u, :],
                                  start=(u == 0), stop=(u == PER_KV - 1))
                ins.then_inc(pe.sem, pe.step("wo", G))

            def tail(i, n, k_head):
                t.wait_ge(head.low.sem, head.low.done(k_head, "lo"))
                t.wait_ge(vec.sem, vec.done(i, "wo", 2 * n + 1))
                for q in range(NQ):
                    ins = nc.tensor.transpose(ps[:, TR, q * P:(q + 1) * P], out_sb[:, q * P:(q + 1) * P], core.ident[:, :])
                ins.then_inc(pe.sem, pe.step("tail", n))

            head.start()
            head.tensor_tr(t, 0)
            for unit in order:
                project_unit(None, 2, 0, unit)
            project_rest(None, 2, 0)
            t.wait_ge(act_seq.sem, act_seq.done(0, "kt", 0))
            with t.Fori(0, PAIRS) as i:
                pe.start()
                scores(i, 0)
                for s in range(SLOTS):
                    G, c = divmod(s, NQ)
                    n, gp = divmod(G + 1, 2)
                    if s + 1 < SLOTS:
                        scores(i, s + 1)
                    for unit in units[c]:
                        project_unit(i, n, gp, unit)
                    if c == 2:
                        project_rest(i, n, gp)
                    if c == 0 and G > 0:
                        output(i, G - 1)
                    if c == 1 and G == 2:
                        tail(i, 0, 2 * i + 1)
                    if c == 3 and G == 0:
                        head.start()
                        t.wait_ge(vec.sem, vec.done(i, "tail", 1, back=1))
                        head.tensor_tr(t, 2 * i + 1)
                    if c == 3 and G == 2:
                        head.start()
                        t.wait_ge(vec.sem, vec.done(i, "tail", 0))
                        head.tensor_tr(t, 2 * i + 2)
                    attend(i, s)
                output(i, GROUPS - 1)
                tail(i, 1, 2 * i + 2)

        @block.scalar
        def _(a):
            act.credit(a)
            act_seq.credit(a)
            head.act.credit(a)
            copy = lambda to, frm: nc.scalar.activation(to, frm, ACT.Copy)

            def split_unit(i, n, gp, unit):
                k = seq_of(i, n)
                a.wait_ge(pool_seq.sem, pool_seq.done(k, "sum", gp, unit))
                if unit == "k":
                    if gp == 0:
                        act_seq.start()
                    for r in range(2):
                        rows = slice(64 * r, 64 * r + 64)
                        ins = copy(kz_hi[rows, gp, r, :], kf[rows, gp, :])
                    ins.then_inc(act_seq.sem, act_seq.step("hi", gp, unit))
                else:
                    q = gp * 4 + int(unit[1])
                    copy(q_hi[:, q, :], qf[:, q, :]).then_inc(act_seq.sem, act_seq.step("hi", gp, unit))

            def rest(i, n, gp):
                k = seq_of(i, n)
                if gp == 0:
                    if i is not None:
                        back, m = earlier(2 * n + 1, 4, 4)
                        a.wait_ge(pe.sem, pe.done(i, "o", m * NQ + NQ - 1, back=back))
                    for b2 in range(2):
                        a.wait_ge(pe_seq.sem, pe_seq.done(k, "v", gp, b2))
                        copy(V[:, n % 2, 2 * b2:2 * b2 + 2, :], ps[:, bank_of(("v", n, gp, b2)), :].rearrange("p (c e) -> p c e", e=256)
                             ).then_inc(act_seq.sem, act_seq.step("v", gp, b2))
                a.wait_ge(pe_seq.sem, pe_seq.done(k, "kt", gp))
                copy(kt[:, gp, :, :], ps[:, bank_of(("kt", n, gp)), 0:3 * P].rearrange("p (c e) -> p c e", e=P)
                     ).then_inc(act_seq.sem, act_seq.step("kt", gp))

            def o_part(i, s):
                G, c = divmod(s, NQ)
                if c == 0:
                    back, m = earlier(G, 1, GROUPS)
                    a.wait_ge(pe.sem, pe.done(i, "wo", m, back=back))
                a.wait_ge(pe.sem, pe.done(i, "o", s))
                copy(o_hi[:, :, c * P:(c + 1) * P], ps[:, O[s % 2], :].rearrange("p (u t) -> p u t", t=P)
                     ).then_inc(act.sem, act.step("o_hi", s))

            def out_part(i, G):
                back, m = earlier(G // 2, 1, 2)
                a.wait_ge(pe.sem, pe.done(i, "tail", m, back=back))
                a.wait_ge(pe.sem, pe.done(i, "wo", G))
                copy(out_sb[:, :], ps[:, bank_of(("wo", G)), :]).then_inc(act.sem, act.step("wo", G))

            head.start()
            head.scalar_hi(a, 0, 0)
            a.wait_ge(ready, 3)
            for unit in order:
                split_unit(None, 2, 0, unit)
            rest(None, 2, 0)
            with a.Fori(0, PAIRS) as i:
                act.start()
                for s in range(SLOTS):
                    G, c = divmod(s, NQ)
                    n, gp = divmod(G + 1, 2)
                    if s > 0:
                        o_part(i, s - 1)
                    if c == 0:
                        back, m = group_before(G + 1)
                        a.wait_ge(pe.sem, pe.done(i, "o", m * NQ + NQ - 1, back=back))
                    for unit in units[c]:
                        split_unit(i, n, gp, unit)
                    if c == 2:
                        rest(i, n, gp)
                    if c == 0 and G in (1, 3):
                        out_part(i, G - 1)
                    if c == 3 and G == 0:
                        head.start()
                        head.scalar_hi(a, 2 * i + 1, 1)
                    if c == 3 and G == 2:
                        head.start()
                        head.scalar_hi(a, 2 * i + 2, 0)
                o_part(i, SLOTS - 1)

        @block.vector
        def _(d):
            vec.credit(d)
            vec_seq.credit(d)
            head.vec.credit(d)
            head.low.credit(d)

            def head_before(k, par, seq):
                head.start()
                head.vector_stats(d, k, par, seq)
                head.vector_z(d, k, par, seq)

            def rotate(i, n, gp, unit):
                k = seq_of(i, n)
                if unit == "k" and gp == 0:
                    vec_seq.start()
                x = gp * len(order) + order.index(unit)
                back, m = earlier(x, 2, 2 * len(order))
                d.wait_ge(pool_seq.sem, pool_seq.done(k, "sum", m // len(order), order[m % len(order)], back=back))
                for half, (user, table) in enumerate(zip(banks_of_unit(n, gp, unit), (cos, sin))):
                    d.wait_ge(pe_seq.sem, pe_seq.done(k, "proj", *user[2:]))
                    nc.vector.tensor_tensor(turned[:, x % 2, half, :], ps[:, bank_of(user), :], table[:, :], ALU.mult
                                            ).then_inc(vec_seq.sem, vec_seq.step("term", *user[2:]))

            def low(i, n, gp, unit):
                k = seq_of(i, n)
                d.wait_ge(act_seq.sem, act_seq.done(k, "hi", gp, unit))
                if unit == "k":
                    for r in range(2):
                        rows = slice(64 * r, 64 * r + 64)
                        ins = nc.vector.tensor_tensor(kz_lo[rows, gp, r, :], kf[rows, gp, :], kz_hi[rows, gp, r, :], ALU.subtract)
                    ins.then_inc(vec_seq.sem, vec_seq.step("lo", gp, unit))
                else:
                    q = gp * 4 + int(unit[1])
                    nc.vector.tensor_tensor(q_lo[:, q, :], qf[:, q, :], q_hi[:, q, :], ALU.subtract
                                            ).then_inc(vec_seq.sem, vec_seq.step("lo", gp, unit))

            def masked(i, s):
                G, c = divmod(s, NQ)
                back, m = earlier(s, 2, SLOTS)
                d.wait_ge(pe.sem, pe.done(i, "o", m, back=back))
                for r in range(2):
                    d.wait_ge(pe.sem, pe.done(i, "scores", s, r))
                    nc.vector.tensor_tensor(A[:, s % 2, r, :], ps[:, S[r], :], mask[:, 2 * (G % 2) + r, :], ALU.mult
                                            ).then_inc(vec.sem, vec.step("masked", s, r))

            def state_after(i, s):
                G, c = divmod(s, NQ)
                back, m = earlier(G, 1, GROUPS)
                d.wait_ge(pe.sem, pe.done(i, "o", m * NQ + c + 1, back=back))
                if c > 0:
                    d.wait_ge(pool.sem, pool.done(i, "decayed", s))
                elif G > 0:
                    d.wait_ge(pool.sem, pool.done(i, "decayed", s - 2))
                else:
                    d.wait_ge(pool.sem, pool.done(i, "decayed", SLOTS - 2, back=1))
                d.wait_ge(pe.sem, pe.done(i, "kv", s))
                for r in range(2):
                    rows = slice(64 * r, 64 * r + 64)
                    new = ps[rows, bank_of(("kv", s)), r * 256:(r + 1) * 256].rearrange("p (u e) -> p u e", e=HD)
                    to = state[rows, c + 1, :, r * HD:(r + 1) * HD]
                    ins = (nc.vector.tensor_copy(to, new) if c == 0 else
                           nc.vector.tensor_tensor(to, new, decayed[rows, :, r * HD:(r + 1) * HD], ALU.add))
                ins.then_inc(vec.sem, vec.step("kv", s))

            def o_part(i, s):
                c = s % NQ
                cc = slice(c * P, (c + 1) * P)
                d.wait_ge(act.sem, act.done(i, "o_hi", s))
                nc.vector.tensor_tensor(o_lo[:, :, cc], ps[:, O[s % 2], :].rearrange("p (u t) -> p u t", t=P), o_hi[:, :, cc],
                                        ALU.subtract).then_inc(vec.sem, vec.step("o_lo", s))

            def out_part(i, G):
                d.wait_ge(act.sem, act.done(i, "wo", G - 1))
                d.wait_ge(pe.sem, pe.done(i, "wo", G))
                nc.vector.tensor_tensor(out_sb[:, :], ps[:, bank_of(("wo", G)), :], out_sb[:, :], ALU.add
                                        ).then_inc(vec.sem, vec.step("wo", G))

            def tail(i, n):
                d.wait_ge(pe.sem, pe.done(i, "tail", n))
                at = cut((2 * i + n) * T, T)
                nc.vector.tensor_tensor(core.x[:, at], core.x[:, at], ps[:, TR, :], ALU.add).then_inc(vec.sem, vec.step("tail", n))

            head_before(0, 0, 0)
            head.vector_lo(d, 0, 0)
            d.wait_ge(loaded, 16 * 6)
            d.wait_ge(ready, 3)
            for c in range(NQ):
                for unit in units[c - 1] if c else ():
                    low(None, 2, 0, unit)
                for unit in units[c]:
                    rotate(None, 2, 0, unit)
            with d.Fori(0, PAIRS) as i:
                vec.start()
                masked(i, 0)
                for s in range(SLOTS):
                    G, c = divmod(s, NQ)
                    n, gp = divmod(G + 1, 2)
                    if s > 0 and c > 0:
                        state_after(i, s - 1)
                    if c > 0:
                        for unit in units[c - 1]:
                            low(i, n, gp, unit)
                    if s + 1 < SLOTS:
                        masked(i, s + 1)
                    if s > 0:
                        o_part(i, s - 1)
                    if c == 1 and G == 2:
                        out_part(i, 1)
                    for unit in units[c]:
                        rotate(i, n, gp, unit)
                    if c == 1 and G == 2:
                        tail(i, 0)
                    if c == 2 and G == 0:
                        head_before(2 * i + 1, 1, 2 * i + 1)
                    if c == 3 and G == 0:
                        head.vector_lo(d, 2 * i + 1, 1)
                    if c == 2 and G == 2:
                        head_before(2 * i + 2, 0, (2 * i + 2) % NSEQ)
                    if c == 3 and G == 2:
                        head.vector_lo(d, 2 * i + 2, 0)
                o_part(i, SLOTS - 1)
                out_part(i, 3)
                tail(i, 1)

        @block.gpsimd
        def _(p):
            pool.credit(p)
            pool_seq.credit(p)
            head.pool.credit(p)

            def add_terms(i, n, gp, unit):
                k = seq_of(i, n)
                if unit == "k" and gp == 0:
                    pool_seq.start()
                x = gp * len(order) + order.index(unit)
                if i is not None and unit == "k":
                    back, m = group_before(2 * n + gp)
                    p.wait_ge(pe.sem, pe.done(i, "o", m * NQ + NQ - 1, back=back))
                p.wait_ge(vec_seq.sem, vec_seq.done(k, "term", gp, unit, 1))
                to = kf[:, gp, :] if unit == "k" else qf[:, gp * 4 + int(unit[1]), :]
                nc.gpsimd.tensor_tensor(to, turned[:, x % 2, 0, :], turned[:, x % 2, 1, :], ALU.add
                                        ).then_inc(pool_seq.sem, pool_seq.step("sum", gp, unit))

            def decay_queries(i, n, gp, u):
                k = seq_of(i, n)
                q = gp * 4 + u
                p.wait_ge(vec_seq.sem, vec_seq.done(k, "lo", gp, f"q{u}"))
                later = qf[:, q, P:T].rearrange("p (c t) -> p c t", t=P)
                nc.gpsimd.tensor_tensor(later, later, q_dec[:, q, :, :].to_broadcast([P, 3, P]), ALU.mult
                                        ).then_inc(pool_seq.sem, pool_seq.step("decay", gp, u))

            def values_decayed(i, s):
                G, c = divmod(s, NQ)
                n, gp = divmod(G, 2)
                back, m = earlier(G * 3 + c, 2, GROUPS * 3)
                p.wait_ge(pe.sem, pe.done(i, "kv", m // 3 * NQ + m % 3, back=back))
                p.wait_ge(act_seq.sem, act_seq.done(2 * i + n, "v", 0, 1))
                v = V[:, n, c, gp * P:(gp + 1) * P].rearrange("p (r e) -> p r e", e=HD).unsqueeze(2).to_broadcast([P, 2, PER_KV, HD])
                dec = k_dec[:, gp * 8:gp * 8 + 8].rearrange("p (r u) -> p r u", u=PER_KV).unsqueeze(3).to_broadcast([P, 2, PER_KV, HD])
                nc.gpsimd.tensor_tensor(v_dec[:, kv_place(s), :, :, :], v, dec, ALU.mult).then_inc(pool.sem, pool.step("v_dec", s))

            def decay_state(i, s):
                G, c = divmod(s, NQ)
                gp = G % 2
                p.wait_ge(vec.sem, vec.done(i, "kv", s - 1))
                dec = blk_dec[:, gp * 4:gp * 4 + 4].unsqueeze(2).to_broadcast([P, PER_KV, P])
                nc.gpsimd.tensor_tensor(decayed[:, :, :], state[:, c, :, :], dec, ALU.mult).then_inc(pool.sem, pool.step("decayed", s))

            p.memset(kz_hi[:, :, :, :].bitcast(F32), 0.0).then_inc(ready, 1)
            p.memset(kz_lo[:, :, :, :].bitcast(F32), 0.0).then_inc(ready, 1)
            p.memset(state[:, :, :, :], 0.0).then_inc(ready, 1)
            head.start()
            head.pool_scale(p, 0, 0)
            p.wait_ge(loaded, 16 * 6)
            for c in range(NQ):
                for unit in units[c]:
                    add_terms(None, 2, 0, unit)
                for unit in units[c - 1] if c else ():
                    if unit != "k":
                        decay_queries(None, 2, 0, int(unit[1]))
            with p.Fori(0, PAIRS) as i:
                pool.start()
                for s in range(SLOTS):
                    G, c = divmod(s, NQ)
                    n, gp = divmod(G + 1, 2)
                    if c < 3:
                        values_decayed(i, s)
                    if c in (1, 2):
                        decay_state(i, s)
                    for unit in units[c]:
                        add_terms(i, n, gp, unit)
                    if c > 0:
                        for unit in units[c - 1]:
                            if unit != "k":
                                decay_queries(i, n, gp, int(unit[1]))
                    if c == 2 and G == 0:
                        head.start()
                        head.pool_scale(p, 2 * i + 1, 1)
                    if c == 2 and G == 2:
                        head.start()
                        head.pool_scale(p, 2 * i + 2, 0)


def light_layer(core, ctx, name):
    hi, lo = split_weights(core, ctx, name + "w", None, LI_COLS)
    weights_block(core, name + "w", "light_w", hi, lo)
    light_block(core, name, hi, lo)


RA_K, RA_V, RA_R = 0, 2 * P, 4 * P
RA_COLS = 6 * P


def load_vectors(core, block, loaded, pairs):
    @block.sync
    def _(sp):
        for column, vector in pairs:
            sp.dma_start(column, vector.unsqueeze(1)).then_inc(loaded, 16)


def mixed(nc, out, w_hi, w_lo, c, head, par):
    now, before = slice(1, 1 + T), slice(0, T)
    a, b = slice(c, c + P), slice(c + P, c + 2 * P)
    product(nc, out, w_hi[:, a], w_lo[:, a], head.hi[:, par, now], head.lo[:, par, now], stop=False)
    return product(nc, out, w_hi[:, b], w_lo[:, b], head.hi[:, par, before], head.lo[:, par, before], start=False)


def time_mix_block(core, name, w_hi, w_lo):
    nc, plan, ps, d_ = core.nc, core.plan, core.psum, core.dram
    TR, KB, VB, RB = 0, (1, 2), (3, 4), (5, 6)
    J = (0, 1)
    with ExitStack() as ctx:
        sb = lambda n, s, t=F32: ctx.enter_context(nc.sbuf_tensor(name + n, s, t))
        cols = sb("cols", [P, 5])
        w, u, gain, bias, w_u = (cols[:, c:c + 1] for c in range(5))
        head = Head(core, ctx, name, "ln2", core.x, TR, affine=(gain, bias))
        vec, act = Steps(nc, ctx, plan, name + "_vector"), Steps(nc, ctx, plan, name + "_scalar")
        pe, pool = Steps(nc, ctx, plan, name + "_tensor"), Steps(nc, ctx, plan, name + "_pool")
        loaded = core_semaphore(nc, name + "_vectors_loaded")
        fixed = core_semaphore(nc, name + "_fixed_ready")
        two = lambda n, width=T: sb(n, [P, 2, width])
        kw, er, ec, ln_s = two("kw"), two("er"), two("ec"), two("ln_s")
        M, S, A = two("M", 1 + T), two("S", 1 + T), two("A", 1 + T)
        q, lower, upper, e1, e2 = two("q"), two("lower"), two("upper"), two("e1"), two("e2")
        ev, sig, r, y = two("ev"), two("sig"), two("r"), two("y")
        block = ctx.enter_context(nc.Block())
        load_vectors(core, block, loaded, [(w, d_["L0_attn_a_time_decay"]), (u, d_["L0_attn_a_time_first"]),
                                           (gain, d_["L0_attn_a_ln1_g"]), (bias, d_["L0_attn_a_ln1_b"])])

        @block.tensor
        def _(t):
            pe.credit(t)
            head.pe.credit(t)
            for k in J:
                head.start()
                head.tensor_tr(t, k)
            with t.Fori(0, PAIRS) as i:
                pe.start()
                t.wait_ge(fixed, 4)
                for j in J:
                    t.wait_ge(head.low.sem, head.low.done(2 * i + j, "lo"))
                    t.wait_ge(act.sem, act.done(i, "kw", j, back=1))
                    mixed(nc, ps[:, KB[j], :], w_hi, w_lo, RA_K, head, j).then_inc(pe.sem, pe.step("k", j))
                    t.wait_ge(vec.sem, vec.done(i, "y", j, back=1))
                    mixed(nc, ps[:, VB[j], :], w_hi, w_lo, RA_V, head, j).then_inc(pe.sem, pe.step("v", j))
                    t.wait_ge(act.sem, act.done(i, "r", j, back=1))
                    mixed(nc, ps[:, RB[j], :], w_hi, w_lo, RA_R, head, j).then_inc(pe.sem, pe.step("r", j))
                for j in J:
                    head.start()
                    if j == 0:
                        t.wait_ge(vec.sem, vec.done(i, "tail", 1, back=1))
                    head.tensor_tr(t, 2 * i + 2 + j)
                for j in J:
                    t.wait_ge(pool.sem, pool.done(i, "ry", j))
                    t.wait_ge(*((head.act.sem, head.act.done(2 * i + 3, "full")) if j == 0 else (vec.sem, vec.done(i, "tail", 0))))
                    for n in range(NQ):
                        ins = nc.tensor.transpose(ps[:, TR, n * P:(n + 1) * P], y[:, j, n * P:(n + 1) * P], core.ident[:, :])
                    ins.then_inc(pe.sem, pe.step("tail", j))

        @block.scalar
        def _(a):
            act.credit(a)
            head.act.credit(a)
            a.wait_ge(loaded, 16 * 4)
            for k in J:
                head.start()
                head.scalar_hi(a, k, k)
            a.wait_ge(fixed, 4)

            with a.Fori(0, PAIRS) as i:
                act.start()
                for j in J:
                    a.wait_ge(pe.sem, pe.done(i, "k", j))
                    a.wait_ge(pool.sem, pool.done(i, "q1", j, back=1))
                    nc.scalar.activation(kw[:, j, :], ps[:, KB[j], :], ACT.Identity, bias=w).then_inc(act.sem, act.step("kw", j))
                nc.scalar.preload_act_table_set("natural_log_exp_and_others")
                for j in J:
                    a.wait_ge(vec.sem, vec.done(i, "rr", j))
                    nc.scalar.activation(er[:, j, :], er[:, j, :], ACT.Exp, bias=w).then_inc(act.sem, act.step("er", j))
                    a.wait_ge(vec.sem, vec.done(i, "cc", j))
                    nc.scalar.activation(ec[:, j, :], ec[:, j, :], ACT.Exp).then_inc(act.sem, act.step("ec", j))
                for j in J:
                    a.wait_ge(vec.sem, vec.done(i, "S", j))
                    nc.scalar.activation(ln_s[:, j, :], S[:, j, 0:T], ACT.Ln).then_inc(act.sem, act.step("ln_s", j))
                for j in J:
                    a.wait_ge(vec.sem, vec.done(i, "upper", j))
                    nc.scalar.activation(e1[:, j, :], lower[:, j, :], ACT.Exp).then_inc(act.sem, act.step("e1", j))
                    nc.scalar.activation(e2[:, j, :], upper[:, j, :], ACT.Exp, scale=-1.0).then_inc(act.sem, act.step("e2", j))
                for j in J:
                    nc.scalar.activation(sig[:, j, :], q[:, j, :], ACT.Sigmoid, bias=w_u).then_inc(act.sem, act.step("sig", j))
                    a.wait_ge(pe.sem, pe.done(i, "r", j))
                    nc.scalar.activation(r[:, j, :], ps[:, RB[j], :], ACT.Sigmoid).then_inc(act.sem, act.step("r", j))
                for j in J:
                    head.start()
                    head.scalar_hi(a, 2 * i + 2 + j, j)

        @block.vector
        def _(d):
            vec.credit(d)
            head.vec.credit(d)
            head.low.credit(d)
            d.wait_ge(loaded, 16 * 4)
            nc.vector.memset(M[:, :, 0:1], -1e38).then_inc(fixed, 1)
            nc.vector.memset(S[:, :, 0:1], 1.0)
            nc.vector.memset(A[:, :, 0:1], 0.0)
            nc.vector.memset(head.hi[:, :, 0:1].bitcast(F32), 0.0).then_inc(fixed, 1)
            nc.vector.memset(head.lo[:, :, 0:1].bitcast(F32), 0.0).then_inc(fixed, 1)
            nc.vector.tensor_tensor(w_u, w, u, ALU.subtract).then_inc(fixed, 1)
            for k in J:
                head.start()
                head.vector_stats(d, k, k, k)
                head.vector_z(d, k, k, k)
                head.vector_lo(d, k, k)
            n = nc.vector
            with d.Fori(0, PAIRS) as i:
                vec.start()
                inc = lambda ins, *key: ins.then_inc(vec.sem, vec.step(*key))
                head.start()
                for j in J:
                    d.wait_ge(act.sem, act.done(i, "kw", j))
                    d.wait_ge(pool.sem, pool.done(i, "q1", j, back=1))
                    inc(n.tensor_tensor_scan(M[:, j, 1:1 + T], w.to_broadcast([P, T]), kw[:, j, :], -1e38, ALU.add, ALU.max), "M", j)
                for j in J:
                    d.wait_ge(vec.sem, vec.done(i, "M", j))
                    d.wait_ge(vec.sem, vec.done(i, "S", j, back=1))
                    inc(n.tensor_tensor(er[:, j, :], M[:, j, 0:T], M[:, j, 1:1 + T], ALU.subtract), "rr", j)
                    inc(n.tensor_tensor(ec[:, j, :], kw[:, j, :], M[:, j, 1:1 + T], ALU.subtract), "cc", j)
                for j in J:
                    head.start()
                    k, seq = 2 * i + 2 + j, (2 * i + 2 + j) % NSEQ
                    head.vector_stats(d, k, j, seq)
                    if j == 0:
                        d.wait_ge(act.sem, act.done(i, "ec", 0))
                        d.wait_ge(act.sem, act.done(i, "ln_s", 0, back=1))
                        inc(n.tensor_tensor_scan(S[:, 0, 1:1 + T], er[:, 0, :], ec[:, 0, :], 1.0, ALU.mult, ALU.add), "S", 0)
                    else:
                        d.wait_ge(act.sem, act.done(i, "ec", 1))
                        d.wait_ge(act.sem, act.done(i, "ln_s", 1, back=1))
                        inc(n.tensor_tensor_scan(S[:, 1, 1:1 + T], er[:, 1, :], ec[:, 1, :], 1.0, ALU.mult, ALU.add), "S", 1)
                    head.vector_z(d, k, j, seq)
                for j in J:
                    d.wait_ge(pool.sem, pool.done(i, "q", j))
                    d.wait_ge(act.sem, act.done(i, "e1", j, back=1))
                    d.wait_ge(act.sem, act.done(i, "e2", j, back=1))
                    inc(n.tensor_scalar(lower[:, j, :], q[:, j, :], w, 0.0, ALU.add, ALU.min), "lower", j)
                    inc(n.tensor_scalar(upper[:, j, :], q[:, j, :], w, 0.0, ALU.add, ALU.max), "upper", j)
                for j in J:
                    d.wait_ge(pe.sem, pe.done(i, "v", j))
                    d.wait_ge(act.sem, act.done(i, "e2", j))
                    d.wait_ge(vec.sem, vec.done(i, "A", j, back=1))
                    inc(n.tensor_tensor(ev[:, j, :], e2[:, j, :], ps[:, VB[j], :], ALU.mult), "ev", j)
                for j in J:
                    d.wait_ge(vec.sem, vec.done(i, "ev", j))
                    d.wait_ge(act.sem, act.done(i, "e1", j))
                    inc(n.tensor_tensor_scan(A[:, j, 1:1 + T], e1[:, j, :], ev[:, j, :], 0.0, ALU.mult, ALU.add), "A", j)
                for j in J:
                    d.wait_ge(vec.sem, vec.done(i, "A", j))
                    d.wait_ge(pe.sem, pe.done(i, "tail", j, back=1))
                    inc(n.tensor_tensor(y[:, j, :], A[:, j, 0:T], ps[:, VB[j], :], ALU.subtract), "a_v", j)
                for j in J:
                    d.wait_ge(pool.sem, pool.done(i, "sy", j))
                    inc(n.tensor_tensor(y[:, j, :], y[:, j, :], ps[:, VB[j], :], ALU.add), "y", j)
                for j in J:
                    head.start()
                    head.vector_lo(d, 2 * i + 2 + j, j)
                for j in J:
                    d.wait_ge(head.kept.sem, head.kept.done(2 * i + j, "keep"))
                    d.wait_ge(pe.sem, pe.done(i, "tail", j))
                    inc(n.tensor_tensor(core.x2[:, cut((2 * i + j) * T, T)], head.keep[:, j, :], ps[:, TR, :], ALU.add), "tail", j)

        @block.gpsimd
        def _(p):
            pool.credit(p)
            head.pool.credit(p)
            head.kept.credit(p)
            p.wait_ge(fixed, 4)
            for k in J:
                head.start()
                head.pool_scale(p, k, k)
                head.pool_keep(p, k, k, k)
            tt = nc.gpsimd.tensor_tensor
            with p.Fori(0, PAIRS) as i:
                pool.start()
                for j in J:
                    p.wait_ge(vec.sem, vec.done(i, "cc", j))
                    p.wait_ge(act.sem, act.done(i, "sig", j, back=1))
                    p.wait_ge(vec.sem, vec.done(i, "upper", j, back=1))
                    tt(q[:, j, :], M[:, j, 0:T], kw[:, j, :], ALU.subtract).then_inc(pool.sem, pool.step("q1", j))
                for j in J:
                    head.start()
                    head.pool_scale(p, 2 * i + 2 + j, j)
                for j in J:
                    p.wait_ge(act.sem, act.done(i, "ln_s", j))
                    p.wait_ge(pool.sem, pool.done(i, "q1", j))
                    tt(q[:, j, :], q[:, j, :], ln_s[:, j, :], ALU.add).then_inc(pool.sem, pool.step("q", j))
                for j in J:
                    p.wait_ge(act.sem, act.done(i, "sig", j))
                    p.wait_ge(vec.sem, vec.done(i, "a_v", j))
                    tt(y[:, j, :], y[:, j, :], sig[:, j, :], ALU.mult).then_inc(pool.sem, pool.step("sy", j))
                for j in J:
                    p.wait_ge(act.sem, act.done(i, "r", j))
                    p.wait_ge(vec.sem, vec.done(i, "y", j))
                    tt(y[:, j, :], y[:, j, :], r[:, j, :], ALU.mult).then_inc(pool.sem, pool.step("ry", j))
                for j in J:
                    head.start()
                    p.wait_ge(vec.sem, vec.done(i, "tail", j))
                    head.pool_keep(p, 2 * i + 2 + j, j, (2 * i + 2 + j) % NSEQ)


RB_CK, RB_CR = 0, 8 * P
RB_CV = RB_CR + 2 * P
RB_COLS = RB_CV + 4 * P


def channel_mix_block(core, name, w_hi, w_lo):
    nc, plan, ps, d_ = core.nc, core.plan, core.psum, core.dram
    TR, H, CR, OUT = 0, (1, 2, 3), 4, 5
    FT = 4
    NS, LAG, RING = 2 * FT, 2, 4
    with ExitStack() as ctx:
        sb = lambda n, s, t=F32: ctx.enter_context(nc.sbuf_tensor(name + n, s, t))
        cols = sb("cols", [P, 2])
        head = Head(core, ctx, name, "ln", core.x2, TR, affine=(cols[:, 0:1], cols[:, 1:2]))
        vec, act = Steps(nc, ctx, plan, name + "_vector"), Steps(nc, ctx, plan, name + "_scalar")
        pe, pool = Steps(nc, ctx, plan, name + "_tensor"), Steps(nc, ctx, plan, name + "_pool")
        loaded = core_semaphore(nc, name + "_vectors_loaded")
        fixed = core_semaphore(nc, name + "_fixed_ready")
        a_sb, sq = sb("relu", [P, 2, T]), sb("square", [P, 2, T])
        sq_hi, sq_lo = sb("square_hi", [P, RING, T], F32R), sb("square_lo", [P, RING, T], F32R)
        gate, out_sb = sb("gate", [P, T]), sb("out_sb", [P, T])
        block = ctx.enter_context(nc.Block())
        load_vectors(core, block, loaded, [(cols[:, 0:1], d_["L0_attn_a_ln2_g"]), (cols[:, 1:2], d_["L0_attn_a_ln2_b"])])

        @block.tensor
        def _(t):
            pe.credit(t)
            head.pe.credit(t)
            head.start()
            head.tensor_tr(t, 0)
            t.wait_ge(fixed, 2)

            def down(i, n):
                j, f = divmod(n, FT)
                if f == 0:
                    back, m = earlier(j, 1, 2)
                    t.wait_ge(vec.sem, vec.done(i, "out", m, back=back))
                t.wait_ge(vec.sem, vec.done(i, "sq_lo", n))
                c = RB_CV + f * P
                product(nc, ps[:, OUT, :], w_hi[:, c:c + P], w_lo[:, c:c + P], sq_hi[:, n % RING, :], sq_lo[:, n % RING, :],
                        start=(f == 0), stop=(f == FT - 1)).then_inc(pe.sem, pe.step("down", n))

            def tail(i, j):
                t.wait_ge(vec.sem, vec.done(i, "out", j))
                t.wait_ge(head.act.sem, head.act.done(2 * i + j + 1, "full"))
                for q in range(NQ):
                    ins = nc.tensor.transpose(ps[:, TR, q * P:(q + 1) * P], out_sb[:, q * P:(q + 1) * P], core.ident[:, :])
                ins.then_inc(pe.sem, pe.step("tail", j))

            with t.Fori(0, PAIRS) as i:
                pe.start()
                for n in range(NS):
                    j, f = divmod(n, FT)
                    if f == 0:
                        t.wait_ge(head.low.sem, head.low.done(2 * i + j, "lo"))
                        back, m = earlier(j, 1, 2)
                        t.wait_ge(act.sem, act.done(i, "gate", m, back=back))
                        mixed(nc, ps[:, CR, :], w_hi, w_lo, RB_CR, head, j).then_inc(pe.sem, pe.step("cr", j))
                    back, m = earlier(n, len(H), NS)
                    t.wait_ge(act.sem, act.done(i, "relu", m, back=back))
                    c = RB_CK + f * 2 * P
                    mixed(nc, ps[:, H[n % 3], :], w_hi, w_lo, c, head, j).then_inc(pe.sem, pe.step("ck", n))
                    if n >= LAG:
                        down(i, n - LAG)
                    if f == 1:
                        head.start()
                        t.wait_ge(vec.sem, vec.done(i, "tail", 0) if False else vec.done(i, "tail", 1, back=1)) if j == 0 else None
                        if j == 0:
                            head.tensor_tr(t, 2 * i + 1)
                    if j == 1 and f == 2:
                        tail(i, 0)
                        head.start()
                        t.wait_ge(vec.sem, vec.done(i, "tail", 0))
                        head.tensor_tr(t, 2 * i + 2)
                for n in range(NS - LAG, NS):
                    down(i, n)
                tail(i, 1)

        @block.scalar
        def _(a):
            act.credit(a)
            head.act.credit(a)
            a.wait_ge(loaded, 32)
            head.start()
            head.scalar_hi(a, 0, 0)

            def part(i, n):
                back, m = earlier(n, RING, NS)
                a.wait_ge(pe.sem, pe.done(i, "down", m, back=back))
                a.wait_ge(pool.sem, pool.done(i, "sq", n))
                nc.scalar.activation(sq_hi[:, n % RING, :], sq[:, n % 2, :], ACT.Copy).then_inc(act.sem, act.step("sq_hi", n))

            with a.Fori(0, PAIRS) as i:
                act.start()
                for n in range(NS):
                    j, f = divmod(n, FT)
                    if f == 0:
                        back, m = earlier(j, 1, 2)
                        a.wait_ge(pe.sem, pe.done(i, "cr", j))
                        if j == 0:
                            a.wait_ge(vec.sem, vec.done(i, "out", 1, back=1))
                            nc.scalar.activation(gate[:, :], ps[:, CR, :], ACT.Sigmoid).then_inc(act.sem, act.step("gate", 0))
                    back, m = earlier(n, 2, NS)
                    a.wait_ge(pool.sem, pool.done(i, "sq", m, back=back))
                    a.wait_ge(pe.sem, pe.done(i, "ck", n))
                    nc.scalar.activation(a_sb[:, n % 2, :], ps[:, H[n % 3], :], ACT.Relu).then_inc(act.sem, act.step("relu", n))
                    if n >= 1:
                        part(i, n - 1)
                    if j == 1 and f == 2:
                        a.wait_ge(vec.sem, vec.done(i, "out", 0))
                        nc.scalar.activation(gate[:, :], ps[:, CR, :], ACT.Sigmoid).then_inc(act.sem, act.step("gate", 1))
                    if n == 1:
                        head.start()
                        head.scalar_hi(a, 2 * i + 1, 1)
                part(i, NS - 1)
                head.start()
                head.scalar_hi(a, 2 * i + 2, 0)

        @block.vector
        def _(d):
            vec.credit(d)
            head.vec.credit(d)
            head.low.credit(d)
            nc.vector.memset(head.hi[:, :, 0:1].bitcast(F32), 0.0).then_inc(fixed, 1)
            nc.vector.memset(head.lo[:, :, 0:1].bitcast(F32), 0.0).then_inc(fixed, 1)

            def before(k, par, seq):
                head.start()
                head.vector_stats(d, k, par, seq)
                head.vector_z(d, k, par, seq)

            before(0, 0, 0)
            head.vector_lo(d, 0, 0)

            def out(i, j):
                d.wait_ge(pe.sem, pe.done(i, "down", j * FT + FT - 1))
                d.wait_ge(act.sem, act.done(i, "gate", j))
                back, m = earlier(j, 1, 2)
                d.wait_ge(pe.sem, pe.done(i, "tail", m, back=back))
                nc.vector.tensor_tensor(out_sb[:, :], gate[:, :], ps[:, OUT, :], ALU.mult).then_inc(vec.sem, vec.step("out", j))

            def tail(i, j):
                d.wait_ge(pe.sem, pe.done(i, "tail", j))
                d.wait_ge(pool.sem, pool.done(i, "added", j))
                at = cut((2 * i + j) * T, T)
                nc.vector.tensor_tensor(core.x[:, at], core.x[:, at], ps[:, TR, :], ALU.add).then_inc(vec.sem, vec.step("tail", j))

            def part(i, n):
                d.wait_ge(act.sem, act.done(i, "sq_hi", n))
                nc.vector.tensor_tensor(sq_lo[:, n % RING, :], sq[:, n % 2, :], sq_hi[:, n % RING, :],
                                        ALU.subtract).then_inc(vec.sem, vec.step("sq_lo", n))

            with d.Fori(0, PAIRS) as i:
                vec.start()
                before(2 * i + 1, 1, 2 * i + 1)
                for n in range(NS):
                    j, f = divmod(n, FT)
                    if n >= 1:
                        part(i, n - 1)
                    if n == 2:
                        head.vector_lo(d, 2 * i + 1, 1)
                    if n == 5:
                        out(i, 0)
                    if n == 6:
                        before(2 * i + 2, 0, (2 * i + 2) % NSEQ)
                        tail(i, 0)
                part(i, NS - 1)
                head.vector_lo(d, 2 * i + 2, 0)
                out(i, 1)
                tail(i, 1)

        @block.gpsimd
        def _(p):
            pool.credit(p)
            head.pool.credit(p)
            head.start()
            head.pool_scale(p, 0, 0)
            with p.Fori(0, PAIRS) as i:
                pool.start()
                head.start()
                head.pool_scale(p, 2 * i + 1, 1)
                for n in range(NS):
                    j, f = divmod(n, FT)
                    p.wait_ge(act.sem, act.done(i, "relu", n))
                    back, m = earlier(n, 2, NS)
                    p.wait_ge(vec.sem, vec.done(i, "sq_lo", m, back=back))
                    nc.gpsimd.tensor_tensor(sq[:, n % 2, :], a_sb[:, n % 2, :], a_sb[:, n % 2, :], ALU.mult).then_inc(pool.sem, pool.step("sq", n))
                    if f == 1:
                        at = cut((2 * i + j) * T, T)
                        nc.gpsimd.tensor_tensor(core.x[:, at], core.x[:, at], core.x2[:, at], ALU.add).then_inc(pool.sem, pool.step("added", j))
                    if n == 6:
                        head.start()
                        head.pool_scale(p, 2 * i + 2, 0)


def rwkv_layer(core, ctx, name):
    d = core.dram
    with ExitStack() as own:
        hi, lo = split_weights(core, own, name + "a", None, RA_COLS)
        weights_block(core, name + "a", "time_w", hi, lo,
                      [(c + P * prev, c + P * prev + P, d["L0_attn_a_mix_" + m].unsqueeze(1)) + ("one minus",) * prev
                       for c, m in ((RA_K, "k"), (RA_V, "v"), (RA_R, "r")) for prev in (0, 1)])
        time_mix_block(core, name + "t", hi, lo)
    with ExitStack() as own:
        hi, lo = split_weights(core, own, name + "b", None, RB_COLS)
        weights_block(core, name + "b", "channel_w", hi, lo,
                      [(c + P * prev, c + P * prev + P, d["L0_attn_a_cmix_" + m].unsqueeze(1)) + ("one minus",) * prev
                       for c, m in [(RB_CK + 2 * P * f, "k") for f in range(4)] + [(RB_CR, "r")] for prev in (0, 1)])
        channel_mix_block(core, name + "c", hi, lo)


class Moe:

    def __init__(self, shared, experts, tiles):
        self.shared, self.experts, self.tiles = shared, experts, tiles
        self.slots = shared + experts
        self.w1 = 8
        self.w3 = self.w1 + self.slots * tiles * P
        self.w2 = self.w3 + self.slots * tiles * P
        self.cols = self.w2 + self.slots * tiles * P


MOE0 = Moe(1, 8, 1)
MOE1 = Moe(0, 8, 2)


def earlier(n, ring, total):
    if n >= ring:
        return 0, n - ring
    return 1, max(m for m in range(total) if m % ring == n % ring)


def moe_block(core, name, moe, w_hi, w_lo, kind, src, add_to, bias):
    nc, plan, NE, HT = core.nc, core.plan, moe.slots, moe.tiles
    NS = 2 * NE
    LAG, RING = 2, 4
    H1, H3, BC, OUT, TR, GATE = (0, 1), (2, 3), 4, 5, 6, 7
    ps = core.psum
    with ExitStack() as ctx:
        sb = lambda n, s, t=F32: ctx.enter_context(nc.sbuf_tensor(name + n, s, t))
        head = Head(core, ctx, name, kind, src, TR)
        vec, act = Steps(nc, ctx, plan, name + "_vector"), Steps(nc, ctx, plan, name + "_scalar")
        pe, pool = Steps(nc, ctx, plan, name + "_tensor"), Steps(nc, ctx, plan, name + "_pool")
        bias_loaded = core_semaphore(nc, name + "_bias_loaded")
        bias_sb = sb("bias", [P, 8]) if bias is not None else None
        logits, top, idx = sb("logits", [P, NQ, 8]), sb("top", [P, NQ, 8]), sb("idx", [P, NQ, 8], U32)
        ex = sb("ex", [P, NQ, 8])
        lmax, lsum = sb("lmax", [P, NQ]), sb("lsum", [P, NQ])
        idxf, diff, e2, den, p1, p2 = (sb(n, s) for n, s in (("idxf", [P, NQ, 2]), ("diff", [P, NQ]), ("e2", [P, NQ]),
                                                             ("den", [P, NQ]), ("p1", [P, NQ]), ("p2", [P, NQ])))
        hot1, hot2 = sb("hot1", [P, NQ, 8]), sb("hot2", [P, NQ, 8])
        comb = sb("comb", [P, 2, NQ, 8])
        bcs = sb("bcs", [P, 2, T])
        s = sb("s", [P, 2, HT, T])
        sc = sb("sc", [P, 2, HT, T])
        g = sb("g", [P, 2, HT, T])
        g_hi, g_lo = sb("g_hi", [P, RING, HT, T], F32R), sb("g_lo", [P, RING, HT, T], F32R)
        out_sb = sb("out_sb", [P, T])
        block = ctx.enter_context(nc.Block())

        def is_shared(n):
            return n % NE < moe.shared

        def prev_scaled(n, ring=1):
            m, back = n - ring, 0
            while True:
                if m < 0:
                    m, back = m + NS, 1
                if not is_shared(m):
                    return back, m
                m -= ring

        def gate_tensor(t, k, par):
            h = head
            t.wait_ge(h.act.sem, h.act.done(k, "hi"))
            t.wait_ge(h.low.sem, h.low.done(k, "lo"))
            t.wait_ge(h.vec.sem, h.vec.done(k, "logits", back=1))
            for q in range(NQ):
                c = slice(q * P, (q + 1) * P)
                ins = product3(nc, ps[:, GATE, q * 8:q * 8 + 8], h.hi[:, par, c], h.lo[:, par, c], w_hi[:, 0:8], w_lo[:, 0:8])
            ins.then_inc(h.pe.sem, h.pe.step("gate"))

        def gate_vector(d, k, par):
            h, v, n = head, head.vec, nc.vector
            inc = lambda ins, *key: ins.then_inc(v.sem, v.step(*key))
            wait = lambda *key: d.wait_ge(v.sem, v.done(k, *key))
            gate = ps[:, GATE, 0:NQ * 8].rearrange("p (q e) -> p q e", e=8)
            wide = lambda a: a.unsqueeze(2).to_broadcast([P, NQ, 8])
            d.wait_ge(h.pe.sem, h.pe.done(k, "gate"))
            if bias is None:
                inc(n.tensor_copy(logits[:, :, :], gate), "logits")
                values = logits
            else:
                inc(n.tensor_tensor(logits[:, :, :], gate, bias_sb[:, :].unsqueeze(1).to_broadcast([P, NQ, 8]), ALU.add), "logits")
                wait("logits")
                inc(n.tensor_reduce(lmax[:, :], logits[:, :, :], AXX, ALU.max), "lmax")
                wait("lmax")
                inc(n.tensor_tensor(hot1[:, :, :], logits[:, :, :], wide(lmax[:, :]), ALU.subtract), "shifted")
                wait("shifted")
                inc(n.tensor_scalar(hot2[:, :, :], hot1[:, :, :], LOG2E, None, ALU.mult), "shifted2")
                d.wait_ge(h.pool.sem, h.pool.done(k, "ex"))
                inc(n.reduce_sum(lsum[:, :], ex[:, :, :], AXX), "lsum")
                wait("lsum")
                inc(n.reciprocal(den[:, :], lsum[:, :]), "lrec")
                wait("lrec")
                inc(n.tensor_tensor(logits[:, :, :], ex[:, :, :], wide(den[:, :]), ALU.mult), "rw")
                wait("rw")
                values = logits
            if bias is None:
                wait("logits")
            settle(core, d)
            for q in range(NQ):
                inc(n.max(top[:, q, :], values[:, q, :]), "top", q)
            wait("top", NQ - 1)
            settle(core, d)
            for q in range(NQ):
                inc(n.max_index(idx[:, q, :], top[:, q, :], values[:, q, :]), "idx", q)
            inc(n.tensor_tensor(diff[:, :], top[:, :, 1], top[:, :, 0], ALU.subtract), "diff")
            wait("diff")
            inc(n.tensor_scalar(p1[:, :], diff[:, :], LOG2E, None, ALU.mult), "diff2")
            inc(n.tensor_copy(idxf[:, :, :], idx[:, :, 0:2]), "idxf")
            wait("idxf")
            it = core.iota[:, :].unsqueeze(1).to_broadcast([P, NQ, 8])
            inc(n.tensor_tensor(hot1[:, :, :], idxf[:, :, 0:1].to_broadcast([P, NQ, 8]), it, ALU.is_equal), "hot1")
            inc(n.tensor_tensor(hot2[:, :, :], idxf[:, :, 1:2].to_broadcast([P, NQ, 8]), it, ALU.is_equal), "hot2")
            d.wait_ge(h.pool.sem, h.pool.done(k, "e2"))
            inc(n.tensor_scalar(den[:, :], e2[:, :], 1.0, None, ALU.add), "den")
            wait("den")
            inc(n.reciprocal(p1[:, :], den[:, :]), "p1")
            wait("p1")
            inc(n.tensor_tensor(p2[:, :], p1[:, :], e2[:, :], ALU.mult), "p2")
            inc(n.tensor_tensor(hot1[:, :, :], hot1[:, :, :], wide(p1[:, :]), ALU.mult), "c1")
            wait("p2")
            inc(n.tensor_tensor(hot2[:, :, :], hot2[:, :, :], wide(p2[:, :]), ALU.mult), "c2")
            wait("c2")
            inc(n.tensor_tensor(comb[:, par, :, :], hot1[:, :, :], hot2[:, :, :], ALU.add), "comb")

        def gate_pool(p, k):
            h, o = head, head.pool
            if bias is not None:
                p.wait_ge(h.vec.sem, h.vec.done(k, "shifted2"))
                nc.gpsimd.tensor_tensor(ex[:, :, :], core.two.rearrange("p (q e) -> p q e", e=8), hot2[:, :, :],
                                        ALU.pow).then_inc(o.sem, o.step("ex"))
            p.wait_ge(h.vec.sem, h.vec.done(k, "diff2"))
            nc.gpsimd.tensor_tensor(e2[:, :], core.two[:, 0:NQ], p1[:, :], ALU.pow).then_inc(o.sem, o.step("e2"))

        def head_vector_all(d, k, par, seq):
            head.start()
            head.vector_stats(d, k, par, seq)
            head.vector_z(d, k, par, seq)
            head.vector_lo(d, k, par)
            gate_vector(d, k, par)

        @block.sync
        def _(sp):
            if bias is not None:
                sp.dma_start(bias_sb[:, :], bias.unsqueeze(0).to_broadcast([P, 8])).then_inc(bias_loaded, 16)

        @block.tensor
        def _(t):
            pe.credit(t)
            head.pe.credit(t)
            head.pe.start()
            head.tensor_tr(t, 0)
            gate_tensor(t, 0, 0)

            def up(i, n):
                j, e = divmod(n, NE)
                hi, lo = head.hi[:, j, :], head.lo[:, j, :]
                if e == 0:
                    t.wait_ge(head.low.sem, head.low.done(2 * i + j, "lo"))
                if not is_shared(n):
                    if e == moe.shared:
                        t.wait_ge(head.vec.sem, head.vec.done(2 * i + j, "comb"))
                    back, m = prev_scaled(n)
                    t.wait_ge(act.sem, act.done(i, "bc", m, back=back))
                    for q in range(NQ):
                        ins = nc.tensor.transpose(ps[:, BC, q * P:(q + 1) * P],
                                                  comb[:, j, q, e - moe.shared:e - moe.shared + 1].to_broadcast([P, P]),
                                                  core.ident[:, :])
                    ins.then_inc(pe.sem, pe.step("bc", n))
                for h in range(HT):
                    u = n * HT + h
                    c = e * HT * P + h * P
                    back, m = earlier(u, 2, NS * HT)
                    t.wait_ge(act.sem, act.done(i, "silu", m, back=back))
                    product(nc, ps[:, H1[u % 2], :], w_hi[:, moe.w1 + c:moe.w1 + c + P], w_lo[:, moe.w1 + c:moe.w1 + c + P],
                            hi, lo).then_inc(pe.sem, pe.step("h1", u))
                    t.wait_ge(vec.sem, vec.done(i, "g", m, back=back))
                    product(nc, ps[:, H3[u % 2], :], w_hi[:, moe.w3 + c:moe.w3 + c + P], w_lo[:, moe.w3 + c:moe.w3 + c + P],
                            hi, lo).then_inc(pe.sem, pe.step("h3", u))

            def down(i, n):
                j, e = divmod(n, NE)
                if e == 0:
                    back, m = earlier(j, 1, 2)
                    t.wait_ge(act.sem, act.done(i, "out", m, back=back))
                for h in range(HT):
                    u = n * HT + h
                    c = moe.w2 + e * HT * P + h * P
                    t.wait_ge(vec.sem, vec.done(i, "g_lo", u))
                    ins = product(nc, ps[:, OUT, :], w_hi[:, c:c + P], w_lo[:, c:c + P], g_hi[:, n % RING, h, :],
                                  g_lo[:, n % RING, h, :], start=(e == 0 and h == 0), stop=(e == NE - 1 and h == HT - 1))
                ins.then_inc(pe.sem, pe.step("down", n))

            def tail(i, j):
                t.wait_ge(act.sem, act.done(i, "out", j))
                t.wait_ge(head.low.sem, head.low.done(2 * i + j + 1, "lo"))
                for q in range(NQ):
                    ins = nc.tensor.transpose(ps[:, TR, q * P:(q + 1) * P], out_sb[:, q * P:(q + 1) * P], core.ident[:, :])
                ins.then_inc(pe.sem, pe.step("tail", j))

            with t.Fori(0, PAIRS) as i:
                pe.start()
                for n in range(NS):
                    j, e = divmod(n, NE)
                    up(i, n)
                    if n >= LAG:
                        down(i, n - LAG)
                    if j == 1 and e == LAG:
                        tail(i, 0)
                    if e == 4:
                        head.pe.start()
                        t.wait_ge(vec.sem, vec.done(i, "tail", 0) if j else vec.done(i, "tail", 1, back=1))
                        head.tensor_tr(t, 2 * i + j + 1)
                    if e == 6:
                        gate_tensor(t, 2 * i + j + 1, 1 - j)
                for n in range(NS - LAG, NS):
                    down(i, n)
                tail(i, 1)

        @block.scalar
        def _(a):
            act.credit(a)
            head.act.credit(a)
            head.act.start()
            head.scalar_hi(a, 0, 0)

            def g_part(i, n, h):
                u = n * HT + h
                back, m = earlier(n, RING, NS)
                a.wait_ge(vec.sem, vec.done(i, "g", u))
                a.wait_ge(pe.sem, pe.done(i, "down", m, back=back))
                nc.scalar.activation(g_hi[:, n % RING, h, :], g[:, n % 2, h, :], ACT.Copy).then_inc(act.sem, act.step("g_hi", u))

            def out(i, j):
                a.wait_ge(pe.sem, pe.done(i, "down", (j + 1) * NE - 1))
                back, m = earlier(j, 1, 2)
                a.wait_ge(pe.sem, pe.done(i, "tail", m, back=back))
                nc.scalar.activation(out_sb[:, :], ps[:, OUT, :], ACT.Copy).then_inc(act.sem, act.step("out", j))

            with a.Fori(0, PAIRS) as i:
                act.start()
                for n in range(NS):
                    j, e = divmod(n, NE)
                    if not is_shared(n):
                        a.wait_ge(pe.sem, pe.done(i, "bc", n))
                        back, m = prev_scaled(n, 2)
                        a.wait_ge(pool.sem, pool.done(i, "sc", m * HT + HT - 1, back=back))
                        nc.scalar.activation(bcs[:, n % 2, :], ps[:, BC, :], ACT.Copy).then_inc(act.sem, act.step("bc", n))
                    for h in range(HT):
                        u = n * HT + h
                        if n > 0:
                            g_part(i, n - 1, h)
                        a.wait_ge(pe.sem, pe.done(i, "h1", u))
                        back, m = earlier(n, 2, NS)
                        if is_shared(m):
                            a.wait_ge(vec.sem, vec.done(i, "g", m * HT + h, back=back))
                        else:
                            a.wait_ge(pool.sem, pool.done(i, "sc", m * HT + h, back=back))
                        nc.scalar.activation(s[:, n % 2, h, :], ps[:, H1[u % 2], :], ACT.Silu).then_inc(act.sem, act.step("silu", u))
                    if j == 1 and e == LAG - 1:
                        out(i, 0)
                    if e == 4:
                        head.act.start()
                        head.scalar_hi(a, 2 * i + j + 1, 1 - j)
                for h in range(HT):
                    g_part(i, NS - 1, h)
                out(i, 1)

        @block.gpsimd
        def _(p):
            pool.credit(p)
            head.pool.credit(p)

            def head_pool(k, par):
                head.pool.start()
                head.pool_scale(p, k, par)
                gate_pool(p, k)

            if bias is not None:
                p.wait_ge(bias_loaded, 16)
            head_pool(0, 0)
            with p.Fori(0, PAIRS) as i:
                pool.start()
                for n in range(NS):
                    j, e = divmod(n, NE)
                    if not is_shared(n):
                        for h in range(HT):
                            u = n * HT + h
                            p.wait_ge(act.sem, act.done(i, "silu", u))
                            back, m = earlier(n, 2, NS)
                            p.wait_ge(vec.sem, vec.done(i, "g", m * HT + h, back=back))
                            nc.gpsimd.tensor_tensor(sc[:, n % 2, h, :], s[:, n % 2, h, :], bcs[:, n % 2, :],
                                                    ALU.mult).then_inc(pool.sem, pool.step("sc", u))
                    if e == 1 and add_to is not None:
                        at = cut((2 * i + j) * T, T)
                        nc.gpsimd.tensor_tensor(add_to[:, at], add_to[:, at], src[:, at], ALU.add).then_inc(pool.sem, pool.step("added", j))
                    if e == 2:
                        head.pool.start()
                        head.pool_scale(p, 2 * i + j + 1, 1 - j)
                    if e == 7:
                        gate_pool(p, 2 * i + j + 1)

        @block.vector
        def _(d):
            vec.credit(d)
            head.vec.credit(d)
            head.low.credit(d)
            if bias is not None:
                d.wait_ge(bias_loaded, 16)
            head_vector_all(d, 0, 0, 0)

            def g_lo_part(i, n, h):
                u = n * HT + h
                d.wait_ge(act.sem, act.done(i, "g_hi", u))
                nc.vector.tensor_tensor(g_lo[:, n % RING, h, :], g[:, n % 2, h, :], g_hi[:, n % RING, h, :],
                                        ALU.subtract).then_inc(vec.sem, vec.step("g_lo", u))

            def tail(i, j):
                d.wait_ge(pe.sem, pe.done(i, "tail", j))
                if add_to is not None:
                    d.wait_ge(pool.sem, pool.done(i, "added", j))
                seq = 2 * i + j
                nc.vector.tensor_tensor(core.x[:, cut(seq * T, T)], core.x[:, cut(seq * T, T)], ps[:, TR, :],
                                        ALU.add).then_inc(vec.sem, vec.step("tail", j))

            with d.Fori(0, PAIRS) as i:
                vec.start()
                for n in range(NS):
                    j, e = divmod(n, NE)
                    for h in range(HT):
                        u = n * HT + h
                        if n > 0:
                            g_lo_part(i, n - 1, h)
                        if is_shared(n):
                            d.wait_ge(act.sem, act.done(i, "silu", u))
                        else:
                            d.wait_ge(pool.sem, pool.done(i, "sc", u))
                        d.wait_ge(pe.sem, pe.done(i, "h3", u))
                        back, m = earlier(n, 2, NS)
                        d.wait_ge(vec.sem, vec.done(i, "g_lo", m * HT + h, back=back))
                        nc.vector.tensor_tensor(g[:, n % 2, h, :], (s if is_shared(n) else sc)[:, n % 2, h, :],
                                                ps[:, H3[u % 2], :], ALU.mult).then_inc(vec.sem, vec.step("g", u))
                    if j == 1 and e == LAG:
                        tail(i, 0)
                    seq = 2 * i + 1 if j == 0 else (2 * i + 2) % NSEQ
                    if e == 1:
                        head.start()
                        head.vector_stats(d, 2 * i + j + 1, 1 - j, seq)
                    if e == 3:
                        head.vector_z(d, 2 * i + j + 1, 1 - j, seq)
                    if e == 5:
                        head.vector_lo(d, 2 * i + j + 1, 1 - j)
                    if e == 7:
                        gate_vector(d, 2 * i + j + 1, 1 - j)
                for h in range(HT):
                    g_lo_part(i, NS - 1, h)
                tail(i, 1)


def product3(nc, out, x_hi, x_lo, w_hi, w_lo):
    nc.tensor.matmul(out, x_hi, w_hi, start=True, stop=False)
    nc.tensor.matmul(out, x_lo, w_hi, start=False, stop=False)
    return nc.tensor.matmul(out, x_hi, w_lo, start=False, stop=True)


LAYERS = ['rwkv', 'attn0', 'moe0', 'alibi', 'attn0', 'moe0', 'light', 'moe1', 'diff', 'moe1']


def build(nc, dram, plan):
    with ExitStack() as ctx:
        core = Core(nc, ctx, plan, dram)
        load_block(core)
        for n, layer in enumerate(LAYERS):
            with ExitStack() as own:
                LAYER_BLOCKS[layer](core, own, f"l{n}_{layer}")
            clear_semaphores(nc)
        store_block(core)
        clear_semaphores(nc)


def moe1_layer(core, ctx, name):
    hi, lo = split_weights(core, ctx, name + "w", None, MOE1.cols)
    weights_block(core, name + "w", "moe1_w", hi, lo)
    moe_block(core, name, MOE1, hi, lo, "ln", core.x, None, None)


def moe0_layer(core, ctx, name):
    hi, lo = split_weights(core, ctx, name + "w", None, MOE0.cols)
    weights_block(core, name + "w", "moe0_w", hi, lo, [(0, MOE0.w2, core.dram["L0_ffn_g2"].unsqueeze(1))])
    moe_block(core, name, MOE0, hi, lo, "rms", core.x2, core.x, core.dram["L0_ffn_expert_bias"])


LAYER_BLOCKS = {"moe1": moe1_layer, "moe0": moe0_layer, "attn0": attn0_layer, "rwkv": rwkv_layer, "alibi": alibi_layer, "light": light_layer, "diff": diff_layer}


VECTORS = ["L0_attn_a_" + n for n in ("time_decay", "time_first", "ln1_g", "ln1_b", "ln2_g", "ln2_b", "mix_k", "mix_v", "mix_r",
                                      "cmix_k", "cmix_r")]
VECTORS += ["L0_attn_b_alibi_slope"]
VECTORS += ["L0_ffn_g1", "L0_ffn_g2", "L0_ffn_expert_bias"]

VECTORS += ["L1_attn_b_" + n for n in ("bv", "bp", "lambda_q1", "lambda_k1", "lambda_q2", "lambda_k2")]


def laid_out(inputs):
    import numpy as np
    f = lambda n: np.asarray(inputs[n])
    cat = lambda *a: np.ascontiguousarray(np.concatenate([x.reshape(P, -1) for x in a], axis=1))
    out = {"x": np.ascontiguousarray(f("L0_attn_a_x"))}
    for n in VECTORS:
        out[n] = np.ascontiguousarray(f(n).reshape(-1))
    w2 = f("L1_ffn_w2").reshape(8, 2, P, P).transpose(2, 0, 1, 3)
    out["moe1_w"] = cat(f("L1_ffn_w_gate"), f("L1_ffn_w1").transpose(1, 0, 2), f("L1_ffn_w3").transpose(1, 0, 2), w2)
    both = lambda s, e: np.concatenate([f(s)[None], f(e)], axis=0).transpose(2, 0, 1)
    out["moe0_w"] = cat(f("L0_ffn_Wr").T, both("L0_ffn_sW1", "L0_ffn_eW1"), both("L0_ffn_sW3", "L0_ffn_eW3"),
                        both("L0_ffn_sW2", "L0_ffn_eW2"))
    twice = lambda n: (f("L0_attn_a_" + n),) * 2
    out["time_w"] = cat(*twice("w_tk"), *twice("w_tv"), *twice("w_tr"))
    ck = f("L0_attn_a_w_ck").reshape(P, 4, 1, P).repeat(2, axis=2)
    out["channel_w"] = cat(ck, *twice("w_cr"), f("L0_attn_a_w_cv").reshape(4, P, P).transpose(1, 0, 2))
    wq = f("L0_ffn_Wq").T.reshape(P, A0_HEADS, 1, DK).repeat(3, axis=2)
    wk = f("L0_ffn_Wkc").T.reshape(P, 1, DK).repeat(3, axis=1)
    out["attn0_w"] = cat(wq, wk, f("L0_ffn_Wvc").T, f("L0_ffn_Wo").T)
    out["alibi_w"] = cat(f("L0_attn_b_W_qk"), f("L0_attn_b_W_v").T)
    lwq = f("L1_attn_a_Wq").T.reshape(P, 2, 2, 4, HD).transpose(0, 1, 3, 2, 4)
    lwk = f("L1_attn_a_Wk").T.reshape(P, 4, HD)
    swapped = (np.arange(HD) + HD // 2) % HD
    lwo = f("L1_attn_a_Wo").T.reshape(2, 2, 4, HD, P).transpose(1, 3, 0, 2, 4)
    out["light_w"] = cat(lwq, lwq[..., swapped], lwk, lwk[..., swapped], f("L1_attn_a_Wv").T, lwo)
    thrice = lambda n: f(n).T.reshape(P, D_GROUPS, 1, 32).repeat(3, axis=2)
    out["diff_w"] = cat(thrice("L1_attn_b_Wq"), thrice("L1_attn_b_Wk"), f("L1_attn_b_Wv").T, f("L1_attn_b_Wp").T)
    rows3 = lambda n: np.ascontiguousarray(np.tile(f(n).reshape(D_GROUPS, 32).T, (3, 1)))
    out["diff_bq"], out["diff_bk"] = rows3("L1_attn_b_bq"), rows3("L1_attn_b_bk")
    row, hh = np.arange(P)[:, None], np.arange(PER_GROUP)
    out["diff_head_rows"] = np.where(row < D_ROWS, row % 32 // DH == hh, row - D_ROWS == hh).astype(np.float32)
    slopes = np.array([2.0 ** (-8.0 / 16 * (h + 1)) for h in range(16)], dtype=np.float32)
    inv = 1.0 / 10000.0 ** (np.arange(0, HD, 2, dtype=np.float64) / HD)
    angle = np.outer(np.concatenate([inv, inv, inv, inv]), np.arange(T, dtype=np.float64))
    sign = np.where(np.arange(P) % HD < HD // 2, -1.0, 1.0)[:, None]
    out["rope_cos"] = np.cos(angle).astype(np.float32)
    out["rope_sin"] = (sign * np.sin(angle)).astype(np.float32)
    t = np.arange(P, dtype=np.float32)
    past = (t[None, :] - t[:, None])[:, None, :]
    out["light_mask"] = np.where(past >= 0, np.exp(-slopes[:, None] * np.maximum(past, 0)), np.float32(0)).astype(np.float32).reshape(P, 4, 4 * P)
    per_row = slopes.reshape(2, 2, 4).transpose(1, 0, 2).reshape(2, 1, 8).repeat(HD, axis=1).reshape(P, 8)
    out["light_q_dec"] = np.exp(-per_row[:, :, None] * (t + 1)).astype(np.float32).reshape(P, 8, 1, P)
    out["light_k_dec"] = np.exp(-slopes[None, :] * (P - 1 - t)[:, None]).astype(np.float32)
    out["light_blk_dec"] = np.exp(-per_row * P).astype(np.float32)
    key, query = np.arange(T, dtype=np.float32), np.arange(P, dtype=np.float32)[:, None]
    out["distance"] = np.concatenate([key - (query + P * q) for q in range(NQ)], axis=1)
    out["causal"] = np.where(key[:P] <= query, np.float32(0), np.float32(-3e38))
    out["ident"] = np.eye(P, dtype=np.float32)
    out["iota"] = np.ascontiguousarray(np.broadcast_to(np.arange(8, dtype=np.float32), (P, 8)))
    return out


def kernel(**inputs):
    import concourse.bacc as bacc
    from concourse.bass_utils import run_bass_kernel_spmd

    arrays = laid_out(inputs)
    plan = {}
    for final in (False, True):
        nc = bacc.Bacc("TRN2", target_bir_lowering=False, num_devices=1)
        dram = {n: nc.dram_tensor("in_" + n, a.shape, mybir.dt.from_np(a.dtype), kind="ExternalInput").ap()
                for n, a in arrays.items()}
        dram["out"] = nc.dram_tensor("out", (NSEQ, T, P), F32, kind="ExternalOutput").ap()
        build(nc, dram, plan)
    r = run_bass_kernel_spmd(nc, [{"in_" + n: a for n, a in arrays.items()}], core_ids=[0])
    return r.results[0]["out"]
```

```python
from contextlib import ExitStack
import math
import concourse.bass as bass
from concourse import mybir

F32 = mybir.dt.float32
F32R = mybir.dt.float32r
BF16 = mybir.dt.bfloat16
U32 = mybir.dt.uint32
ALU = mybir.AluOpType
ACT = mybir.ActivationFunctionType
AXX = mybir.AxisListType.X

P = 128
NSEQ = 8
T = 512
NQ = T // P
PAIRS = NSEQ // 2
LN_EPS = 1e-5
RMS_EPS = 1e-6
LOG2E = math.log2(math.e)


IN_USE = []


def core_semaphore(nc, name):
    handle = nc.alloc_semaphore(name=name)
    IN_USE.append(handle)
    return handle


def clear_semaphores(nc):
    nc.clear_and_free_semaphores(IN_USE)
    IN_USE.clear()
    nc.all_engine_barrier()


class Steps:

    def __init__(self, nc, ctx, plan, name):
        self.sem = core_semaphore(nc, name)
        self.known = plan.setdefault(name, {})
        self.at = 0

    def start(self):
        self.at = 0

    def step(self, *name):
        place = self.known.setdefault(name, self.at)
        assert place == self.at, (name, place, self.at)
        self.at += 1
        return 1

    def per(self):
        return max(len(self.known), 1)

    def done(self, rep, *name, back=0):
        if name not in self.known:
            return 1
        return (rep + (1 - back)) * self.per() + (self.known[name] + 1)

    def credit(self, engine):
        engine.sem_inc(self.sem, self.per())


def cut(start, size):
    return bass.ds(start, size)


class Core:

    def __init__(self, nc, ctx, plan, dram):
        self.nc, self.plan, self.dram = nc, plan, dram
        self.x = ctx.enter_context(nc.sbuf_tensor("x", [P, NSEQ * T], F32))
        self.x2 = ctx.enter_context(nc.sbuf_tensor("x2", [P, NSEQ * T], F32))
        self.ident = ctx.enter_context(nc.sbuf_tensor("ident", [P, P], F32))
        self.iota = ctx.enter_context(nc.sbuf_tensor("iota", [P, 8], F32))
        self.powers = ctx.enter_context(nc.sbuf_tensor("powers", [P, 2 * 32 + NQ], F32))
        self.psum = ctx.enter_context(nc.psum_tensor("psum", [P, 8, 512], F32))
        self.settled = ctx.enter_context(nc.sbuf_tensor("settled", [P, 2], F32))
        self.eps = self.powers[:, 64:64 + NQ]
        self.half = self.powers[:, 0:NQ]
        self.two = self.powers[:, 32:64]


class Load:

    def __init__(self, core):
        nc = core.nc
        self.core = core
        self.x_loaded = [core_semaphore(nc, f"x_loaded{b}") for b in range(2)]
        self.rest_loaded = core_semaphore(nc, "x_rest_loaded")
        self.constants_loaded = core_semaphore(nc, "constants_loaded")
        self.powers_made = core_semaphore(nc, "powers_made")

    def sync_first(self, sp):
        core, d = self.core, self.core.dram
        for b in range(2):
            self.sequence(sp, b, self.x_loaded[b])
        sp.dma_start(core.ident[:, :], d["ident"]).then_inc(self.constants_loaded, 16)

    def sync_rest(self, sp):
        sp.dma_start(self.core.iota[:, :], self.core.dram["iota"]).then_inc(self.constants_loaded, 16)
        for b in range(2, NSEQ):
            self.sequence(sp, b, self.rest_loaded)
        sp.wait_ge(self.rest_loaded, 16 * (NSEQ - 2))
        sp.wait_ge(self.constants_loaded, 32)

    def sequence(self, sp, b, loaded):
        sp.dma_start(self.core.x[:, b * T:(b + 1) * T].rearrange("p (q d) -> p q d", d=P),
                     self.core.dram["x"][b, :, :].rearrange("(q p) d -> p q d", p=P)).then_inc(loaded, 16)

    def gpsimd_part(self, pool):
        pool.memset(self.core.powers[:, 0:32], -0.5).then_inc(self.powers_made, 1)
        pool.memset(self.core.powers[:, 32:64], 2.0).then_inc(self.powers_made, 1)
        pool.memset(self.core.powers[:, 64:64 + NQ], LN_EPS).then_inc(self.powers_made, 1)
        pool.wait_ge(self.powers_made, 3)


def settle(core, engine):
    if engine.engine == core.nc.gpsimd.engine:
        core.nc.gpsimd.tensor_tensor(core.settled[:, 0:1], core.half[:, 0:1], core.half[:, 0:1], ALU.add)
    else:
        core.nc.vector.memset(core.settled[:, 1:2], 0.0)


class Head:

    def __init__(self, core, ctx, name, kind, src, bank, affine=None):
        nc, plan = core.nc, core.plan
        self.core, self.kind, self.src, self.bank = core, kind, src, bank
        self.affine = affine
        self.vec = Steps(nc, ctx, plan, name + "_head_vector")
        self.pool = Steps(nc, ctx, plan, name + "_head_pool")
        self.pe = Steps(nc, ctx, plan, name + "_head_tensor")
        self.act = Steps(nc, ctx, plan, name + "_head_scalar")
        self.low = Steps(nc, ctx, plan, name + "_head_low")
        self.kept = Steps(nc, ctx, plan, name + "_head_kept")
        sb = lambda n, s, t=F32: ctx.enter_context(nc.sbuf_tensor(name + n, s, t))
        self.stats = sb("stats", [P, NQ, 6])
        self.mv = sb("mv", [P, 2, NQ, 2])
        self.var = sb("var", [P, NQ])
        self.rstd = sb("rstd", [P, NQ])
        self.var2 = sb("var2", [P, NQ])
        self.scale = sb("scale", [P, NQ])
        self.z = sb("z", [P, NQ, P])
        self.pad = 1 if affine else 0
        self.hi = sb("hi", [P, 2, self.pad + T], F32R)
        self.lo = sb("lo", [P, 2, self.pad + T], F32R)
        self.full = sb("full", [P, T]) if affine else None
        self.keep = sb("keep", [P, 2, T]) if kind in ("ln2", "lnr") else None

    def start(self):
        for s in (self.vec, self.pool, self.pe, self.act, self.kept, self.low):
            s.start()


    def vector_stats(self, dve, k, par, seq):
        nc, v = self.core.nc, self.vec
        if self.keep is not None and not (isinstance(k, int) and k == 0):
            dve.wait_ge(self.kept.sem, self.kept.done(k - 1, "keep", back=1))
        dve.wait_ge(self.pool.sem, self.pool.done(k, "scale", back=1))
        for q in range(NQ):
            nc.vector.bn_stats(self.stats[:, q, :], self.src[:, cut(seq * T + q * P, P)]).then_inc(v.sem, v.step("stats", q))
        dve.wait_ge(v.sem, v.done(k, "stats", NQ - 1))
        settle(self.core, dve)
        for q in range(NQ):
            nc.vector.bn_aggr(self.mv[:, par, q, :], self.stats[:, q, :]).then_inc(v.sem, v.step("mv", q))

    def pool_scale(self, pool, k, par):
        nc, g, v = self.core.nc, self.pool, self.vec
        pool.wait_ge(v.sem, v.done(k, "mv", NQ - 1))
        settle(self.core, pool)
        var, mean = self.mv[:, par, :, 1], self.mv[:, par, :, 0]
        if self.kind == "rms":
            nc.gpsimd.tensor_tensor(self.var[:, :], mean, mean, ALU.mult).then_inc(g.sem, g.step("sq"))
            pool.wait_ge(g.sem, g.done(k, "sq"))
            nc.gpsimd.tensor_tensor(self.rstd[:, :], self.var[:, :], var, ALU.add).then_inc(g.sem, g.step("ms"))
            pool.wait_ge(g.sem, g.done(k, "ms"))
            settle(self.core, pool)
            nc.gpsimd.tensor_scalar(self.var2[:, :], self.rstd[:, :], RMS_EPS, None, ALU.add).then_inc(g.sem, g.step("var2"))
        elif self.kind == "ln":
            nc.gpsimd.tensor_scalar(self.var2[:, :], var, LN_EPS, None, ALU.add).then_inc(g.sem, g.step("var2"))
        else:
            e2 = LN_EPS if self.kind == "ln2" else RMS_EPS
            nc.gpsimd.tensor_scalar(self.var2[:, :], var, 1.0 + e2, LN_EPS * e2, ALU.mult, ALU.add).then_inc(g.sem, g.step("var2"))
        pool.wait_ge(g.sem, g.done(k, "var2"))
        nc.gpsimd.tensor_tensor(self.scale[:, :], self.var2[:, :], self.core.half, ALU.pow).then_inc(g.sem, g.step("scale"))

    def pool_keep(self, pool, k, par, seq):
        nc, g, v = self.core.nc, self.kept, self.vec
        mean = self.mv[:, par, :, 0]
        nc.gpsimd.tensor_tensor(self.var[:, :], self.mv[:, par, :, 1], self.core.eps, ALU.add).then_inc(g.sem, g.step("var"))
        pool.wait_ge(g.sem, g.done(k, "var"))
        nc.gpsimd.tensor_tensor(self.rstd[:, :], self.var[:, :], self.core.half, ALU.pow).then_inc(g.sem, g.step("rstd"))
        pool.wait_ge(g.sem, g.done(k, "rstd"))
        wide = lambda m: m.unsqueeze(2).to_broadcast([P, NQ, P])
        kept = self.keep[:, par, :].rearrange("p (q d) -> p q d", d=P)
        tokens = self.src[:, cut(seq * T, T)].rearrange("p (q d) -> p q d", d=P)
        nc.gpsimd.tensor_tensor(kept, tokens, wide(mean), ALU.subtract).then_inc(g.sem, g.step("centred"))
        pool.wait_ge(g.sem, g.done(k, "centred"))
        nc.gpsimd.tensor_tensor(kept, kept, wide(self.rstd[:, :]), ALU.mult).then_inc(g.sem, g.step("keep"))

    def vector_z(self, dve, k, par, seq):
        nc, v = self.core.nc, self.vec
        dve.wait_ge(self.pool.sem, self.pool.done(k, "scale"))
        dve.wait_ge(self.pe.sem, self.pe.done(k, "tr", back=1))
        for q in range(NQ):
            src = self.src[:, cut(seq * T + q * P, P)]
            if self.kind == "rms":
                ins = nc.vector.tensor_scalar(self.z[:, q, :], src, self.scale[:, q:q + 1], None, ALU.mult)
            else:
                ins = nc.vector.tensor_scalar(self.z[:, q, :], src, self.mv[:, par, q, 0:1], self.scale[:, q:q + 1],
                                              ALU.subtract, ALU.mult)
            ins.then_inc(v.sem, v.step(*(("z",) if q == NQ - 1 else ("z", q))))

    def tensor_tr(self, pe, k):
        nc = self.core.nc
        pe.wait_ge(self.vec.sem, self.vec.done(k, "z"))
        pe.wait_ge(self.low.sem, self.low.done(k, "lo", back=1))
        pe.wait_ge(self.act.sem, self.act.done(k, "hi", back=1))
        for q in range(NQ):
            ins = nc.tensor.transpose(self.core.psum[:, self.bank, q * P:(q + 1) * P], self.z[:, q, :], self.core.ident[:, :])
        ins.then_inc(self.pe.sem, self.pe.step("tr"))

    def scalar_hi(self, act, k, par):
        nc = self.core.nc
        act.wait_ge(self.pe.sem, self.pe.done(k, "tr"))
        bank, to = self.core.psum[:, self.bank, :], self.hi[:, par, self.pad:self.pad + T]
        if self.affine:
            act.wait_ge(self.low.sem, self.low.done(k, "lo", back=1))
            gain, bias = self.affine
            nc.scalar.activation(self.full[:, :], bank, ACT.Identity, bias=bias, scale=gain).then_inc(self.act.sem, self.act.step("full"))
            act.wait_ge(self.act.sem, self.act.done(k, "full"))
            bank = self.full[:, :]
        nc.scalar.activation(to, bank, ACT.Copy).then_inc(self.act.sem, self.act.step("hi"))

    def vector_lo(self, dve, k, par):
        nc = self.core.nc
        dve.wait_ge(self.act.sem, self.act.done(k, "hi"))
        part = slice(self.pad, self.pad + T)
        whole = self.full[:, :] if self.affine else self.core.psum[:, self.bank, :]
        nc.vector.tensor_tensor(self.lo[:, par, part], whole, self.hi[:, par, part],
                                ALU.subtract).then_inc(self.low.sem, self.low.step("lo"))


class Weights:

    CHUNK = 1024

    def __init__(self, core, ctx, name, source, cols, scales=(), raw=None):
        nc = core.nc
        self.core, self.source, self.cols, self.scales = core, source, cols, scales
        self.hi = ctx.enter_context(nc.sbuf_tensor(name + "_hi", [P, cols], F32R))
        self.lo = ctx.enter_context(nc.sbuf_tensor(name + "_lo", [P, cols], F32R))
        self.raw = raw if raw is not None else ctx.enter_context(nc.sbuf_tensor(name + "_raw", [P, cols], F32))
        self.gain = ctx.enter_context(nc.sbuf_tensor(name + "_gain", [P, max(len(scales), 1)], F32))
        self.chunks = (cols + self.CHUNK - 1) // self.CHUNK
        self.loaded = [core_semaphore(nc, f"{name}_loaded{c}") for c in range(self.chunks)]
        self.gains, self.turned = core_semaphore(nc, name + "_gains"), core_semaphore(nc, name + "_one_minus")
        self.rounded, self.split = core_semaphore(nc, name + "_rounded"), core_semaphore(nc, name + "_split")
        self.one_minus = [n for n, s in enumerate(scales) if len(s) > 3]
        edges = {c * self.CHUNK for c in range(self.chunks)} | {cols} | {e for s in scales for e in s[:2]}
        edges = sorted(edges)
        self.pieces = [(a // self.CHUNK, a, b, next((n for n, s in enumerate(scales) if s[0] <= a < s[1]), None))
                       for a, b in zip(edges, edges[1:])]

    def sync_part(self, sp):
        for n, (_, _, vector, *_) in enumerate(self.scales):
            sp.dma_start(self.gain[:, n:n + 1], vector).then_inc(self.gains, 16)
        for c in range(self.chunks):
            span = slice(c * self.CHUNK, min((c + 1) * self.CHUNK, self.cols))
            sp.dma_start(self.raw[:, span], self.core.dram[self.source][:, span]).then_inc(self.loaded[c], 16)

    def gpsimd_part(self, pool):
        if self.one_minus:
            pool.wait_ge(self.gains, 16 * len(self.scales))
            for n in self.one_minus:
                self.core.nc.gpsimd.tensor_scalar(self.gain[:, n:n + 1], self.gain[:, n:n + 1], -1.0, 1.0, ALU.mult, ALU.add
                                                  ).then_inc(self.turned, 1)

    def gains_ready(self, engine):
        if self.scales:
            engine.wait_ge(self.gains, 16 * len(self.scales))
        if self.one_minus:
            engine.wait_ge(self.turned, len(self.one_minus))

    def scalar_part(self, act):
        nc = self.core.nc
        self.gains_ready(act)
        for c, a, b, n in self.pieces:
            act.wait_ge(self.loaded[c], 16)
            if n is None:
                ins = nc.scalar.activation(self.hi[:, a:b], self.raw[:, a:b], ACT.Copy)
            else:
                ins = nc.scalar.activation(self.hi[:, a:b], self.raw[:, a:b], ACT.Identity, scale=self.gain[:, n:n + 1])
            ins.then_inc(self.rounded, 1)

    def vector_part(self, dve, only=None):
        nc = self.core.nc
        self.gains_ready(dve)
        for m, (c, a, b, n) in list(enumerate(self.pieces))[only or slice(None)]:
            dve.wait_ge(self.loaded[c], 16)
            dve.wait_ge(self.rounded, m + 1)
            if n is None:
                ins = nc.vector.tensor_tensor(self.lo[:, a:b], self.raw[:, a:b], self.hi[:, a:b], ALU.subtract)
            else:
                ins = nc.vector.scalar_tensor_tensor(self.lo[:, a:b], self.raw[:, a:b], self.gain[:, n:n + 1], self.hi[:, a:b],
                                                     ALU.mult, ALU.subtract)
            ins.then_inc(self.split, 1)

    def tensor_part(self, t, first=None):
        t.wait_ge(self.split, first or len(self.pieces))


def product(nc, out, w_hi, w_lo, x_hi, x_lo, start=True, stop=True):
    nc.tensor.matmul(out, w_hi, x_hi, start=start, stop=False)
    nc.tensor.matmul(out, w_lo, x_hi, start=False, stop=False)
    return nc.tensor.matmul(out, w_hi, x_lo, start=False, stop=stop)


AL_QK, AL_V = 0, P
AL_COLS = 2 * P


def alibi_block(core, name, weights_in):
    nc, plan, ps, d_ = core.nc, core.plan, core.psum, core.dram
    w_hi, w_lo = weights_in.hi, weights_in.lo
    TR, Y, VB, S, W, O = 0, 1, 2, (3, 4), 5, (6, 7)
    SCALE = P ** -0.5
    U = 2 * NQ
    with ExitStack() as ctx:
        sb = lambda n, s, t=F32: ctx.enter_context(nc.sbuf_tensor(name + n, s, t))
        head = Head(core, ctx, name, "ln", core.x, TR)
        vec, act = Steps(nc, ctx, plan, name + "_vector"), Steps(nc, ctx, plan, name + "_scalar")
        pe = Steps(nc, ctx, plan, name + "_tensor")
        loaded = core_semaphore(nc, name + "_tables_loaded")
        made = core_semaphore(nc, name + "_bias_made")
        slope = sb("slope", [P, 1])
        bias = sb("bias", [P, NQ, T])
        y_hi, y_lo = sb("y_hi", [P, 2, T], F32R), sb("y_lo", [P, 2, T], F32R)
        V = sb("V", [P, 2, NQ, P])
        sc = sb("sc", [P, 2, T])
        neg_max, sums, rec = sb("neg_max", [P, U]), sb("sums", [P, U]), sb("rec", [P, U])
        w, wT = sb("w", [P, 2, T]), sb("wT", [P, 2, T])
        block = ctx.enter_context(nc.Block())
        keys = lambda u: (u % NQ + 1) * P

        @block.sync
        def _(sp):
            weights_in.sync_part(sp)
            sp.dma_start(slope[:, :], d_["L0_attn_b_alibi_slope"].unsqueeze(0).to_broadcast([P, 1])).then_inc(loaded, 16)
            sp.dma_start(bias[:, :, :], d_["distance"].rearrange("p (q t) -> p q t", t=T)).then_inc(loaded, 16)
            sp.dma_start(sc[:, 0, 0:P], d_["causal"]).then_inc(loaded, 16)

        @block.tensor
        def _(t):
            pe.credit(t)
            head.pe.credit(t)
            head.start()
            head.tensor_tr(t, 0)
            weights_in.tensor_part(t)

            def project(i, j):
                hi, lo = head.hi[:, j, :], head.lo[:, j, :]
                t.wait_ge(head.low.sem, head.low.done(2 * i + j, "lo"))
                back, m = earlier(j, 1, 2)
                t.wait_ge(vec.sem, vec.done(i, "y_lo", m, back=back))
                product(nc, ps[:, Y, :], w_hi[:, AL_QK:AL_QK + P], w_lo[:, AL_QK:AL_QK + P], hi, lo).then_inc(pe.sem, pe.step("y", j))
                t.wait_ge(act.sem, act.done(i, "V", m, back=back))
                for q in range(NQ):
                    c = slice(q * P, (q + 1) * P)
                    ins = product3(nc, ps[:, VB, c], head.hi[:, j, c], head.lo[:, j, c], w_hi[:, AL_V:AL_V + P], w_lo[:, AL_V:AL_V + P])
                ins.then_inc(pe.sem, pe.step("V", j))

            def scores(i, u):
                j, q = divmod(u, NQ)
                c, n = slice(q * P, (q + 1) * P), keys(u)
                t.wait_ge(vec.sem, vec.done(i, "y_lo", j))
                back, m = earlier(u, 2, U)
                t.wait_ge(vec.sem, vec.done(i, "sc", m, back=back))
                out = ps[:, S[u % 2], 0:n]
                nc.tensor.matmul(out, y_hi[:, j, c], head.hi[:, j, 0:n], start=True, stop=False)
                nc.tensor.matmul(out, y_lo[:, j, c], head.hi[:, j, 0:n], start=False, stop=False)
                nc.tensor.matmul(out, y_hi[:, j, c], head.lo[:, j, 0:n], start=False, stop=True).then_inc(pe.sem, pe.step("s", u))

            def turn(i, u):
                t.wait_ge(act.sem, act.done(i, "w", u))
                back, m = earlier(u, 1, U)
                t.wait_ge(act.sem, act.done(i, "wT", m, back=back))
                for k in range(u % NQ + 1):
                    ins = nc.tensor.transpose(ps[:, W, k * P:(k + 1) * P], w[:, u % 2, k * P:(k + 1) * P], core.ident[:, :])
                ins.then_inc(pe.sem, pe.step("turned", u))

            def attend(i, u):
                j, q = divmod(u, NQ)
                t.wait_ge(act.sem, act.done(i, "V", j))
                t.wait_ge(act.sem, act.done(i, "wT", u))
                if q == 0:
                    t.wait_ge(vec.sem, vec.done(i, "tail", j, back=1))
                for k in range(q + 1):
                    ins = nc.tensor.matmul(ps[:, O[j], q * P:(q + 1) * P], wT[:, u % 2, k * P:(k + 1) * P], V[:, j, k, :],
                                           start=(k == 0), stop=(k == q))
                ins.then_inc(pe.sem, pe.step("o", u))

            with t.Fori(0, PAIRS) as i:
                pe.start()
                project(i, 0)
                for n in range(U + 3):
                    if n < U:
                        scores(i, n)
                    if n == 1:
                        head.start()
                        head.tensor_tr(t, 2 * i + 1)
                    if n == 3:
                        project(i, 1)
                    if n == 7:
                        head.start()
                        head.tensor_tr(t, 2 * i + 2)
                    if 2 <= n < U + 2:
                        turn(i, n - 2)
                    if n >= 3:
                        attend(i, n - 3)

        @block.scalar
        def _(a):
            act.credit(a)
            head.act.credit(a)
            head.start()
            head.scalar_hi(a, 0, 0)
            weights_in.scalar_part(a)

            def projected(i, j):
                a.wait_ge(pe.sem, pe.done(i, "o", j * NQ + NQ - 1, back=1))
                a.wait_ge(pe.sem, pe.done(i, "y", j))
                nc.scalar.activation(y_hi[:, j, :], ps[:, Y, :], ACT.Copy).then_inc(act.sem, act.step("y_hi", j))
                a.wait_ge(pe.sem, pe.done(i, "V", j))
                nc.scalar.activation(V[:, j, :, :], ps[:, VB, :].rearrange("p (q d) -> p q d", d=P), ACT.Copy).then_inc(act.sem, act.step("V", j))

            with a.Fori(0, PAIRS) as i:
                act.start()
                projected(i, 0)
                for n in range(U + 1):
                    if n < U:
                        a.wait_ge(vec.sem, vec.done(i, "max", n))
                        back, m = earlier(n, 2, U)
                        a.wait_ge(pe.sem, pe.done(i, "turned", m, back=back))
                        a.wait_ge(vec.sem, vec.done(i, "rec", n // NQ, back=1))
                        nc.scalar.activation(w[:, n % 2, 0:keys(n)], sc[:, n % 2, 0:keys(n)], ACT.Exp, bias=neg_max[:, n:n + 1],
                                             accum_out=sums[:, n:n + 1]).then_inc(act.sem, act.step("w", n))
                    if n == 1:
                        head.start()
                        head.scalar_hi(a, 2 * i + 1, 1)
                    if n == 2:
                        projected(i, 1)
                    if n >= 1:
                        u = n - 1
                        back, m = earlier(u, 2, U)
                        a.wait_ge(pe.sem, pe.done(i, "o", m, back=back))
                        a.wait_ge(pe.sem, pe.done(i, "turned", u))
                        nc.scalar.activation(wT[:, u % 2, 0:keys(u)], ps[:, W, 0:keys(u)], ACT.Copy).then_inc(act.sem, act.step("wT", u))
                head.start()
                head.scalar_hi(a, 2 * i + 2, 0)

        @block.vector
        def _(d):
            vec.credit(d)
            head.vec.credit(d)
            head.low.credit(d)

            def before(k, par, seq):
                head.start()
                head.vector_stats(d, k, par, seq)
                head.vector_z(d, k, par, seq)

            before(0, 0, 0)
            head.vector_lo(d, 0, 0)
            weights_in.vector_part(d)
            d.wait_ge(made, 1 + NQ)

            def projected(i, j):
                d.wait_ge(act.sem, act.done(i, "y_hi", j))
                nc.vector.tensor_tensor(y_lo[:, j, :], ps[:, Y, :], y_hi[:, j, :], ALU.subtract).then_inc(vec.sem, vec.step("y_lo", j))

            def tail(i, j):
                d.wait_ge(act.sem, act.done(i, "w", j * NQ + NQ - 1))
                us = slice(j * NQ, (j + 1) * NQ)
                d.wait_ge(vec.sem, vec.done(i, "tail", j, back=1))
                nc.vector.reciprocal(rec[:, us], sums[:, us]).then_inc(vec.sem, vec.step("rec", j))
                d.wait_ge(vec.sem, vec.done(i, "rec", j))
                d.wait_ge(pe.sem, pe.done(i, "o", j * NQ + NQ - 1))
                for q in range(NQ):
                    at = cut((2 * i + j) * T + q * P, P)
                    ins = nc.vector.scalar_tensor_tensor(core.x[:, at], ps[:, O[j], q * P:(q + 1) * P], rec[:, j * NQ + q:j * NQ + q + 1],
                                                         core.x[:, at], ALU.mult, ALU.add)
                ins.then_inc(vec.sem, vec.step("tail", j))

            with d.Fori(0, PAIRS) as i:
                vec.start()
                projected(i, 0)
                for n in range(U):
                    d.wait_ge(pe.sem, pe.done(i, "s", n))
                    back, m = earlier(n, 2, U)
                    d.wait_ge(act.sem, act.done(i, "w", m, back=back))
                    nc.vector.scalar_tensor_tensor(sc[:, n % 2, 0:keys(n)], ps[:, S[n % 2], 0:keys(n)], SCALE, bias[:, n % NQ, 0:keys(n)],
                                                   ALU.mult, ALU.add).then_inc(vec.sem, vec.step("sc", n))
                    d.wait_ge(vec.sem, vec.done(i, "sc", n))
                    nc.vector.tensor_reduce(neg_max[:, n:n + 1], sc[:, n % 2, 0:keys(n)], AXX, ALU.max,
                                            negate=True).then_inc(vec.sem, vec.step("max", n))
                    if n == 0:
                        before(2 * i + 1, 1, 2 * i + 1)
                    if n == 1:
                        head.vector_lo(d, 2 * i + 1, 1)
                    if n == 2:
                        projected(i, 1)
                    if n == 6:
                        before(2 * i + 2, 0, (2 * i + 2) % NSEQ)
                    if n == 7:
                        tail(i, 0)
                head.vector_lo(d, 2 * i + 2, 0)
                tail(i, 1)

        @block.gpsimd
        def _(p):
            head.pool.credit(p)
            head.start()
            head.pool_scale(p, 0, 0)
            p.wait_ge(loaded, 16 * 3)
            nc.gpsimd.tensor_scalar(bias[:, :, :], bias[:, :, :], slope[:, 0:1], None, ALU.mult).then_inc(made, 1)
            p.wait_ge(made, 1)
            for q in range(NQ):
                c = slice(q * P, (q + 1) * P)
                nc.gpsimd.tensor_tensor(bias[:, q, c], bias[:, q, c], sc[:, 0, 0:P], ALU.add).then_inc(made, 1)
            with p.Fori(0, PAIRS) as i:
                head.start()
                head.pool_scale(p, 2 * i + 1, 1)
                head.start()
                head.pool_scale(p, 2 * i + 2, 0)


def alibi_layer(core, ctx, name):
    alibi_block(core, name, Weights(core, ctx, name + "w", "alibi_w", AL_COLS))


DK = 32
A0_HEADS = 4
A0_Q, A0_K = 0, A0_HEADS * 3 * DK
A0_V = A0_K + 3 * DK
A0_O = A0_V + DK
A0_COLS = A0_O + P


def attn0_block(core, name, weights_in):
    nc, plan, ps = core.nc, core.plan, core.psum
    w_hi, w_lo = weights_in.hi, weights_in.lo
    O, R, S = 0, (1, 2, 3), (4, 6)
    ROWS = 3 * DK
    SCALE = DK ** -0.5
    PER_SEQ = A0_HEADS // 2
    UNITS = 2 * PER_SEQ
    BLOCKS = 2 * NQ
    with ExitStack() as ctx:
        sb = lambda n, s, t=F32: ctx.enter_context(nc.sbuf_tensor(name + n, s, t))
        head = Head(core, ctx, name, "lnr", core.x, R[0])
        steps = lambda n: Steps(nc, ctx, plan, name + n)
        pe_proj, act_proj, vec_proj = (steps("_proj_" + e) for e in ("tensor", "scalar", "vector"))
        pe_val, act_val, vec_val = (steps("_keys_" + e) for e in ("tensor", "scalar", "vector"))
        pe_max, act_max, vec_max = (steps("_max_" + e) for e in ("tensor", "scalar", "vector"))
        pe_att, act_att = (steps("_att_" + e) for e in ("tensor", "scalar"))
        pe_out, act_out, vec_out = (steps("_out_" + e) for e in ("tensor", "scalar", "vector"))
        pe_end, act_end, vec_end = (steps("_end_" + e) for e in ("tensor", "scalar", "vector"))
        ready = core_semaphore(nc, name + "_fixed_ready")
        Q = sb("Q", [P, 4, 2, T], F32R)
        K = sb("K", [P, 2, T], F32R)
        V = sb("V", [P, 2, NQ, DK])
        ones = sb("ones", [P, DK])
        neg_max = sb("neg_max", [P, NQ, 2, ROWS + 1])
        weights = sb("weights", [P, NQ, 2, T])
        o_sb = sb("o_sb", [P, T])
        rec = sb("rec", [P, NQ, 2])
        att, att_hi, att_lo = sb("att", [P, NQ, P]), sb("att_hi", [P, T], F32R), sb("att_lo", [P, T], F32R)
        block = ctx.enter_context(nc.Block())

        proj = lambda n: ([("k", n), ("v", n)] if n % PER_SEQ == 0 else []) + [("q", n, 0), ("q", n, 1)]
        maxes = lambda n, blocks: [("max", n, b) for b in blocks]

        def slot_users(G):
            users = maxes(G + 1, range(0, 4)) + [("o", G - 1)] * (G > 0) + proj(G + 2)
            if G == PER_SEQ:
                users += [("turned", 0)]
            last = G == UNITS - 1
            if not last:
                users += maxes(G + 1, range(4, 8))
            if G == PER_SEQ:
                users += [("end", 0)]
            rows = [("nm", G + 1, 0), ("nm", G + 1, 1)]
            if not last:
                users += rows
            if G % 2:
                users += [("head", G // 2 + 2)]
            if last:
                users += [("o", G)] + maxes(G + 1, range(4, 6)) + [("turned", 1)] + maxes(G + 1, range(6, 8)) + [("end", 1)] + rows
            return users

        users = [u for G in range(UNITS) for u in slot_users(G)]
        before_loop = proj(UNITS) + proj(UNITS + 1) + maxes(UNITS, range(BLOCKS)) + [("nm", UNITS, 0), ("nm", UNITS, 1)]
        bank_of = lambda user: R[users.index(user) % len(R)]

        unit_of = lambda i, n: n - UNITS if i is None else UNITS * i + n
        seq_of = lambda i, j: j - 2 if i is None else 2 * i + j

        def freed(i, user, back):
            what, n = user[0], user[1]
            unit = unit_of(i, n) - UNITS * back
            if what == "q":
                return vec_proj.sem, vec_proj.done(unit, "lo", user[2])
            if what == "max":
                return vec_max.sem, vec_max.done(unit, "max", user[2])
            if what == "nm":
                return act_max.sem, act_max.done(unit, "nm", user[2])
            if what == "o":
                return vec_out.sem, vec_out.done(unit, "att")
            seq = seq_of(i, n // PER_SEQ if what in ("k", "v") else n) - 2 * back
            if what == "k":
                return vec_val.sem, vec_val.done(seq, "k")
            if what == "v":
                return act_val.sem, act_val.done(seq, "v")
            if what == "turned":
                return vec_end.sem, vec_end.done(seq, "lo")
            if what == "end":
                return vec_end.sem, vec_end.done(seq, "tail")
            return head.low.sem, head.low.done(seq, "lo")

        def ring(t, i, user):
            if i is None:
                at = before_loop.index(user)
                same = [u for u in before_loop[:at] if bank_of(u) == bank_of(user)]
                if same:
                    t.wait_ge(*freed(None, same[-1], 0))
            else:
                back, m = earlier(users.index(user), len(R), len(users))
                t.wait_ge(*freed(i, users[m], back))
            return bank_of(user)

        def attended(engine, i, n):
            if i is not None:
                engine.wait_ge(pe_att.sem, pe_att.done(unit_of(i, n - 2), "pv", NQ - 1, back=1))

        @block.sync
        def _(sp):
            weights_in.sync_part(sp)

        @block.tensor
        def _(t):
            for s in (pe_proj, pe_val, pe_max, pe_att, pe_out, pe_end, head.pe):
                s.credit(t)

            def project(i, n):
                j, u = divmod(n, PER_SEQ)
                hi, lo = head.hi[:, j % 2, :], head.lo[:, j % 2, :]
                if u == 0:
                    pe_val.start()
                    t.wait_ge(head.low.sem, head.low.done(seq_of(i, j), "lo"))
                    b = ring(t, i, ("k", n))
                    product(nc, ps[0:ROWS, b, :], w_hi[:, A0_K:A0_K + ROWS], w_lo[:, A0_K:A0_K + ROWS], hi, lo
                            ).then_inc(pe_val.sem, pe_val.step("k"))
                    b = ring(t, i, ("v", n))
                    for q in range(NQ):
                        c = slice(q * P, (q + 1) * P)
                        ins = product3(nc, ps[:, b, q * DK:(q + 1) * DK], head.hi[:, j % 2, c], head.lo[:, j % 2, c],
                                       w_hi[:, A0_V:A0_V + DK], w_lo[:, A0_V:A0_V + DK])
                    ins.then_inc(pe_val.sem, pe_val.step("v"))
                pe_proj.start()
                for hh in range(2):
                    b, c = ring(t, i, ("q", n, hh)), A0_Q + (2 * u + hh) * ROWS
                    product(nc, ps[0:ROWS, b, :], w_hi[:, c:c + ROWS], w_lo[:, c:c + ROWS], hi, lo
                            ).then_inc(pe_proj.sem, pe_proj.step("q", hh))

            def scores_for_max(i, n, blocks):
                for b in blocks:
                    hh, st = divmod(b, NQ)
                    if b == 0:
                        pe_max.start()
                        t.wait_ge(vec_val.sem, vec_val.done(seq_of(i, n // PER_SEQ), "k"))
                    if st == 0:
                        t.wait_ge(vec_proj.sem, vec_proj.done(unit_of(i, n), "lo", hh))
                    bank = ring(t, i, ("max", n, b))
                    nc.tensor.matmul(ps[:, bank, :], Q[0:ROWS, n % 4, hh, st * P:(st + 1) * P], K[0:ROWS, n // PER_SEQ % 2, :],
                                     start=True, stop=True).then_inc(pe_max.sem, pe_max.step("max", b))

            def max_rows(i, n):
                for hh in range(2):
                    t.wait_ge(vec_max.sem, vec_max.done(unit_of(i, n), "max", hh * NQ + NQ - 1))
                    bank = ring(t, i, ("nm", n, hh))
                    for st in range(NQ):
                        ins = nc.tensor.transpose(ps[0:ROWS + 1, bank, st * P:(st + 1) * P], neg_max[:, st, hh, :], core.ident[:, :])
                    ins.then_inc(pe_max.sem, pe_max.step("nm", hh))

            def scores(i, n, tt):
                unit = unit_of(i, n)
                if tt == 0:
                    pe_att.start()
                    t.wait_ge(act_max.sem, act_max.done(unit, "nm", 1))
                if tt < 2:
                    t.wait_ge(act_att.sem, act_att.done(unit, "exp", 2 + tt, back=1))
                else:
                    t.wait_ge(act_att.sem, act_att.done(unit, "exp", tt - 2))
                for hh in range(2):
                    ins = nc.tensor.matmul(ps[:, S[tt % 2] + hh, :], K[0:ROWS + 1, n // PER_SEQ, tt * P:(tt + 1) * P],
                                           Q[0:ROWS + 1, n % 4, hh, :], start=True, stop=True)
                ins.then_inc(pe_att.sem, pe_att.step("scores", tt))

            def attend(i, n, tt):
                if tt == 0:
                    t.wait_ge(act_val.sem, act_val.done(seq_of(i, n // PER_SEQ), "v"))
                    t.wait_ge(act_out.sem, act_out.done(unit_of(i, n), "o", back=1))
                t.wait_ge(act_att.sem, act_att.done(unit_of(i, n), "exp", tt))
                for strip in range(4):
                    left = V[:, n // PER_SEQ, tt, :] if strip < 2 else ones[:, :]
                    ins = nc.tensor.matmul(ps[strip * 32:strip * 32 + 32, O, :], left, weights[:, tt, strip % 2, :],
                                           start=(tt == 0), stop=(tt == NQ - 1))
                ins.then_inc(pe_att.sem, pe_att.step("pv", tt))

            def turn_output(i, n):
                pe_out.start()
                t.wait_ge(act_out.sem, act_out.done(unit_of(i, n), "o"))
                bank = ring(t, i, ("o", n))
                for q in range(NQ):
                    ins = nc.tensor.transpose(ps[:, bank, q * P:(q + 1) * P], o_sb[:, q * P:(q + 1) * P], core.ident[:, :])
                ins.then_inc(pe_out.sem, pe_out.step("o"))

            def turn_heads(i, j):
                pe_end.start()
                t.wait_ge(vec_out.sem, vec_out.done(unit_of(i, j * PER_SEQ + PER_SEQ - 1), "att"))
                bank = ring(t, i, ("turned", j))
                for q in range(NQ):
                    ins = nc.tensor.transpose(ps[:, bank, q * P:(q + 1) * P], att[:, q, :], core.ident[:, :])
                ins.then_inc(pe_end.sem, pe_end.step("turned"))

            def end(i, j):
                t.wait_ge(vec_end.sem, vec_end.done(seq_of(i, j), "lo"))
                bank = ring(t, i, ("end", j))
                for q in range(NQ):
                    c = slice(q * P, (q + 1) * P)
                    ins = product3(nc, ps[:, bank, c], att_hi[:, c], att_lo[:, c], w_hi[:, A0_O:A0_O + P], w_lo[:, A0_O:A0_O + P])
                ins.then_inc(pe_end.sem, pe_end.step("end"))

            for k in range(2):
                if k == 1:
                    t.wait_ge(head.low.sem, head.low.done(0, "lo"))
                head.start()
                head.bank = R[0]
                head.tensor_tr(t, k)
            t.wait_ge(ready, 3)
            t.wait_ge(head.low.sem, head.low.done(1, "lo"))
            weights_in.tensor_part(t)
            project(None, UNITS)
            project(None, UNITS + 1)
            scores_for_max(None, UNITS, range(BLOCKS))
            max_rows(None, UNITS)
            for u in before_loop[-3:]:
                t.wait_ge(*freed(None, u, 0))
            with t.Fori(0, PAIRS) as i:
                for G in range(UNITS):
                    scores(i, G, 0)
                    scores_for_max(i, G + 1, range(0, 2))
                    scores(i, G, 1)
                    scores_for_max(i, G + 1, range(2, 4))
                    attend(i, G, 0)
                    if G > 0:
                        turn_output(i, G - 1)
                    project(i, G + 2)
                    if G == PER_SEQ:
                        turn_heads(i, 0)
                    last = G == UNITS - 1
                    scores(i, G, 2)
                    if not last:
                        scores_for_max(i, G + 1, range(4, 6))
                    attend(i, G, 1)
                    scores(i, G, 3)
                    if not last:
                        scores_for_max(i, G + 1, range(6, 8))
                    if G == PER_SEQ:
                        end(i, 0)
                    attend(i, G, 2)
                    if not last:
                        max_rows(i, G + 1)
                    if G % 2:
                        head.start()
                        head.bank = ring(t, i, ("head", G // 2 + 2))
                        head.tensor_tr(t, 2 * i + G // 2 + 2)
                    attend(i, G, 3)
                turn_output(i, UNITS - 1)
                scores_for_max(i, UNITS, range(4, 6))
                turn_heads(i, 1)
                scores_for_max(i, UNITS, range(6, 8))
                end(i, 1)
                max_rows(i, UNITS)

        @block.scalar
        def _(a):
            for s in (act_proj, act_val, act_max, act_att, act_out, act_end, head.act):
                s.credit(a)
            copy = lambda out, in_: nc.scalar.activation(out, in_, ACT.Copy)

            def projected(i, n):
                j = n // PER_SEQ
                attended(a, i, n)
                if n % PER_SEQ == 0:
                    act_val.start()
                    a.wait_ge(pe_val.sem, pe_val.done(seq_of(i, j), "k"))
                    copy(K[0:ROWS, j % 2, :], ps[0:ROWS, bank_of(("k", n)), :]).then_inc(act_val.sem, act_val.step("k"))
                    a.wait_ge(pe_val.sem, pe_val.done(seq_of(i, j), "v"))
                    copy(V[:, j % 2, :, :], ps[:, bank_of(("v", n)), 0:NQ * DK].rearrange("p (q d) -> p q d", d=DK)
                         ).then_inc(act_val.sem, act_val.step("v"))
                act_proj.start()
                for hh in range(2):
                    a.wait_ge(pe_proj.sem, pe_proj.done(unit_of(i, n), "q", hh))
                    copy(Q[0:ROWS, n % 4, hh, :], ps[0:ROWS, bank_of(("q", n, hh)), :]).then_inc(act_proj.sem, act_proj.step("hi", hh))

            def max_rows(i, n):
                act_max.start()
                for hh in range(2):
                    a.wait_ge(pe_max.sem, pe_max.done(unit_of(i, n), "nm", hh))
                    copy(Q[ROWS:ROWS + 1, n % 4, hh, :], ps[ROWS:ROWS + 1, bank_of(("nm", n, hh)), :]
                         ).then_inc(act_max.sem, act_max.step("nm", hh))

            def exps(i, n, tt):
                unit = unit_of(i, n)
                if tt == 0:
                    act_att.start()
                a.wait_ge(pe_att.sem, pe_att.done(unit, "pv", tt, back=1))
                a.wait_ge(pe_att.sem, pe_att.done(unit, "scores", tt))
                nc.scalar.activation(weights[:, tt, :, :], ps[:, S[tt % 2]:S[tt % 2] + 2, :], ACT.Exp,
                                     scale=SCALE).then_inc(act_att.sem, act_att.step("exp", tt))

            def output(i, n):
                act_out.start()
                a.wait_ge(pe_out.sem, pe_out.done(unit_of(i, n), "o", back=1))
                a.wait_ge(pe_att.sem, pe_att.done(unit_of(i, n), "pv", NQ - 1))
                copy(o_sb[:, :], ps[:, O, :]).then_inc(act_out.sem, act_out.step("o"))

            def end(i, j):
                act_end.start()
                k = seq_of(i, j)
                a.wait_ge(pe_end.sem, pe_end.done(k, "end", back=1))
                a.wait_ge(pe_end.sem, pe_end.done(k, "turned"))
                copy(att_hi[:, :], ps[:, bank_of(("turned", j)), :]).then_inc(act_end.sem, act_end.step("hi"))

            for k in range(2):
                head.start()
                head.bank = R[0]
                head.scalar_hi(a, k, k)
            weights_in.scalar_part(a)
            a.wait_ge(ready, 3)
            projected(None, UNITS)
            projected(None, UNITS + 1)
            max_rows(None, UNITS)
            with a.Fori(0, PAIRS) as i:
                for G in range(UNITS):
                    if G > 0:
                        output(i, G - 1)
                    exps(i, G, 0)
                    exps(i, G, 1)
                    projected(i, G + 2)
                    if G == PER_SEQ:
                        end(i, 0)
                    exps(i, G, 2)
                    exps(i, G, 3)
                    if G < UNITS - 1:
                        max_rows(i, G + 1)
                    if G % 2:
                        head.start()
                        head.bank = bank_of(("head", G // 2 + 2))
                        head.scalar_hi(a, 2 * i + G // 2 + 2, G // 2 % 2)
                output(i, UNITS - 1)
                end(i, 1)
                max_rows(i, UNITS)

        @block.vector
        def _(d):
            for s in (vec_proj, vec_val, vec_max, vec_out, vec_end, head.vec, head.low):
                s.credit(d)

            def head_before(k, par, seq):
                head.start()
                head.vector_stats(d, k, par, seq)
                head.vector_z(d, k, par, seq)

            def projected(i, n):
                j = n // PER_SEQ
                if n % PER_SEQ == 0:
                    vec_val.start()
                    d.wait_ge(act_val.sem, act_val.done(seq_of(i, j), "k"))
                    lo = K[32:64, j % 2, :]
                    nc.vector.tensor_tensor(lo, ps[32:64, bank_of(("k", n)), :], lo, ALU.subtract).then_inc(vec_val.sem, vec_val.step("k"))
                vec_proj.start()
                for hh in range(2):
                    d.wait_ge(act_proj.sem, act_proj.done(unit_of(i, n), "hi", hh))
                    lo = Q[64:96, n % 4, hh, :]
                    nc.vector.tensor_tensor(lo, ps[64:96, bank_of(("q", n, hh)), :], lo, ALU.subtract
                                            ).then_inc(vec_proj.sem, vec_proj.step("lo", hh))

            def maxes_of(i, n, blocks):
                for b in blocks:
                    hh, st = divmod(b, NQ)
                    if b == 0:
                        vec_max.start()
                    if st == 0:
                        d.wait_ge(pe_max.sem, pe_max.done(unit_of(i, n), "nm", hh, back=1))
                    d.wait_ge(pe_max.sem, pe_max.done(unit_of(i, n), "max", b))
                    nc.vector.tensor_reduce(neg_max[:, st, hh, ROWS:ROWS + 1], ps[:, bank_of(("max", n, b)), :], AXX, ALU.max,
                                            negate=True).then_inc(vec_max.sem, vec_max.step("max", b))

            def normalise(i, n):
                j, u = divmod(n, PER_SEQ)
                unit = unit_of(i, n)
                vec_out.start()
                turned = ps[:, bank_of(("o", n)), :].rearrange("p (t h e) -> p t h e", t=NQ, e=DK)
                d.wait_ge(vec_out.sem, vec_out.done(unit, "att", back=1))
                d.wait_ge(pe_out.sem, pe_out.done(unit, "o"))
                nc.vector.reciprocal(rec[:, :, :], turned[:, :, 2:4, 0]).then_inc(vec_out.sem, vec_out.step("rec"))
                d.wait_ge(vec_out.sem, vec_out.done(unit, "rec"))
                if u == 0:
                    d.wait_ge(pe_end.sem, pe_end.done(seq_of(i, j), "turned", back=1))
                nc.vector.tensor_tensor(att[:, :, u * 64:u * 64 + 64].rearrange("p t (h e) -> p t h e", e=DK), turned[:, :, 0:2, :],
                                        rec[:, :, :].unsqueeze(3).to_broadcast([P, NQ, 2, DK]), ALU.mult
                                        ).then_inc(vec_out.sem, vec_out.step("att"))

            def end_lo(i, j):
                vec_end.start()
                d.wait_ge(act_end.sem, act_end.done(seq_of(i, j), "hi"))
                nc.vector.tensor_tensor(att_lo[:, :], ps[:, bank_of(("turned", j)), :], att_hi[:, :], ALU.subtract
                                        ).then_inc(vec_end.sem, vec_end.step("lo"))

            def tail(i, j):
                k = seq_of(i, j)
                d.wait_ge(head.kept.sem, head.kept.done(k, "keep"))
                d.wait_ge(pe_end.sem, pe_end.done(k, "end"))
                nc.vector.tensor_tensor(core.x2[:, cut(k * T, T)], head.keep[:, j, :], ps[:, bank_of(("end", j)), :],
                                        ALU.add).then_inc(vec_end.sem, vec_end.step("tail"))

            for k in range(2):
                head_before(k, k, k)
                head.bank = R[0]
                head.vector_lo(d, k, k)
            weights_in.vector_part(d)
            d.wait_ge(ready, 3)
            projected(None, UNITS)
            projected(None, UNITS + 1)
            maxes_of(None, UNITS, range(BLOCKS))
            with d.Fori(0, PAIRS) as i:
                for G in range(UNITS):
                    maxes_of(i, G + 1, range(0, 4))
                    if G > 0:
                        normalise(i, G - 1)
                    if G % 2:
                        k = 2 * i + G // 2 + 2
                        head.start()
                        head.vector_stats(d, k, G // 2 % 2, k % NSEQ)
                    projected(i, G + 2)
                    if G == PER_SEQ:
                        end_lo(i, 0)
                    k, par = 2 * i + G // 2 + 2, G // 2 % 2
                    if G < UNITS - 1:
                        maxes_of(i, G + 1, range(4, 6))
                    if G % 2:
                        head.vector_z(d, k, par, k % NSEQ)
                    if G < UNITS - 1:
                        maxes_of(i, G + 1, range(6, 8))
                    if G == PER_SEQ:
                        tail(i, 0)
                    if G % 2:
                        head.bank = bank_of(("head", G // 2 + 2))
                        head.vector_lo(d, k, par)
                normalise(i, UNITS - 1)
                maxes_of(i, UNITS, range(4, 6))
                end_lo(i, 1)
                maxes_of(i, UNITS, range(6, 8))
                tail(i, 1)

        @block.gpsimd
        def _(p):
            head.pool.credit(p)
            head.kept.credit(p)
            p.memset(K[96:97, :, :].bitcast(F32), 1.0).then_inc(ready, 1)
            p.wait_ge(ready, 1)
            p.memset(ones[:, :], 1.0).then_inc(ready, 1)
            p.wait_ge(ready, 2)
            p.memset(neg_max[:, :, :, :], 0.0).then_inc(ready, 1)
            for k in range(2):
                head.start()
                head.pool_scale(p, k, k)
                head.pool_keep(p, k, k, k)
            with p.Fori(0, PAIRS) as i:
                for j in range(2):
                    k = 2 * i + j + 2
                    head.start()
                    head.pool_scale(p, k, j)
                    p.wait_ge(vec_end.sem, vec_end.done(2 * i + j, "tail"))
                    head.pool_keep(p, k, j, k % NSEQ)


def attn0_layer(core, ctx, name):
    attn0_block(core, name, Weights(core, ctx, name + "w", "attn0_w", A0_COLS, [(0, A0_O, core.dram["L0_ffn_g1"].unsqueeze(1))]))


DH = 8
D_GROUPS = 4
PER_GROUP = 4
D_ROWS = 3 * PER_GROUP * DH
DF_Q = 0
DF_K = DF_Q + D_GROUPS * D_ROWS
DF_V = DF_K + D_GROUPS * D_ROWS
DF_P = DF_V + P
DF_COLS = DF_P + P


def diff_block(core, name, weights_in):
    nc, plan, ps, dram = core.nc, core.plan, core.psum, core.dram
    w_hi, w_lo = weights_in.hi, weights_in.lo
    O, R, S = 0, (1, 2, 3), (4, 6)
    SCALE = DH ** -0.5
    GROUPS = 2 * D_GROUPS
    BLOCKS = PER_GROUP * NQ
    NEG = D_ROWS + PER_GROUP
    with ExitStack() as ctx:
        sb = lambda n, s, t=F32: ctx.enter_context(nc.sbuf_tensor(name + n, s, t))
        head = Head(core, ctx, name, "ln", core.x, R[0])
        steps = lambda n: Steps(nc, ctx, plan, name + n)
        pe_proj, act_proj, vec_proj, pool_proj = (steps("_proj_" + e) for e in ("tensor", "scalar", "vector", "pool"))
        pe_max, act_max, vec_max = (steps("_max_" + e) for e in ("tensor", "scalar", "vector"))
        pe_att, act_att = (steps("_att_" + e) for e in ("tensor", "scalar"))
        pe_out, act_out, vec_out = (steps("_out_" + e) for e in ("tensor", "scalar", "vector"))
        pe_val, vec_val = (steps("_values_" + e) for e in ("tensor", "vector"))
        pe_end, act_end, vec_end, pool_end = (steps("_end_" + e) for e in ("tensor", "scalar", "vector", "pool"))
        loaded = core_semaphore(nc, name + "_rows_loaded")
        ready = core_semaphore(nc, name + "_fixed_ready")
        mixed = core_semaphore(nc, name + "_lambda_ready")
        Q, K = sb("Q", [P, 4, T], F32R), sb("K", [P, 2, T], F32R)
        kz = sb("kz", [P, 4, PER_GROUP, T], F32R)
        head_rows = sb("head_rows", [P, PER_GROUP])
        q_bias, k_bias = sb("q_bias", [D_ROWS, D_GROUPS]), sb("k_bias", [D_ROWS, D_GROUPS])
        v_bias, p_bias = sb("v_bias", [P, P]), sb("p_bias", [P, P])
        V = core.x2[:, :].rearrange("p (j t h e) -> p j t h e", j=2, t=NQ, h=16)
        neg_max = sb("neg_max", [P, NQ, NEG])
        weights = sb("weights", [P, NQ, PER_GROUP, T])
        o_sb = sb("o_sb", [P, T])
        rec = sb("rec", [P, NQ, PER_GROUP])
        on = sb("on", [P, NQ, P])
        f_hi, f_lo = sb("f_hi", [P, T], F32R), sb("f_lo", [P, T], F32R)
        lam = sb("lambdas", [P, 4, 8, DH])
        prod, sums, ex = sb("lambda_prod", [P, 2, 8, DH]), sb("lambda_sums", [P, 2, 8]), sb("lambda_exp", [P, 2, 8])
        gap, neg_lv = sb("lambda_gap", [P, 8]), sb("neg_lv", [P, 2])
        block = ctx.enter_context(nc.Block())

        BLOCK = [range(a, b) for a, b in ((0, 2), (2, 5), (5, 7), (7, 9), (9, 10), (10, 12), (12, 14), (14, 16))]

        proj = lambda n: [("q", n), ("k", n)] + ([("v", n)] if n % D_GROUPS == 0 else [])

        def slot_users(G):
            maxes = lambda *parts: [("max", G + 1, b) for part in parts for b in BLOCK[part]]
            u = maxes(0, 1)
            if G > 0:
                u += [("o", G - 1)]
            u += maxes(2, 3) + proj(G + 2) + maxes(4)
            if G == D_GROUPS:
                u += [("turned", 0)]
            u += maxes(5, 6, 7)
            if G == D_GROUPS:
                u += [("end", 0)]
            u += [("nm", G + 1)]
            if G in (0, 5):
                u += [("head", G // 4 + 1)]
            return u

        users = [u for G in range(GROUPS) for u in slot_users(G)] + [("o", GROUPS - 1), ("turned", 1), ("end", 1)]
        bank_of = lambda user: R[users.index(user) % len(R)]

        def freed(i, user, back):
            what, n = user[0], user[1]
            group = (n if i is None else GROUPS * i + n) - GROUPS * back
            seq = (n // D_GROUPS if what == "v" else n) - 2 * back if i is None else 2 * i + (n // D_GROUPS if what == "v" else n) - 2 * back
            if what in ("q", "k"):
                return vec_proj.sem, vec_proj.done(group, "lo", what)
            if what == "v":
                return vec_val.sem, vec_val.done(seq, "v")
            if what == "max":
                return vec_max.sem, vec_max.done(group, "max", user[2])
            if what == "nm":
                return act_max.sem, act_max.done(group, "nm")
            if what == "o":
                return vec_out.sem, vec_out.done(group, "on")
            if what == "turned":
                return vec_end.sem, vec_end.done(seq, "lo")
            if what == "end":
                return vec_end.sem, vec_end.done(seq, "tail")
            return head.low.sem, head.low.done(seq, "lo")

        before_loop = proj(8) + proj(9) + [("max", 8, b) for b in range(BLOCKS)] + [("nm", 8)]

        def ring(t, i, user):
            if i is None:
                at = before_loop.index(user)
                same = [u for u in before_loop[:at] if bank_of(u) == bank_of(user)]
                if same:
                    t.wait_ge(*freed(None, same[-1], 1))
            else:
                back, m = earlier(users.index(user), len(R), len(users))
                t.wait_ge(*freed(i, users[m], back))
            return bank_of(user)

        group_of = lambda i, n: n - GROUPS if i is None else GROUPS * i + n
        seq_of = lambda i, j: j - 2 if i is None else 2 * i + j

        @block.sync
        def _(sp):
            weights_in.sync_part(sp)
            rows = [(head_rows[:, :], "diff_head_rows"), (q_bias[:, :], "diff_bq"), (k_bias[:, :], "diff_bk")]
            for to, frm in rows:
                sp.dma_start(to, dram[frm]).then_inc(loaded, 16)
            for to, frm in ((v_bias, "L1_attn_b_bv"), (p_bias, "L1_attn_b_bp")):
                sp.dma_start(to[:, :], dram[frm].unsqueeze(0).to_broadcast([P, P])).then_inc(loaded, 16)
            for m, n in enumerate(("q1", "q2", "k1", "k2")):
                sp.dma_start(lam[:, m, :, :].rearrange("p h d -> p (h d)"),
                             dram["L1_attn_b_lambda_" + n].unsqueeze(0).to_broadcast([P, 8 * DH])).then_inc(loaded, 16)

        @block.tensor
        def _(t):
            for s in (pe_proj, pe_max, pe_att, pe_out, pe_val, pe_end, head.pe):
                s.credit(t)

            def project(i, n):
                j = n // D_GROUPS
                hi, lo = head.hi[:, j % 2, :], head.lo[:, j % 2, :]
                pe_proj.start()
                if n % D_GROUPS == 0:
                    t.wait_ge(head.low.sem, head.low.done(seq_of(i, j), "lo"))
                for user, c in ((("q", n), DF_Q), (("k", n), DF_K)):
                    c += (n % D_GROUPS) * D_ROWS
                    b = ring(t, i, user)
                    product(nc, ps[0:D_ROWS, b, :], w_hi[:, c:c + D_ROWS], w_lo[:, c:c + D_ROWS], hi, lo
                            ).then_inc(pe_proj.sem, pe_proj.step(user[0]))
                if n % D_GROUPS == 0:
                    pe_val.start()
                    b = ring(t, i, ("v", n))
                    for q in range(NQ):
                        c = slice(q * P, (q + 1) * P)
                        ins = product3(nc, ps[:, b, c], head.hi[:, j % 2, c], head.lo[:, j % 2, c],
                                       w_hi[:, DF_V:DF_V + P], w_lo[:, DF_V:DF_V + P])
                    ins.then_inc(pe_val.sem, pe_val.step("v"))

            def scores_for_max(i, n, part):
                for b in part:
                    hh, st = divmod(b, NQ)
                    if b == 0:
                        pe_max.start()
                        t.wait_ge(vec_proj.sem, vec_proj.done(group_of(i, n), "lo", "q"))
                    if st == 0:
                        t.wait_ge(pool_proj.sem, pool_proj.done(group_of(i, n), "kz", hh))
                    bank = ring(t, i, ("max", n, b))
                    nc.tensor.matmul(ps[:, bank, :], Q[0:D_ROWS, n % 4, st * P:(st + 1) * P], kz[0:D_ROWS, n % 4, hh, :],
                                     start=True, stop=True).then_inc(pe_max.sem, pe_max.step("max", b))

            def max_rows(i, n):
                t.wait_ge(vec_max.sem, vec_max.done(group_of(i, n), "max", BLOCKS - 1))
                bank = ring(t, i, ("nm", n))
                for st in range(NQ):
                    ins = nc.tensor.transpose(ps[0:NEG, bank, st * P:(st + 1) * P], neg_max[:, st, :], core.ident[:, :])
                ins.then_inc(pe_max.sem, pe_max.step("nm"))

            def scores(i, n, tt, pair):
                m = 2 * tt + pair
                g = group_of(i, n)
                if m == 0:
                    pe_att.start()
                    t.wait_ge(act_max.sem, act_max.done(g, "nm"))
                if m < 2:
                    t.wait_ge(act_att.sem, act_att.done(g, "exp", 6 + m, back=1))
                else:
                    t.wait_ge(act_att.sem, act_att.done(g, "exp", m - 2))
                for h in range(2):
                    ins = nc.tensor.matmul(ps[:, S[m % 2] + h, :], kz[0:NEG, n % 4, 2 * pair + h, tt * P:(tt + 1) * P],
                                           Q[0:NEG, n % 4, :], start=True, stop=True)
                ins.then_inc(pe_att.sem, pe_att.step("scores", m))

            def attend(i, n, tt):
                j, g = divmod(n, D_GROUPS)
                if tt == 0:
                    if g == 0:
                        t.wait_ge(vec_val.sem, vec_val.done(seq_of(i, j), "v"))
                    t.wait_ge(act_out.sem, act_out.done(group_of(i, n), "o", back=1))
                t.wait_ge(act_att.sem, act_att.done(group_of(i, n), "exp", 2 * tt + 1))
                for hh in range(PER_GROUP):
                    ins = nc.tensor.matmul(ps[32 * hh:32 * hh + 32, O, :], V[:, j, tt, g * PER_GROUP + hh, :], weights[:, tt, hh, :],
                                           start=(tt == 0), stop=(tt == NQ - 1))
                ins.then_inc(pe_att.sem, pe_att.step("pv", tt))

            def turn_output(i, n):
                pe_out.start()
                t.wait_ge(act_out.sem, act_out.done(group_of(i, n), "o"))
                bank = ring(t, i, ("o", n))
                for q in range(NQ):
                    ins = nc.tensor.transpose(ps[:, bank, q * P:(q + 1) * P], o_sb[:, q * P:(q + 1) * P], core.ident[:, :])
                ins.then_inc(pe_out.sem, pe_out.step("o"))

            def turn_heads(i, j):
                pe_end.start()
                t.wait_ge(vec_end.sem, vec_end.done(seq_of(i, j), "mixed"))
                bank = ring(t, i, ("turned", j))
                for q in range(NQ):
                    ins = nc.tensor.transpose(ps[:, bank, q * P:(q + 1) * P], on[:, q, :], core.ident[:, :])
                ins.then_inc(pe_end.sem, pe_end.step("turned"))

            def end(i, j):
                t.wait_ge(vec_end.sem, vec_end.done(seq_of(i, j), "lo"))
                bank = ring(t, i, ("end", j))
                for q in range(NQ):
                    c = slice(q * P, (q + 1) * P)
                    ins = product3(nc, ps[:, bank, c], f_hi[:, c], f_lo[:, c], w_hi[:, DF_P:DF_P + P], w_lo[:, DF_P:DF_P + P])
                ins.then_inc(pe_end.sem, pe_end.step("end"))

            head.start()
            head.bank = R[0]
            head.tensor_tr(t, 0)
            t.wait_ge(ready, 4)
            t.wait_ge(head.low.sem, head.low.done(0, "lo"))
            weights_in.tensor_part(t)
            project(None, 8)
            project(None, 9)
            scores_for_max(None, 8, range(BLOCKS))
            max_rows(None, 8)
            for u in before_loop[-3:]:
                t.wait_ge(*freed(None, u, 1))
            with t.Fori(0, PAIRS) as i:
                for G in range(GROUPS):
                    scores(i, G, 0, 0)
                    scores_for_max(i, G + 1, BLOCK[0])
                    scores(i, G, 0, 1)
                    scores_for_max(i, G + 1, BLOCK[1])
                    if G > 0:
                        turn_output(i, G - 1)
                    scores(i, G, 1, 0)
                    scores_for_max(i, G + 1, BLOCK[2])
                    scores(i, G, 1, 1)
                    attend(i, G, 0)
                    scores_for_max(i, G + 1, BLOCK[3])
                    project(i, G + 2)
                    scores_for_max(i, G + 1, BLOCK[4])
                    if G == D_GROUPS:
                        turn_heads(i, 0)
                    scores(i, G, 2, 0)
                    attend(i, G, 1)
                    scores_for_max(i, G + 1, BLOCK[5])
                    scores(i, G, 2, 1)
                    scores_for_max(i, G + 1, BLOCK[6])
                    scores(i, G, 3, 0)
                    scores_for_max(i, G + 1, BLOCK[7])
                    if G == D_GROUPS:
                        end(i, 0)
                    attend(i, G, 2)
                    scores(i, G, 3, 1)
                    max_rows(i, G + 1)
                    if G in (0, 5):
                        head.start()
                        head.bank = ring(t, i, ("head", G // 4 + 1))
                        head.tensor_tr(t, 2 * i + G // 4 + 1)
                    attend(i, G, 3)
                turn_output(i, GROUPS - 1)
                turn_heads(i, 1)
                end(i, 1)

        @block.scalar
        def _(a):
            for s in (act_proj, act_max, act_att, act_out, act_end, head.act):
                s.credit(a)
            copy = lambda to, frm: nc.scalar.activation(to, frm, ACT.Copy)

            def projected(i, n):
                act_proj.start()
                if i is not None:
                    a.wait_ge(pe_att.sem, pe_att.done(group_of(i, n - 2), "pv", NQ - 1, back=1))
                for what, to, bias in (("q", Q[0:D_ROWS, n % 4, :], q_bias), ("k", K[0:D_ROWS, n % 2, :], k_bias)):
                    if what == "k" and i is not None:
                        a.wait_ge(pool_proj.sem, pool_proj.done(group_of(i, n - 1), "kz", PER_GROUP - 1, back=1))
                    a.wait_ge(pe_proj.sem, pe_proj.done(group_of(i, n), what))
                    nc.scalar.activation(to, ps[0:D_ROWS, bank_of((what, n)), :], ACT.Identity,
                                         bias=bias[:, n % D_GROUPS:n % D_GROUPS + 1]).then_inc(act_proj.sem, act_proj.step("hi", what))

            def max_rows(i, n):
                act_max.start()
                a.wait_ge(pe_max.sem, pe_max.done(group_of(i, n), "nm"))
                copy(Q[D_ROWS:NEG, n % 4, :], ps[D_ROWS:NEG, bank_of(("nm", n)), :]).then_inc(act_max.sem, act_max.step("nm"))

            def exps(i, n, tt):
                for pair in range(2):
                    m = 2 * tt + pair
                    g = group_of(i, n)
                    if m == 0:
                        act_att.start()
                    if pair == 0:
                        a.wait_ge(pe_att.sem, pe_att.done(g, "pv", tt, back=1))
                    a.wait_ge(pe_att.sem, pe_att.done(g, "scores", m))
                    nc.scalar.activation(weights[:, tt, 2 * pair:2 * pair + 2, :], ps[:, S[m % 2]:S[m % 2] + 2, :], ACT.Exp,
                                         scale=SCALE).then_inc(act_att.sem, act_att.step("exp", m))

            def output(i, n):
                act_out.start()
                g = group_of(i, n)
                a.wait_ge(pe_out.sem, pe_out.done(g, "o", back=1))
                a.wait_ge(pe_att.sem, pe_att.done(g, "pv", NQ - 1))
                copy(o_sb[:, :], ps[:, O, :]).then_inc(act_out.sem, act_out.step("o"))

            def end(i, j):
                act_end.start()
                k = seq_of(i, j)
                a.wait_ge(pe_end.sem, pe_end.done(k, "end", back=1))
                a.wait_ge(pe_end.sem, pe_end.done(k, "turned"))
                copy(f_hi[:, :], ps[:, bank_of(("turned", j)), :]).then_inc(act_end.sem, act_end.step("hi"))

            head.start()
            head.bank = R[0]
            head.scalar_hi(a, 0, 0)
            weights_in.scalar_part(a)
            a.wait_ge(loaded, 16 * 9)
            a.wait_ge(ready, 4)
            a.wait_ge(mixed, 3)
            nc.scalar.activation(ex[:, :, :], sums[:, :, :], ACT.Exp).then_inc(mixed, 1)
            projected(None, 8)
            projected(None, 9)
            max_rows(None, 8)
            with a.Fori(0, PAIRS) as i:
                for G in range(GROUPS):
                    if G > 0:
                        output(i, G - 1)
                    exps(i, G, 0)
                    exps(i, G, 1)
                    projected(i, G + 2)
                    if G == D_GROUPS:
                        end(i, 0)
                    exps(i, G, 2)
                    exps(i, G, 3)
                    max_rows(i, G + 1)
                    if G in (0, 5):
                        head.start()
                        head.bank = bank_of(("head", G // 4 + 1))
                        head.scalar_hi(a, 2 * i + G // 4 + 1, (G // 4 + 1) % 2)
                output(i, GROUPS - 1)
                end(i, 1)

        @block.vector
        def _(d):
            for s in (vec_proj, vec_max, vec_out, vec_val, vec_end, head.vec, head.low):
                s.credit(d)

            def head_before(k, par, seq):
                head.start()
                head.vector_stats(d, k, par, seq)
                head.vector_z(d, k, par, seq)

            def projected(i, n):
                vec_proj.start()
                for what, to, bias in (("q", Q, q_bias), ("k", K, k_bias)):
                    rows = slice(64, 96) if what == "q" else slice(32, 64)
                    part = to[rows, n % (4 if what == "q" else 2), :]
                    d.wait_ge(act_proj.sem, act_proj.done(group_of(i, n), "hi", what))
                    nc.vector.scalar_tensor_tensor(part, ps[rows, bank_of((what, n)), :], bias[rows, n % D_GROUPS:n % D_GROUPS + 1], part,
                                                   ALU.add, ALU.subtract).then_inc(vec_proj.sem, vec_proj.step("lo", what))
                if n % D_GROUPS == 0:
                    j = n // D_GROUPS
                    vec_val.start()
                    if i is not None:
                        d.wait_ge(pe_att.sem, pe_att.done(group_of(i, n - 2), "pv", NQ - 1, back=1))
                    d.wait_ge(pe_val.sem, pe_val.done(seq_of(i, j), "v"))
                    view = lambda m: m.rearrange("p (t h e) -> p t h e", t=NQ, e=DH)
                    nc.vector.tensor_tensor(V[:, j % 2, :, :, 0:DH], view(ps[:, bank_of(("v", n)), :]),
                                            v_bias[:, :].rearrange("p (h e) -> p h e", e=DH).unsqueeze(1).to_broadcast([P, NQ, 16, DH]),
                                            ALU.add).then_inc(vec_val.sem, vec_val.step("v"))

            def maxes(i, n, part):
                for b in part:
                    hh, st = divmod(b, NQ)
                    if b == 0:
                        vec_max.start()
                        d.wait_ge(pe_max.sem, pe_max.done(group_of(i, n), "nm", back=1))
                    d.wait_ge(pe_max.sem, pe_max.done(group_of(i, n), "max", b))
                    nc.vector.tensor_reduce(neg_max[:, st, D_ROWS + hh:D_ROWS + hh + 1], ps[:, bank_of(("max", n, b)), :], AXX, ALU.max,
                                            negate=True).then_inc(vec_max.sem, vec_max.step("max", b))

            def normalise(i, n):
                j, g = divmod(n, D_GROUPS)
                vec_out.start()
                n_ = group_of(i, n)
                turned = ps[:, bank_of(("o", n)), :].rearrange("p (t h e) -> p t h e", t=NQ, e=32)
                d.wait_ge(vec_out.sem, vec_out.done(n_, "on", back=1))
                d.wait_ge(pe_out.sem, pe_out.done(n_, "o"))
                nc.vector.reciprocal(rec[:, :, :], turned[:, :, :, DH]).then_inc(vec_out.sem, vec_out.step("rec"))
                d.wait_ge(vec_out.sem, vec_out.done(n_, "rec"))
                if g == 0:
                    d.wait_ge(pe_end.sem, pe_end.done(seq_of(i, j), "turned", back=1))
                for st in range(NQ):
                    ins = nc.vector.tensor_tensor(on[:, st, 32 * g:32 * g + 32].rearrange("p (h e) -> p h e", e=DH), turned[:, st, :, 0:DH],
                                                  rec[:, st, :].unsqueeze(2).to_broadcast([P, PER_GROUP, DH]), ALU.mult)
                ins.then_inc(vec_out.sem, vec_out.step("on"))

            def mix(i, j):
                vec_end.start()
                d.wait_ge(vec_out.sem, vec_out.done(group_of(i, j * D_GROUPS + 3), "on"))
                nc.vector.scalar_tensor_tensor(on[:, :, 0:64], on[:, :, 64:P], neg_lv[:, 1:2], on[:, :, 0:64], ALU.mult, ALU.add
                                               ).then_inc(vec_end.sem, vec_end.step("mixed"))

            def end_lo(i, j):
                d.wait_ge(act_end.sem, act_end.done(seq_of(i, j), "hi"))
                nc.vector.tensor_tensor(f_lo[:, :], ps[:, bank_of(("turned", j)), :], f_hi[:, :], ALU.subtract
                                        ).then_inc(vec_end.sem, vec_end.step("lo"))

            def tail(i, j):
                k = seq_of(i, j)
                d.wait_ge(pool_end.sem, pool_end.done(k, "bias"))
                d.wait_ge(pe_end.sem, pe_end.done(k, "end"))
                at = cut(k * T, T)
                nc.vector.tensor_tensor(core.x[:, at], core.x[:, at], ps[:, bank_of(("end", j)), :], ALU.add
                                        ).then_inc(vec_end.sem, vec_end.step("tail"))

            head_before(0, 0, 0)
            head.bank = R[0]
            head.vector_lo(d, 0, 0)
            weights_in.vector_part(d)
            d.wait_ge(loaded, 16 * 9)
            d.wait_ge(ready, 4)
            nc.vector.tensor_tensor(prod[:, :, :, :], lam[:, 0:2, :, :], lam[:, 2:4, :, :], ALU.mult).then_inc(mixed, 1)
            d.wait_ge(mixed, 1)
            nc.vector.tensor_reduce(sums[:, :, :], prod[:, :, :, :], AXX, ALU.add).then_inc(mixed, 1)
            d.wait_ge(mixed, 2)
            nc.vector.tensor_scalar(sums[:, :, :], sums[:, :, :], 5.0, None, ALU.min).then_inc(mixed, 1)
            d.wait_ge(mixed, 4)
            nc.vector.tensor_tensor(gap[:, :], ex[:, 0, :], ex[:, 1, :], ALU.subtract).then_inc(mixed, 1)
            d.wait_ge(mixed, 5)
            nc.vector.tensor_scalar(gap[:, :], gap[:, :], 0.8, None, ALU.add).then_inc(mixed, 1)
            d.wait_ge(mixed, 6)
            nc.vector.tensor_reduce(neg_lv[:, 0:1], gap[:, :], AXX, ALU.add).then_inc(mixed, 1)
            d.wait_ge(mixed, 7)
            nc.vector.tensor_scalar(neg_lv[:, 1:2], neg_lv[:, 0:1], -0.125, None, ALU.mult).then_inc(mixed, 1)
            d.wait_ge(mixed, 8)
            projected(None, 8)
            projected(None, 9)
            maxes(None, 8, range(BLOCKS))
            with d.Fori(0, PAIRS) as i:
                for G in range(GROUPS):
                    maxes(i, G + 1, range(BLOCK[0].start, BLOCK[1].stop))
                    if G > 0:
                        normalise(i, G - 1)
                    if G == D_GROUPS:
                        mix(i, 0)
                    if G in (0, 5):
                        k = 2 * i + G // 4 + 1
                        head.start()
                        head.vector_stats(d, k, (G // 4 + 1) % 2, k % NSEQ if G else k)
                    maxes(i, G + 1, range(BLOCK[2].start, BLOCK[3].stop))
                    projected(i, G + 2)
                    if G == D_GROUPS:
                        end_lo(i, 0)
                    k, par = 2 * i + G // 4 + 1, (G // 4 + 1) % 2
                    seq = k % NSEQ if G else k
                    maxes(i, G + 1, range(BLOCK[4].start, BLOCK[5].stop))
                    if G in (0, 5):
                        head.vector_z(d, k, par, seq)
                    maxes(i, G + 1, range(BLOCK[6].start, BLOCK[7].stop))
                    if G == D_GROUPS:
                        tail(i, 0)
                    if G in (0, 5):
                        head.bank = bank_of(("head", G // 4 + 1))
                        head.vector_lo(d, 2 * i + G // 4 + 1, (G // 4 + 1) % 2)
                normalise(i, GROUPS - 1)
                mix(i, 1)
                end_lo(i, 1)
                tail(i, 1)

        @block.gpsimd
        def _(p):
            for s in (pool_proj, pool_end, head.pool):
                s.credit(p)

            def keys(i, n):
                pool_proj.start()
                if i is not None:
                    p.wait_ge(pe_att.sem, pe_att.done(group_of(i, n - 2), "pv", NQ - 1, back=1))
                p.wait_ge(vec_proj.sem, vec_proj.done(group_of(i, n), "lo", "k"))
                for hh in range(PER_GROUP):
                    nc.gpsimd.tensor_tensor(kz[:, n % 4, hh, :], K[:, n % 2, :], head_rows[:, hh:hh + 1].to_broadcast([P, T]), ALU.mult
                                            ).then_inc(pool_proj.sem, pool_proj.step("kz", hh))

            def bias(i, j):
                k = 2 * i + j
                pool_end.start()
                p.wait_ge(head.vec.sem, head.vec.done(k, "z"))
                tokens = core.x[:, cut(k * T, T)].rearrange("p (q d) -> p q d", d=P)
                nc.gpsimd.tensor_tensor(tokens, tokens, p_bias[:, :].unsqueeze(1).to_broadcast([P, NQ, P]), ALU.add
                                        ).then_inc(pool_end.sem, pool_end.step("bias"))

            head.start()
            head.pool_scale(p, 0, 0)
            p.memset(K[:, :, :].bitcast(F32), 0.0).then_inc(ready, 1)
            p.memset(neg_max[:, :, :], 0.0)
            p.memset(V[:, :, :, :, :], 0.0).then_inc(ready, 1)
            p.wait_ge(ready, 2)
            p.memset(V[:, :, :, :, DH:DH + 1], 1.0).then_inc(ready, 1)
            p.wait_ge(ready, 3)
            p.memset(K[D_ROWS:NEG, :, :].bitcast(F32), 1.0).then_inc(ready, 1)
            p.wait_ge(ready, 4)
            p.wait_ge(loaded, 16 * 9)
            keys(None, 8)
            keys(None, 9)
            with p.Fori(0, PAIRS) as i:
                for G in range(GROUPS):
                    if G in (0, 5):
                        head.start()
                        head.pool_scale(p, 2 * i + G // 4 + 1, (G // 4 + 1) % 2)
                    keys(i, G + 2)
                    if G in (1, 3):
                        bias(i, G // 2)


def diff_layer(core, ctx, name):
    diff_block(core, name, Weights(core, ctx, name + "w", "diff_w", DF_COLS))


HD, KV_TILES, PER_KV = 64, 2, 4
Q_TILES = KV_TILES * PER_KV
LI_Q, LI_QS = 0, Q_TILES * P
LI_K = LI_QS + Q_TILES * P
LI_KS = LI_K + KV_TILES * P
LI_V = LI_KS + KV_TILES * P
LI_O = LI_V + KV_TILES * P
LI_COLS = LI_O + Q_TILES * P


def light_block(core, name, weights_in):
    nc, plan, ps, dram = core.nc, core.plan, core.psum, core.dram
    w_hi, w_lo = weights_in.hi, weights_in.lo
    TR, R, S, O = 0, (1, 2, 3), (4, 5), (6, 7)
    GROUPS = 2 * KV_TILES
    SLOTS = GROUPS * NQ
    with ExitStack() as ctx:
        sb = lambda n, s, t=F32: ctx.enter_context(nc.sbuf_tensor(name + n, s, t))
        head = Head(core, ctx, name, "ln", core.x, TR)
        steps = lambda n: Steps(nc, ctx, plan, name + n)
        pe, act, vec, pool = steps("_tensor"), steps("_scalar"), steps("_vector"), steps("_pool")
        pe_seq, act_seq, vec_seq, pool_seq = (steps("_seq_tensor"), steps("_seq_scalar"), steps("_seq_vector"),
                                              steps("_seq_pool"))
        loaded = core_semaphore(nc, name + "_tables_loaded")
        ready = core_semaphore(nc, name + "_zeros_ready")
        cos, sin = sb("cos", [P, T]), sb("sin", [P, T])
        mask = sb("mask", [P, KV_TILES * 2, PER_KV * P])
        q_dec = sb("q_dec", [P, Q_TILES, 1, P])
        k_dec = sb("k_dec", [P, 4 * PER_KV])
        blk_dec = sb("blk_dec", [P, Q_TILES])
        turned = sb("turned", [P, 2, 2, T])
        qf = core.x2[:, :].rearrange("p (n t) -> p n t", t=T)
        q_hi, q_lo = sb("q_hi", [P, Q_TILES, T], F32R), sb("q_lo", [P, Q_TILES, T], F32R)
        kf = sb("kf", [P, KV_TILES, T])
        kz_hi = sb("kz_hi", [P, KV_TILES, 2, T], F32R)
        kz_lo = sb("kz_lo", [P, KV_TILES, 2, T], F32R)
        kt = sb("kt", [P, KV_TILES, 3, P])
        V = sb("V", [P, 2, NQ, KV_TILES * P])
        v_dec = sb("v_dec", [P, 2, 2, PER_KV, HD])
        state = sb("state", [P, NQ, PER_KV, P])
        decayed = sb("decayed", [P, PER_KV, P])
        A = sb("A", [P, 2, 2, T])
        o_hi, o_lo = sb("o_hi", [P, PER_KV, T], F32R), sb("o_lo", [P, PER_KV, T], F32R)
        out_sb = sb("out_sb", [P, T])
        block = ctx.enter_context(nc.Block())

        units = {0: ["k", "q0"], 1: ["q1", "q2"], 2: ["q3"], 3: []}
        order = ["k", "q0", "q1", "q2", "q3"]
        banks_of_unit = lambda n, gp, unit: [("proj", n, gp, unit, half) for half in range(2)]

        def slot_users(s):
            G, c = divmod(s, NQ)
            n, gp = divmod(G + 1, 2)
            users = [u for unit in units[c] for u in banks_of_unit(n, gp, unit)]
            if c == 2:
                users += [("v", n, gp, b) for b in range(2) if gp == 0] + [("kt", n, gp)]
            if c == 0 and G > 0:
                users += [("wo", G - 1)]
            if c < 3:
                users += [("kv", s)]
            return users

        users = [u for s in range(SLOTS) for u in slot_users(s)] + [("wo", GROUPS - 1)]
        bank_of = lambda user: R[users.index(user) % len(R)]

        def freed(i, user, back):
            if user[0] == "proj":
                return vec_seq.sem, vec_seq.done(2 * i + user[1] - 2 * back, "term", *user[2:])
            if user[0] in ("v", "kt"):
                return act_seq.sem, act_seq.done(2 * i + user[1] - 2 * back, user[0], *user[2:])
            if user[0] == "wo":
                eng = vec if user[1] % 2 else act
                return eng.sem, eng.done(i, *user, back=back)
            return vec.sem, vec.done(i, *user, back=back)

        def ring(t, i, user):
            at = users.index(user)
            if i is None:
                before = [m for m in range(at) if m % len(R) == at % len(R) and users[m][1:3] == user[1:3]
                          and users[m][0] in ("proj", "v", "kt")]
                if before:
                    t.wait_ge(*freed(-1, users[before[-1]], 0))
            else:
                back, m = earlier(at, len(R), len(users))
                t.wait_ge(*freed(i, users[m], back))
            return bank_of(user)

        def group_before(G):
            return (0, G - 2) if G >= 2 else (1, G + 2)

        def kv_place(s):
            return (s // NQ * 3 + s % NQ) % 2

        @block.sync
        def _(sp):
            weights_in.sync_part(sp)
            for to, frm in ((cos[:, :], "rope_cos"), (sin[:, :], "rope_sin"), (mask[:, :, :], "light_mask"),
                            (q_dec[:, :, :, :], "light_q_dec"), (k_dec[:, :], "light_k_dec"), (blk_dec[:, :], "light_blk_dec")):
                sp.dma_start(to, dram[frm]).then_inc(loaded, 16)

        def seq_of(i, n):
            return 0 if i is None else 2 * i + n

        @block.tensor
        def _(t):
            pe.credit(t)
            pe_seq.credit(t)
            head.pe.credit(t)

            def project_unit(i, n, gp, unit):
                k, par = seq_of(i, n), n % 2
                if unit == "k" and gp == 0:
                    pe_seq.start()
                    t.wait_ge(head.low.sem, head.low.done(k, "lo"))
                cols = (LI_K + gp * P, LI_KS + gp * P) if unit == "k" else [c + (gp * 4 + int(unit[1])) * P for c in (LI_Q, LI_QS)]
                for user, c in zip(banks_of_unit(n, gp, unit), cols):
                    b = ring(t, i, user)
                    product(nc, ps[:, b, :], w_hi[:, c:c + P], w_lo[:, c:c + P], head.hi[:, par, :], head.lo[:, par, :]
                            ).then_inc(pe_seq.sem, pe_seq.step("proj", *user[2:]))

            def project_rest(i, n, gp):
                k, par = seq_of(i, n), n % 2
                if gp == 0:
                    for b2 in range(2):
                        b = ring(t, i, ("v", n, gp, b2))
                        for h in range(2):
                            c = slice((2 * b2 + h) * P, (2 * b2 + h + 1) * P)
                            ins = product3(nc, ps[:, b, h * 256:h * 256 + 256], head.hi[:, par, c], head.lo[:, par, c],
                                           w_hi[:, LI_V:LI_V + 256], w_lo[:, LI_V:LI_V + 256])
                        ins.then_inc(pe_seq.sem, pe_seq.step("v", gp, b2))
                t.wait_ge(pool_seq.sem, pool_seq.done(k, "sum", gp, "k"))
                b = ring(t, i, ("kt", n, gp))
                for c in range(3):
                    ins = nc.tensor.transpose(ps[:, b, c * P:(c + 1) * P], kf[:, gp, c * P:(c + 1) * P], core.ident[:, :])
                ins.then_inc(pe_seq.sem, pe_seq.step("kt", gp))

            def scores(i, s):
                G, c = divmod(s, NQ)
                n, gp = divmod(G, 2)
                if c == 0:
                    t.wait_ge(vec_seq.sem, vec_seq.done(2 * i + n, "lo", gp, "q3"))
                for r in range(2):
                    back, m = earlier(s, 1, SLOTS)
                    t.wait_ge(vec.sem, vec.done(i, "masked", m, r, back=back))
                    cc = slice(c * P, (c + 1) * P)
                    q = lambda part: part[:, gp * 4:gp * 4 + 4, cc]
                    product(nc, ps[:, S[r], :].rearrange("p (u t) -> p u t", t=P), kz_hi[:, gp, r, cc], kz_lo[:, gp, r, cc],
                            q(q_hi), q(q_lo)).then_inc(pe.sem, pe.step("scores", s, r))

            def attend(i, s):
                G, c = divmod(s, NQ)
                n, gp = divmod(G, 2)
                bank = O[s % 2]
                back, m = earlier(s, 2, SLOTS)
                t.wait_ge(vec.sem, vec.done(i, "o_lo", m, back=back))
                t.wait_ge(act_seq.sem, act_seq.done(2 * i + n, "v", 0, 1))
                for r in range(2):
                    g = 2 * gp + r
                    t.wait_ge(vec.sem, vec.done(i, "masked", s, r))
                    ins = nc.tensor.matmul(ps[64 * r:64 * r + 64, bank, :], V[:, n, c, g * HD:(g + 1) * HD], A[:, s % 2, r, :],
                                           start=True, stop=(c == 0), skip_group_check=True)
                if c > 0:
                    t.wait_ge(vec.sem, vec.done(i, "kv", s - 1))
                    t.wait_ge(pool_seq.sem, pool_seq.done(2 * i + n, "decay", gp, 3))
                    for u in range(PER_KV):
                        ins = nc.tensor.matmul(ps[:, bank, u * P:(u + 1) * P], state[:, c, u, :], qf[:, gp * 4 + u, c * P:(c + 1) * P],
                                               start=False, stop=True, skip_group_check=True)
                ins.then_inc(pe.sem, pe.step("o", s))
                if c < 3:
                    t.wait_ge(act_seq.sem, act_seq.done(2 * i + n, "kt", gp))
                    t.wait_ge(pool.sem, pool.done(i, "v_dec", s))
                    b = ring(t, i, ("kv", s))
                    vs = v_dec[:, kv_place(s), :, :, :].rearrange("p r u e -> p (r u e)")
                    nc.tensor.matmul(ps[:, b, :], kt[:, gp, c, :], vs, start=True, stop=True).then_inc(pe.sem, pe.step("kv", s))

            def output(i, G):
                t.wait_ge(vec.sem, vec.done(i, "o_lo", G * NQ + NQ - 1))
                b = ring(t, i, ("wo", G))
                for u in range(PER_KV):
                    c = LI_O + ((G % 2) * 4 + u) * P
                    ins = product(nc, ps[:, b, :], w_hi[:, c:c + P], w_lo[:, c:c + P], o_hi[:, u, :], o_lo[:, u, :],
                                  start=(u == 0), stop=(u == PER_KV - 1))
                ins.then_inc(pe.sem, pe.step("wo", G))

            def tail(i, n, k_head):
                t.wait_ge(head.low.sem, head.low.done(k_head, "lo"))
                t.wait_ge(vec.sem, vec.done(i, "wo", 2 * n + 1))
                for q in range(NQ):
                    ins = nc.tensor.transpose(ps[:, TR, q * P:(q + 1) * P], out_sb[:, q * P:(q + 1) * P], core.ident[:, :])
                ins.then_inc(pe.sem, pe.step("tail", n))

            head.start()
            head.tensor_tr(t, 0)
            weights_in.tensor_part(t)
            for unit in order:
                project_unit(None, 2, 0, unit)
            project_rest(None, 2, 0)
            t.wait_ge(act_seq.sem, act_seq.done(0, "kt", 0))
            with t.Fori(0, PAIRS) as i:
                pe.start()
                scores(i, 0)
                for s in range(SLOTS):
                    G, c = divmod(s, NQ)
                    n, gp = divmod(G + 1, 2)
                    if s + 1 < SLOTS:
                        scores(i, s + 1)
                    for unit in units[c]:
                        project_unit(i, n, gp, unit)
                    if c == 2:
                        project_rest(i, n, gp)
                    if c == 0 and G > 0:
                        output(i, G - 1)
                    if c == 1 and G == 2:
                        tail(i, 0, 2 * i + 1)
                    if c == 3 and G == 0:
                        head.start()
                        t.wait_ge(vec.sem, vec.done(i, "tail", 1, back=1))
                        head.tensor_tr(t, 2 * i + 1)
                    if c == 3 and G == 2:
                        head.start()
                        t.wait_ge(vec.sem, vec.done(i, "tail", 0))
                        head.tensor_tr(t, 2 * i + 2)
                    attend(i, s)
                output(i, GROUPS - 1)
                tail(i, 1, 2 * i + 2)

        @block.scalar
        def _(a):
            act.credit(a)
            act_seq.credit(a)
            head.act.credit(a)
            copy = lambda to, frm: nc.scalar.activation(to, frm, ACT.Copy)

            def split_unit(i, n, gp, unit):
                k = seq_of(i, n)
                a.wait_ge(pool_seq.sem, pool_seq.done(k, "sum", gp, unit))
                if unit == "k":
                    if gp == 0:
                        act_seq.start()
                    for r in range(2):
                        rows = slice(64 * r, 64 * r + 64)
                        ins = copy(kz_hi[rows, gp, r, :], kf[rows, gp, :])
                    ins.then_inc(act_seq.sem, act_seq.step("hi", gp, unit))
                else:
                    q = gp * 4 + int(unit[1])
                    copy(q_hi[:, q, :], qf[:, q, :]).then_inc(act_seq.sem, act_seq.step("hi", gp, unit))

            def rest(i, n, gp):
                k = seq_of(i, n)
                if gp == 0:
                    if i is not None:
                        back, m = earlier(2 * n + 1, 4, 4)
                        a.wait_ge(pe.sem, pe.done(i, "o", m * NQ + NQ - 1, back=back))
                    for b2 in range(2):
                        a.wait_ge(pe_seq.sem, pe_seq.done(k, "v", gp, b2))
                        copy(V[:, n % 2, 2 * b2:2 * b2 + 2, :], ps[:, bank_of(("v", n, gp, b2)), :].rearrange("p (c e) -> p c e", e=256)
                             ).then_inc(act_seq.sem, act_seq.step("v", gp, b2))
                a.wait_ge(pe_seq.sem, pe_seq.done(k, "kt", gp))
                copy(kt[:, gp, :, :], ps[:, bank_of(("kt", n, gp)), 0:3 * P].rearrange("p (c e) -> p c e", e=P)
                     ).then_inc(act_seq.sem, act_seq.step("kt", gp))

            def o_part(i, s):
                G, c = divmod(s, NQ)
                if c == 0:
                    back, m = earlier(G, 1, GROUPS)
                    a.wait_ge(pe.sem, pe.done(i, "wo", m, back=back))
                a.wait_ge(pe.sem, pe.done(i, "o", s))
                copy(o_hi[:, :, c * P:(c + 1) * P], ps[:, O[s % 2], :].rearrange("p (u t) -> p u t", t=P)
                     ).then_inc(act.sem, act.step("o_hi", s))

            def out_part(i, G):
                back, m = earlier(G // 2, 1, 2)
                a.wait_ge(pe.sem, pe.done(i, "tail", m, back=back))
                a.wait_ge(pe.sem, pe.done(i, "wo", G))
                copy(out_sb[:, :], ps[:, bank_of(("wo", G)), :]).then_inc(act.sem, act.step("wo", G))

            head.start()
            head.scalar_hi(a, 0, 0)
            weights_in.scalar_part(a)
            a.wait_ge(ready, 3)
            for unit in order:
                split_unit(None, 2, 0, unit)
            rest(None, 2, 0)
            with a.Fori(0, PAIRS) as i:
                act.start()
                for s in range(SLOTS):
                    G, c = divmod(s, NQ)
                    n, gp = divmod(G + 1, 2)
                    if s > 0:
                        o_part(i, s - 1)
                    if c == 0:
                        back, m = group_before(G + 1)
                        a.wait_ge(pe.sem, pe.done(i, "o", m * NQ + NQ - 1, back=back))
                    for unit in units[c]:
                        split_unit(i, n, gp, unit)
                    if c == 2:
                        rest(i, n, gp)
                    if c == 0 and G in (1, 3):
                        out_part(i, G - 1)
                    if c == 3 and G == 0:
                        head.start()
                        head.scalar_hi(a, 2 * i + 1, 1)
                    if c == 3 and G == 2:
                        head.start()
                        head.scalar_hi(a, 2 * i + 2, 0)
                o_part(i, SLOTS - 1)

        @block.vector
        def _(d):
            vec.credit(d)
            vec_seq.credit(d)
            head.vec.credit(d)
            head.low.credit(d)

            def head_before(k, par, seq):
                head.start()
                head.vector_stats(d, k, par, seq)
                head.vector_z(d, k, par, seq)

            def rotate(i, n, gp, unit):
                k = seq_of(i, n)
                if unit == "k" and gp == 0:
                    vec_seq.start()
                x = gp * len(order) + order.index(unit)
                back, m = earlier(x, 2, 2 * len(order))
                d.wait_ge(pool_seq.sem, pool_seq.done(k, "sum", m // len(order), order[m % len(order)], back=back))
                for half, (user, table) in enumerate(zip(banks_of_unit(n, gp, unit), (cos, sin))):
                    d.wait_ge(pe_seq.sem, pe_seq.done(k, "proj", *user[2:]))
                    nc.vector.tensor_tensor(turned[:, x % 2, half, :], ps[:, bank_of(user), :], table[:, :], ALU.mult
                                            ).then_inc(vec_seq.sem, vec_seq.step("term", *user[2:]))

            def low(i, n, gp, unit):
                k = seq_of(i, n)
                d.wait_ge(act_seq.sem, act_seq.done(k, "hi", gp, unit))
                if unit == "k":
                    for r in range(2):
                        rows = slice(64 * r, 64 * r + 64)
                        ins = nc.vector.tensor_tensor(kz_lo[rows, gp, r, :], kf[rows, gp, :], kz_hi[rows, gp, r, :], ALU.subtract)
                    ins.then_inc(vec_seq.sem, vec_seq.step("lo", gp, unit))
                else:
                    q = gp * 4 + int(unit[1])
                    nc.vector.tensor_tensor(q_lo[:, q, :], qf[:, q, :], q_hi[:, q, :], ALU.subtract
                                            ).then_inc(vec_seq.sem, vec_seq.step("lo", gp, unit))

            def masked(i, s):
                G, c = divmod(s, NQ)
                back, m = earlier(s, 2, SLOTS)
                d.wait_ge(pe.sem, pe.done(i, "o", m, back=back))
                for r in range(2):
                    d.wait_ge(pe.sem, pe.done(i, "scores", s, r))
                    nc.vector.tensor_tensor(A[:, s % 2, r, :], ps[:, S[r], :], mask[:, 2 * (G % 2) + r, :], ALU.mult
                                            ).then_inc(vec.sem, vec.step("masked", s, r))

            def state_after(i, s):
                G, c = divmod(s, NQ)
                back, m = earlier(G, 1, GROUPS)
                d.wait_ge(pe.sem, pe.done(i, "o", m * NQ + c + 1, back=back))
                if c > 0:
                    d.wait_ge(pool.sem, pool.done(i, "decayed", s))
                elif G > 0:
                    d.wait_ge(pool.sem, pool.done(i, "decayed", s - 2))
                else:
                    d.wait_ge(pool.sem, pool.done(i, "decayed", SLOTS - 2, back=1))
                d.wait_ge(pe.sem, pe.done(i, "kv", s))
                for r in range(2):
                    rows = slice(64 * r, 64 * r + 64)
                    new = ps[rows, bank_of(("kv", s)), r * 256:(r + 1) * 256].rearrange("p (u e) -> p u e", e=HD)
                    to = state[rows, c + 1, :, r * HD:(r + 1) * HD]
                    ins = (nc.vector.tensor_copy(to, new) if c == 0 else
                           nc.vector.tensor_tensor(to, new, decayed[rows, :, r * HD:(r + 1) * HD], ALU.add))
                ins.then_inc(vec.sem, vec.step("kv", s))

            def o_part(i, s):
                c = s % NQ
                cc = slice(c * P, (c + 1) * P)
                d.wait_ge(act.sem, act.done(i, "o_hi", s))
                nc.vector.tensor_tensor(o_lo[:, :, cc], ps[:, O[s % 2], :].rearrange("p (u t) -> p u t", t=P), o_hi[:, :, cc],
                                        ALU.subtract).then_inc(vec.sem, vec.step("o_lo", s))

            def out_part(i, G):
                d.wait_ge(act.sem, act.done(i, "wo", G - 1))
                d.wait_ge(pe.sem, pe.done(i, "wo", G))
                nc.vector.tensor_tensor(out_sb[:, :], ps[:, bank_of(("wo", G)), :], out_sb[:, :], ALU.add
                                        ).then_inc(vec.sem, vec.step("wo", G))

            def tail(i, n):
                d.wait_ge(pe.sem, pe.done(i, "tail", n))
                at = cut((2 * i + n) * T, T)
                nc.vector.tensor_tensor(core.x[:, at], core.x[:, at], ps[:, TR, :], ALU.add).then_inc(vec.sem, vec.step("tail", n))

            head_before(0, 0, 0)
            head.vector_lo(d, 0, 0)
            weights_in.vector_part(d)
            d.wait_ge(loaded, 16 * 6)
            d.wait_ge(ready, 3)
            for c in range(NQ):
                for unit in units[c - 1] if c else ():
                    low(None, 2, 0, unit)
                for unit in units[c]:
                    rotate(None, 2, 0, unit)
            with d.Fori(0, PAIRS) as i:
                vec.start()
                masked(i, 0)
                for s in range(SLOTS):
                    G, c = divmod(s, NQ)
                    n, gp = divmod(G + 1, 2)
                    if s > 0 and c > 0:
                        state_after(i, s - 1)
                    if c > 0:
                        for unit in units[c - 1]:
                            low(i, n, gp, unit)
                    if s + 1 < SLOTS:
                        masked(i, s + 1)
                    if s > 0:
                        o_part(i, s - 1)
                    if c == 1 and G == 2:
                        out_part(i, 1)
                    for unit in units[c]:
                        rotate(i, n, gp, unit)
                    if c == 1 and G == 2:
                        tail(i, 0)
                    if c == 1 and G == 0:
                        head.start()
                        head.vector_stats(d, 2 * i + 1, 1, 2 * i + 1)
                    if c == 2 and G == 0:
                        head.vector_z(d, 2 * i + 1, 1, 2 * i + 1)
                    if c == 3 and G == 0:
                        head.vector_lo(d, 2 * i + 1, 1)
                    if c == 1 and G == 2:
                        head.start()
                        head.vector_stats(d, 2 * i + 2, 0, (2 * i + 2) % NSEQ)
                    if c == 2 and G == 2:
                        head.vector_z(d, 2 * i + 2, 0, (2 * i + 2) % NSEQ)
                    if c == 3 and G == 2:
                        head.vector_lo(d, 2 * i + 2, 0)
                o_part(i, SLOTS - 1)
                out_part(i, 3)
                tail(i, 1)

        @block.gpsimd
        def _(p):
            pool.credit(p)
            pool_seq.credit(p)
            head.pool.credit(p)

            def add_terms(i, n, gp, unit):
                k = seq_of(i, n)
                if unit == "k" and gp == 0:
                    pool_seq.start()
                x = gp * len(order) + order.index(unit)
                if i is not None and unit == "k":
                    back, m = group_before(2 * n + gp)
                    p.wait_ge(pe.sem, pe.done(i, "o", m * NQ + NQ - 1, back=back))
                p.wait_ge(vec_seq.sem, vec_seq.done(k, "term", gp, unit, 1))
                to = kf[:, gp, :] if unit == "k" else qf[:, gp * 4 + int(unit[1]), :]
                nc.gpsimd.tensor_tensor(to, turned[:, x % 2, 0, :], turned[:, x % 2, 1, :], ALU.add
                                        ).then_inc(pool_seq.sem, pool_seq.step("sum", gp, unit))

            def decay_queries(i, n, gp, u):
                k = seq_of(i, n)
                q = gp * 4 + u
                p.wait_ge(vec_seq.sem, vec_seq.done(k, "lo", gp, f"q{u}"))
                later = qf[:, q, P:T].rearrange("p (c t) -> p c t", t=P)
                nc.gpsimd.tensor_tensor(later, later, q_dec[:, q, :, :].to_broadcast([P, 3, P]), ALU.mult
                                        ).then_inc(pool_seq.sem, pool_seq.step("decay", gp, u))

            def values_decayed(i, s):
                G, c = divmod(s, NQ)
                n, gp = divmod(G, 2)
                back, m = earlier(G * 3 + c, 2, GROUPS * 3)
                p.wait_ge(pe.sem, pe.done(i, "kv", m // 3 * NQ + m % 3, back=back))
                p.wait_ge(act_seq.sem, act_seq.done(2 * i + n, "v", 0, 1))
                v = V[:, n, c, gp * P:(gp + 1) * P].rearrange("p (r e) -> p r e", e=HD).unsqueeze(2).to_broadcast([P, 2, PER_KV, HD])
                dec = k_dec[:, gp * 8:gp * 8 + 8].rearrange("p (r u) -> p r u", u=PER_KV).unsqueeze(3).to_broadcast([P, 2, PER_KV, HD])
                nc.gpsimd.tensor_tensor(v_dec[:, kv_place(s), :, :, :], v, dec, ALU.mult).then_inc(pool.sem, pool.step("v_dec", s))

            def decay_state(i, s):
                G, c = divmod(s, NQ)
                gp = G % 2
                p.wait_ge(vec.sem, vec.done(i, "kv", s - 1))
                dec = blk_dec[:, gp * 4:gp * 4 + 4].unsqueeze(2).to_broadcast([P, PER_KV, P])
                nc.gpsimd.tensor_tensor(decayed[:, :, :], state[:, c, :, :], dec, ALU.mult).then_inc(pool.sem, pool.step("decayed", s))

            head.start()
            head.pool_scale(p, 0, 0)
            p.memset(kz_hi[:, :, :, :].bitcast(F32), 0.0).then_inc(ready, 1)
            p.memset(kz_lo[:, :, :, :].bitcast(F32), 0.0).then_inc(ready, 1)
            p.memset(state[:, :, :, :], 0.0).then_inc(ready, 1)
            p.wait_ge(loaded, 16 * 6)
            for c in range(NQ):
                for unit in units[c]:
                    add_terms(None, 2, 0, unit)
                for unit in units[c - 1] if c else ():
                    if unit != "k":
                        decay_queries(None, 2, 0, int(unit[1]))
            with p.Fori(0, PAIRS) as i:
                pool.start()
                for s in range(SLOTS):
                    G, c = divmod(s, NQ)
                    n, gp = divmod(G + 1, 2)
                    if c == 2 and G == 0:
                        head.start()
                        head.pool_scale(p, 2 * i + 1, 1)
                    if c == 2 and G == 2:
                        head.start()
                        head.pool_scale(p, 2 * i + 2, 0)
                    if c < 3:
                        values_decayed(i, s)
                    if c in (1, 2):
                        decay_state(i, s)
                    for unit in units[c]:
                        add_terms(i, n, gp, unit)
                    if c > 0:
                        for unit in units[c - 1]:
                            if unit != "k":
                                decay_queries(i, n, gp, int(unit[1]))


def light_layer(core, ctx, name):
    light_block(core, name, Weights(core, ctx, name + "w", "light_w", LI_COLS, raw=core.x2))


RA_K, RA_V, RA_R = 0, 2 * P, 4 * P
RA_COLS = 6 * P


def load_vectors(core, block, loaded, weights_in, pairs, load=None):
    @block.sync
    def _(sp):
        if load:
            load.sync_first(sp)
        for column, vector in pairs:
            sp.dma_start(column, vector.unsqueeze(1)).then_inc(loaded, 16)
        weights_in.sync_part(sp)
        if load:
            load.sync_rest(sp)


def mixed(nc, out, w_hi, w_lo, c, head, par):
    now, before = slice(1, 1 + T), slice(0, T)
    a, b = slice(c, c + P), slice(c + P, c + 2 * P)
    product(nc, out, w_hi[:, a], w_lo[:, a], head.hi[:, par, now], head.lo[:, par, now], stop=False)
    return product(nc, out, w_hi[:, b], w_lo[:, b], head.hi[:, par, before], head.lo[:, par, before], start=False)


def time_mix_block(core, name, weights_in):
    nc, plan, ps, d_ = core.nc, core.plan, core.psum, core.dram
    w_hi, w_lo = weights_in.hi, weights_in.lo
    TR, KB, VB, RB = 0, (1, 2), (3, 4), (5, 6)
    J = (0, 1)
    with ExitStack() as ctx:
        sb = lambda n, s, t=F32: ctx.enter_context(nc.sbuf_tensor(name + n, s, t))
        cols = sb("cols", [P, 5])
        w, u, gain, bias, w_u = (cols[:, c:c + 1] for c in range(5))
        head = Head(core, ctx, name, "ln2", core.x, TR, affine=(gain, bias))
        vec, act = Steps(nc, ctx, plan, name + "_vector"), Steps(nc, ctx, plan, name + "_scalar")
        pe, pool = Steps(nc, ctx, plan, name + "_tensor"), Steps(nc, ctx, plan, name + "_pool")
        load = Load(core)
        pe_in = Steps(nc, ctx, plan, name + "_in_tensor")
        loaded = core_semaphore(nc, name + "_vectors_loaded")
        fixed = core_semaphore(nc, name + "_fixed_ready")
        two = lambda n, width=T: sb(n, [P, 2, width])
        kw, er, ec, ln_s = two("kw"), two("er"), two("ec"), two("ln_s")
        M, S, A = two("M", 1 + T), two("S", 1 + T), two("A", 1 + T)
        q, lower, upper, e1, e2 = two("q"), two("lower"), two("upper"), two("e1"), two("e2")
        ev, sig, r, y = two("ev"), two("sig"), two("r"), two("y")
        block = ctx.enter_context(nc.Block())
        load_vectors(core, block, loaded, weights_in, [(w, d_["L0_attn_a_time_decay"]), (u, d_["L0_attn_a_time_first"]),
                                           (gain, d_["L0_attn_a_ln1_g"]), (bias, d_["L0_attn_a_ln1_b"])], load)

        @block.tensor
        def _(t):
            pe.credit(t)
            head.pe.credit(t)
            t.wait_ge(load.constants_loaded, 16)
            for k in J:
                head.start()
                head.tensor_tr(t, k)
            weights_in.tensor_part(t)
            t.wait_ge(fixed, 4)
            pe_in.credit(t)

            def make(what, banks, c, j):
                mixed(nc, ps[:, banks[j], :], w_hi, w_lo, c, head, j).then_inc(pe_in.sem, pe_in.step(what, j))

            t.wait_ge(head.low.sem, head.low.done(1, "lo"))
            pe_in.start()
            for what, banks, c in (("k", KB, RA_K), ("r", RB, RA_R), ("v", VB, RA_V)):
                for j in J:
                    make(what, banks, c, j)
            with t.Fori(0, PAIRS) as i:
                pe.start()
                for j in J:
                    head.start()
                    if j == 0:
                        t.wait_ge(vec.sem, vec.done(i, "tail", 1, back=1))
                    head.tensor_tr(t, 2 * i + 2 + j)
                pe_in.start()
                for j in J:
                    t.wait_ge(head.low.sem, head.low.done(2 * i + 2 + j, "lo"))
                    t.wait_ge(act.sem, act.done(i, "kw", j))
                    make("k", KB, RA_K, j)
                for j in J:
                    t.wait_ge(act.sem, act.done(i, "r", j))
                    make("r", RB, RA_R, j)
                for j in J:
                    t.wait_ge(vec.sem, vec.done(i, "y", j))
                    make("v", VB, RA_V, j)
                for j in J:
                    t.wait_ge(pool.sem, pool.done(i, "ry", j))
                    t.wait_ge(*((head.act.sem, head.act.done(2 * i + 3, "full")) if j == 0 else (vec.sem, vec.done(i, "tail", 0))))
                    for n in range(NQ):
                        ins = nc.tensor.transpose(ps[:, TR, n * P:(n + 1) * P], y[:, j, n * P:(n + 1) * P], core.ident[:, :])
                    ins.then_inc(pe.sem, pe.step("tail", j))

        @block.scalar
        def _(a):
            act.credit(a)
            head.act.credit(a)
            a.wait_ge(loaded, 16 * 4)
            for k in J:
                head.start()
                head.scalar_hi(a, k, k)
            weights_in.scalar_part(a)
            a.wait_ge(fixed, 4)

            def head_hi(i, j):
                a.wait_ge(pe_in.sem, pe_in.done(i, "v", 1))
                head.start()
                head.scalar_hi(a, 2 * i + 2 + j, j)

            with a.Fori(0, PAIRS) as i:
                act.start()
                for j in J:
                    a.wait_ge(pe_in.sem, pe_in.done(i, "k", j))
                    a.wait_ge(pool.sem, pool.done(i, "q1", j, back=1))
                    nc.scalar.activation(kw[:, j, :], ps[:, KB[j], :], ACT.Identity, bias=w).then_inc(act.sem, act.step("kw", j))
                nc.scalar.preload_act_table_set("natural_log_exp_and_others")
                for j in J:
                    a.wait_ge(vec.sem, vec.done(i, "rr", j))
                    nc.scalar.activation(er[:, j, :], er[:, j, :], ACT.Exp, bias=w).then_inc(act.sem, act.step("er", j))
                    a.wait_ge(vec.sem, vec.done(i, "cc", j))
                    nc.scalar.activation(ec[:, j, :], ec[:, j, :], ACT.Exp).then_inc(act.sem, act.step("ec", j))
                for j in J:
                    a.wait_ge(vec.sem, vec.done(i, "S", j))
                    nc.scalar.activation(ln_s[:, j, :], S[:, j, 0:T], ACT.Ln).then_inc(act.sem, act.step("ln_s", j))
                head_hi(i, 0)
                for j in J:
                    a.wait_ge(vec.sem, vec.done(i, "upper", j))
                    nc.scalar.activation(e1[:, j, :], lower[:, j, :], ACT.Exp).then_inc(act.sem, act.step("e1", j))
                    nc.scalar.activation(e2[:, j, :], upper[:, j, :], ACT.Exp, scale=-1.0).then_inc(act.sem, act.step("e2", j))
                head_hi(i, 1)
                for j in J:
                    nc.scalar.activation(sig[:, j, :], q[:, j, :], ACT.Sigmoid, bias=w_u).then_inc(act.sem, act.step("sig", j))
                    a.wait_ge(pe_in.sem, pe_in.done(i, "r", j))
                    nc.scalar.activation(r[:, j, :], ps[:, RB[j], :], ACT.Sigmoid).then_inc(act.sem, act.step("r", j))

        @block.vector
        def _(d):
            vec.credit(d)
            head.vec.credit(d)
            head.low.credit(d)
            d.wait_ge(loaded, 16 * 4)
            nc.vector.memset(M[:, :, 0:1], -1e38).then_inc(fixed, 1)
            nc.vector.memset(S[:, :, 0:1], 1.0)
            nc.vector.memset(A[:, :, 0:1], 0.0)
            nc.vector.memset(head.hi[:, :, 0:1].bitcast(F32), 0.0).then_inc(fixed, 1)
            nc.vector.memset(head.lo[:, :, 0:1].bitcast(F32), 0.0).then_inc(fixed, 1)
            nc.vector.tensor_tensor(w_u, w, u, ALU.subtract).then_inc(fixed, 1)
            for k in J:
                d.wait_ge(load.x_loaded[k], 16)
                head.start()
                head.vector_stats(d, k, k, k)
                head.vector_z(d, k, k, k)
                head.vector_lo(d, k, k)
            weights_in.vector_part(d)
            d.wait_ge(load.rest_loaded, 16 * (NSEQ - 2))
            n = nc.vector
            with d.Fori(0, PAIRS) as i:
                vec.start()
                inc = lambda ins, *key: ins.then_inc(vec.sem, vec.step(*key))
                head.start()
                for j in J:
                    d.wait_ge(act.sem, act.done(i, "kw", j))
                    d.wait_ge(pool.sem, pool.done(i, "q1", j, back=1))
                    inc(n.tensor_tensor_scan(M[:, j, 1:1 + T], w.to_broadcast([P, T]), kw[:, j, :], -1e38, ALU.add, ALU.max), "M", j)
                for j in J:
                    d.wait_ge(vec.sem, vec.done(i, "M", j))
                    d.wait_ge(vec.sem, vec.done(i, "S", j, back=1))
                    inc(n.tensor_tensor(er[:, j, :], M[:, j, 0:T], M[:, j, 1:1 + T], ALU.subtract), "rr", j)
                    inc(n.tensor_tensor(ec[:, j, :], kw[:, j, :], M[:, j, 1:1 + T], ALU.subtract), "cc", j)
                for j in J:
                    head.start()
                    k, seq = 2 * i + 2 + j, (2 * i + 2 + j) % NSEQ
                    head.vector_stats(d, k, j, seq)
                    if j == 0:
                        d.wait_ge(act.sem, act.done(i, "ec", 0))
                        d.wait_ge(act.sem, act.done(i, "ln_s", 0, back=1))
                        inc(n.tensor_tensor_scan(S[:, 0, 1:1 + T], er[:, 0, :], ec[:, 0, :], 1.0, ALU.mult, ALU.add), "S", 0)
                    else:
                        d.wait_ge(act.sem, act.done(i, "ec", 1))
                        d.wait_ge(act.sem, act.done(i, "ln_s", 1, back=1))
                        inc(n.tensor_tensor_scan(S[:, 1, 1:1 + T], er[:, 1, :], ec[:, 1, :], 1.0, ALU.mult, ALU.add), "S", 1)
                    head.vector_z(d, k, j, seq)
                for j in J:
                    d.wait_ge(pool.sem, pool.done(i, "q", j))
                    d.wait_ge(act.sem, act.done(i, "e1", j, back=1))
                    d.wait_ge(act.sem, act.done(i, "e2", j, back=1))
                    inc(n.tensor_scalar(lower[:, j, :], q[:, j, :], w, 0.0, ALU.add, ALU.min), "lower", j)
                    inc(n.tensor_scalar(upper[:, j, :], q[:, j, :], w, 0.0, ALU.add, ALU.max), "upper", j)
                head.start()
                head.vector_lo(d, 2 * i + 2, 0)
                for j in J:
                    d.wait_ge(pe_in.sem, pe_in.done(i, "v", j))
                    d.wait_ge(act.sem, act.done(i, "e2", j))
                    d.wait_ge(vec.sem, vec.done(i, "A", j, back=1))
                    inc(n.tensor_tensor(ev[:, j, :], e2[:, j, :], ps[:, VB[j], :], ALU.mult), "ev", j)
                head.start()
                head.vector_lo(d, 2 * i + 3, 1)
                for j in J:
                    d.wait_ge(vec.sem, vec.done(i, "ev", j))
                    d.wait_ge(act.sem, act.done(i, "e1", j))
                    inc(n.tensor_tensor_scan(A[:, j, 1:1 + T], e1[:, j, :], ev[:, j, :], 0.0, ALU.mult, ALU.add), "A", j)
                for j in J:
                    d.wait_ge(vec.sem, vec.done(i, "A", j))
                    d.wait_ge(pe.sem, pe.done(i, "tail", j, back=1))
                    inc(n.tensor_tensor(y[:, j, :], A[:, j, 0:T], ps[:, VB[j], :], ALU.subtract), "a_v", j)
                for j in J:
                    d.wait_ge(pool.sem, pool.done(i, "sy", j))
                    inc(n.tensor_tensor(y[:, j, :], y[:, j, :], ps[:, VB[j], :], ALU.add), "y", j)
                for j in J:
                    d.wait_ge(head.kept.sem, head.kept.done(2 * i + j, "keep"))
                    d.wait_ge(pe.sem, pe.done(i, "tail", j))
                    inc(n.tensor_tensor(core.x2[:, cut((2 * i + j) * T, T)], head.keep[:, j, :], ps[:, TR, :], ALU.add), "tail", j)

        @block.gpsimd
        def _(p):
            pool.credit(p)
            head.pool.credit(p)
            head.kept.credit(p)
            load.gpsimd_part(p)
            for k in J:
                head.start()
                head.pool_scale(p, k, k)
                head.pool_keep(p, k, k, k)
                if k == 0:
                    weights_in.gpsimd_part(p)
            tt = nc.gpsimd.tensor_tensor
            with p.Fori(0, PAIRS) as i:
                pool.start()
                for j in J:
                    p.wait_ge(vec.sem, vec.done(i, "cc", j))
                    p.wait_ge(act.sem, act.done(i, "sig", j, back=1))
                    p.wait_ge(vec.sem, vec.done(i, "upper", j, back=1))
                    tt(q[:, j, :], M[:, j, 0:T], kw[:, j, :], ALU.subtract).then_inc(pool.sem, pool.step("q1", j))
                for j in J:
                    head.start()
                    head.pool_scale(p, 2 * i + 2 + j, j)
                for j in J:
                    p.wait_ge(act.sem, act.done(i, "ln_s", j))
                    p.wait_ge(pool.sem, pool.done(i, "q1", j))
                    tt(q[:, j, :], q[:, j, :], ln_s[:, j, :], ALU.add).then_inc(pool.sem, pool.step("q", j))
                for j in J:
                    p.wait_ge(act.sem, act.done(i, "sig", j))
                    p.wait_ge(vec.sem, vec.done(i, "a_v", j))
                    tt(y[:, j, :], y[:, j, :], sig[:, j, :], ALU.mult).then_inc(pool.sem, pool.step("sy", j))
                for j in J:
                    p.wait_ge(act.sem, act.done(i, "r", j))
                    p.wait_ge(vec.sem, vec.done(i, "y", j))
                    tt(y[:, j, :], y[:, j, :], r[:, j, :], ALU.mult).then_inc(pool.sem, pool.step("ry", j))
                for j in J:
                    head.start()
                    p.wait_ge(vec.sem, vec.done(i, "tail", j))
                    head.pool_keep(p, 2 * i + 2 + j, j, (2 * i + 2 + j) % NSEQ)


RB_CK, RB_CR = 0, 8 * P
RB_CV = RB_CR + 2 * P
RB_COLS = RB_CV + 4 * P


def channel_mix_block(core, name, weights_in):
    nc, plan, ps, d_ = core.nc, core.plan, core.psum, core.dram
    w_hi, w_lo = weights_in.hi, weights_in.lo
    TR, H, CR, OUT = 0, (1, 2, 3), 4, 5
    FT = 4
    NS, LAG, RING = 2 * FT, 2, 4
    with ExitStack() as ctx:
        sb = lambda n, s, t=F32: ctx.enter_context(nc.sbuf_tensor(name + n, s, t))
        cols = sb("cols", [P, 2])
        head = Head(core, ctx, name, "ln", core.x2, TR, affine=(cols[:, 0:1], cols[:, 1:2]))
        vec, act = Steps(nc, ctx, plan, name + "_vector"), Steps(nc, ctx, plan, name + "_scalar")
        pe, pool = Steps(nc, ctx, plan, name + "_tensor"), Steps(nc, ctx, plan, name + "_pool")
        loaded = core_semaphore(nc, name + "_vectors_loaded")
        fixed = core_semaphore(nc, name + "_fixed_ready")
        a_sb, sq = sb("relu", [P, 2, T]), sb("square", [P, 2, T])
        sq_hi, sq_lo = sb("square_hi", [P, RING, T], F32R), sb("square_lo", [P, RING, T], F32R)
        gate, out_sb = sb("gate", [P, T]), sb("out_sb", [P, T])
        block = ctx.enter_context(nc.Block())
        load_vectors(core, block, loaded, weights_in, [(cols[:, 0:1], d_["L0_attn_a_ln2_g"]), (cols[:, 1:2], d_["L0_attn_a_ln2_b"])])

        @block.tensor
        def _(t):
            pe.credit(t)
            head.pe.credit(t)
            head.start()
            head.tensor_tr(t, 0)
            t.wait_ge(fixed, 2)
            weights_in.tensor_part(t)

            def down(i, n):
                j, f = divmod(n, FT)
                if f == 0:
                    back, m = earlier(j, 1, 2)
                    t.wait_ge(vec.sem, vec.done(i, "out", m, back=back))
                t.wait_ge(vec.sem, vec.done(i, "sq_lo", n))
                c = RB_CV + f * P
                product(nc, ps[:, OUT, :], w_hi[:, c:c + P], w_lo[:, c:c + P], sq_hi[:, n % RING, :], sq_lo[:, n % RING, :],
                        start=(f == 0), stop=(f == FT - 1)).then_inc(pe.sem, pe.step("down", n))

            def tail(i, j):
                t.wait_ge(vec.sem, vec.done(i, "out", j))
                t.wait_ge(head.act.sem, head.act.done(2 * i + j + 1, "full"))
                for q in range(NQ):
                    ins = nc.tensor.transpose(ps[:, TR, q * P:(q + 1) * P], out_sb[:, q * P:(q + 1) * P], core.ident[:, :])
                ins.then_inc(pe.sem, pe.step("tail", j))

            with t.Fori(0, PAIRS) as i:
                pe.start()
                for n in range(NS):
                    j, f = divmod(n, FT)
                    if f == 0:
                        t.wait_ge(head.low.sem, head.low.done(2 * i + j, "lo"))
                        back, m = earlier(j, 1, 2)
                        t.wait_ge(act.sem, act.done(i, "gate", m, back=back))
                        mixed(nc, ps[:, CR, :], w_hi, w_lo, RB_CR, head, j).then_inc(pe.sem, pe.step("cr", j))
                    back, m = earlier(n, len(H), NS)
                    t.wait_ge(act.sem, act.done(i, "relu", m, back=back))
                    c = RB_CK + f * 2 * P
                    mixed(nc, ps[:, H[n % 3], :], w_hi, w_lo, c, head, j).then_inc(pe.sem, pe.step("ck", n))
                    if n >= LAG:
                        down(i, n - LAG)
                    if n == 1:
                        head.start()
                        t.wait_ge(vec.sem, vec.done(i, "tail", 1, back=1))
                        head.tensor_tr(t, 2 * i + 1)
                    if j == 1 and f == 2:
                        tail(i, 0)
                down(i, NS - 2)
                head.start()
                t.wait_ge(vec.sem, vec.done(i, "tail", 0))
                head.tensor_tr(t, 2 * i + 2)
                down(i, NS - 1)
                tail(i, 1)

        @block.scalar
        def _(a):
            act.credit(a)
            head.act.credit(a)
            a.wait_ge(loaded, 32)
            head.start()
            head.scalar_hi(a, 0, 0)
            weights_in.scalar_part(a)

            def part(i, n):
                back, m = earlier(n, RING, NS)
                a.wait_ge(pe.sem, pe.done(i, "down", m, back=back))
                a.wait_ge(pool.sem, pool.done(i, "sq", n))
                nc.scalar.activation(sq_hi[:, n % RING, :], sq[:, n % 2, :], ACT.Copy).then_inc(act.sem, act.step("sq_hi", n))

            with a.Fori(0, PAIRS) as i:
                act.start()
                for n in range(NS):
                    j, f = divmod(n, FT)
                    if f == 0:
                        back, m = earlier(j, 1, 2)
                        a.wait_ge(pe.sem, pe.done(i, "cr", j))
                        if j == 0:
                            a.wait_ge(vec.sem, vec.done(i, "out", 1, back=1))
                            nc.scalar.activation(gate[:, :], ps[:, CR, :], ACT.Sigmoid).then_inc(act.sem, act.step("gate", 0))
                    back, m = earlier(n, 2, NS)
                    a.wait_ge(pool.sem, pool.done(i, "sq", m, back=back))
                    a.wait_ge(pe.sem, pe.done(i, "ck", n))
                    nc.scalar.activation(a_sb[:, n % 2, :], ps[:, H[n % 3], :], ACT.Relu).then_inc(act.sem, act.step("relu", n))
                    if n >= 1:
                        part(i, n - 1)
                    if n == NS - 1:
                        a.wait_ge(vec.sem, vec.done(i, "out", 0))
                        nc.scalar.activation(gate[:, :], ps[:, CR, :], ACT.Sigmoid).then_inc(act.sem, act.step("gate", 1))
                    if n == 1:
                        head.start()
                        head.scalar_hi(a, 2 * i + 1, 1)
                part(i, NS - 1)
                head.start()
                head.scalar_hi(a, 2 * i + 2, 0)

        @block.vector
        def _(d):
            vec.credit(d)
            head.vec.credit(d)
            head.low.credit(d)
            nc.vector.memset(head.hi[:, :, 0:1].bitcast(F32), 0.0).then_inc(fixed, 1)
            nc.vector.memset(head.lo[:, :, 0:1].bitcast(F32), 0.0).then_inc(fixed, 1)

            def before(k, par, seq):
                head.start()
                head.vector_stats(d, k, par, seq)
                head.vector_z(d, k, par, seq)

            before(0, 0, 0)
            head.vector_lo(d, 0, 0)
            weights_in.vector_part(d)

            def out(i, j):
                d.wait_ge(pe.sem, pe.done(i, "down", j * FT + FT - 1))
                d.wait_ge(act.sem, act.done(i, "gate", j))
                back, m = earlier(j, 1, 2)
                d.wait_ge(pe.sem, pe.done(i, "tail", m, back=back))
                nc.vector.tensor_tensor(out_sb[:, :], gate[:, :], ps[:, OUT, :], ALU.mult).then_inc(vec.sem, vec.step("out", j))

            def tail(i, j):
                d.wait_ge(pe.sem, pe.done(i, "tail", j))
                d.wait_ge(pool.sem, pool.done(i, "added", j))
                at = cut((2 * i + j) * T, T)
                nc.vector.tensor_tensor(core.x[:, at], core.x[:, at], ps[:, TR, :], ALU.add).then_inc(vec.sem, vec.step("tail", j))

            def part(i, n):
                d.wait_ge(act.sem, act.done(i, "sq_hi", n))
                nc.vector.tensor_tensor(sq_lo[:, n % RING, :], sq[:, n % 2, :], sq_hi[:, n % RING, :],
                                        ALU.subtract).then_inc(vec.sem, vec.step("sq_lo", n))

            with d.Fori(0, PAIRS) as i:
                vec.start()
                before(2 * i + 1, 1, 2 * i + 1)
                for n in range(NS):
                    j, f = divmod(n, FT)
                    if n >= 1:
                        part(i, n - 1)
                    if n == 2:
                        head.vector_lo(d, 2 * i + 1, 1)
                    if n == 4:
                        head.start()
                        head.vector_stats(d, 2 * i + 2, 0, (2 * i + 2) % NSEQ)
                    if n == 5:
                        out(i, 0)
                    if n == 6:
                        head.vector_z(d, 2 * i + 2, 0, (2 * i + 2) % NSEQ)
                        tail(i, 0)
                part(i, NS - 1)
                head.vector_lo(d, 2 * i + 2, 0)
                out(i, 1)
                tail(i, 1)

        @block.gpsimd
        def _(p):
            pool.credit(p)
            head.pool.credit(p)
            head.start()
            head.pool_scale(p, 0, 0)
            weights_in.gpsimd_part(p)
            with p.Fori(0, PAIRS) as i:
                pool.start()
                head.start()
                head.pool_scale(p, 2 * i + 1, 1)
                for n in range(NS):
                    j, f = divmod(n, FT)
                    p.wait_ge(act.sem, act.done(i, "relu", n))
                    back, m = earlier(n, 2, NS)
                    p.wait_ge(vec.sem, vec.done(i, "sq_lo", m, back=back))
                    nc.gpsimd.tensor_tensor(sq[:, n % 2, :], a_sb[:, n % 2, :], a_sb[:, n % 2, :], ALU.mult).then_inc(pool.sem, pool.step("sq", n))
                    if f == 1:
                        at = cut((2 * i + j) * T, T)
                        nc.gpsimd.tensor_tensor(core.x[:, at], core.x[:, at], core.x2[:, at], ALU.add).then_inc(pool.sem, pool.step("added", j))
                    if n == 4:
                        head.start()
                        head.pool_scale(p, 2 * i + 2, 0)


def rwkv_layer(core, ctx, name):
    d = core.dram
    with ExitStack() as own:
        scales = [(c + P * prev, c + P * prev + P, d["L0_attn_a_mix_" + m].unsqueeze(1)) + ("one minus",) * prev
                  for c, m in ((RA_K, "k"), (RA_V, "v"), (RA_R, "r")) for prev in (0, 1)]
        time_mix_block(core, name + "t", Weights(core, own, name + "a", "time_w", RA_COLS, scales))
    with ExitStack() as own:
        scales = [(c + P * prev, c + P * prev + P, d["L0_attn_a_cmix_" + m].unsqueeze(1)) + ("one minus",) * prev
                  for c, m in [(RB_CK + 2 * P * f, "k") for f in range(4)] + [(RB_CR, "r")] for prev in (0, 1)]
        channel_mix_block(core, name + "c", Weights(core, own, name + "b", "channel_w", RB_COLS, scales))


class Moe:

    def __init__(self, shared, experts, tiles):
        self.shared, self.experts, self.tiles = shared, experts, tiles
        self.slots = shared + experts
        self.w1 = 8
        self.w3 = self.w1 + self.slots * tiles * P
        self.w2 = self.w3 + self.slots * tiles * P
        self.cols = self.w2 + self.slots * tiles * P


MOE0 = Moe(1, 8, 1)
MOE1 = Moe(0, 8, 2)


def earlier(n, ring, total):
    if n >= ring:
        return 0, n - ring
    return 1, max(m for m in range(total) if m % ring == n % ring)


def moe_block(core, name, moe, weights_in, kind, src, add_to, bias, store=False):
    nc, plan, NE, HT = core.nc, core.plan, moe.slots, moe.tiles
    w_hi, w_lo = weights_in.hi, weights_in.lo
    NS = 2 * NE
    LAG, RING = 2, 4
    H1, H3, BC, OUT, TR, GATE = (0, 1), (2, 3), 4, 5, 6, 7
    ps = core.psum
    with ExitStack() as ctx:
        sb = lambda n, s, t=F32: ctx.enter_context(nc.sbuf_tensor(name + n, s, t))
        head = Head(core, ctx, name, kind, src, TR)
        vec, act = Steps(nc, ctx, plan, name + "_vector"), Steps(nc, ctx, plan, name + "_scalar")
        pe, pool = Steps(nc, ctx, plan, name + "_tensor"), Steps(nc, ctx, plan, name + "_pool")
        stored = core_semaphore(nc, name + "_stored")
        bias_loaded = core_semaphore(nc, name + "_bias_loaded")
        bias_sb = sb("bias", [P, 8]) if bias is not None else None
        logits, top, idx = sb("logits", [P, NQ, 8]), sb("top", [P, NQ, 8]), sb("idx", [P, NQ, 8], U32)
        ex = sb("ex", [P, NQ, 8])
        lmax, lsum = sb("lmax", [P, NQ]), sb("lsum", [P, NQ])
        idxf, diff, e2, den, p1, p2 = (sb(n, s) for n, s in (("idxf", [P, NQ, 2]), ("diff", [P, NQ]), ("e2", [P, NQ]),
                                                             ("den", [P, NQ]), ("p1", [P, NQ]), ("p2", [P, NQ])))
        hot1, hot2 = sb("hot1", [P, NQ, 8]), sb("hot2", [P, NQ, 8])
        comb = sb("comb", [P, 2, NQ, 8])
        bcs = sb("bcs", [P, 2, T])
        s = sb("s", [P, 2, HT, T])
        sc = sb("sc", [P, 2, HT, T])
        g = sb("g", [P, 2, HT, T])
        g_hi, g_lo = sb("g_hi", [P, RING, HT, T], F32R), sb("g_lo", [P, RING, HT, T], F32R)
        out_sb = sb("out_sb", [P, T])
        block = ctx.enter_context(nc.Block())

        def is_shared(n):
            return n % NE < moe.shared

        def on_vector(n):
            return bias is not None or n % NE == 1

        def late_c(n):
            return n % NE == moe.shared

        def scaled(i, n, h, back=0):
            by = vec if on_vector(n) else pool
            return by.sem, by.done(i, "sc", n * HT + h, back=back)

        def prev_scaled(n, ring=1):
            m, back = n - ring, 0
            while True:
                if m < 0:
                    m, back = m + NS, 1
                if not is_shared(m):
                    return back, m
                m -= ring

        def gate_tensor(t, k, par):
            h = head
            t.wait_ge(h.act.sem, h.act.done(k, "hi"))
            t.wait_ge(h.low.sem, h.low.done(k, "lo"))
            t.wait_ge(h.vec.sem, h.vec.done(k, "logits", back=1))
            for q in range(NQ):
                c = slice(q * P, (q + 1) * P)
                ins = product3(nc, ps[:, GATE, q * 8:q * 8 + 8], h.hi[:, par, c], h.lo[:, par, c], w_hi[:, 0:8], w_lo[:, 0:8])
            ins.then_inc(h.pe.sem, h.pe.step("gate"))

        def gate_logits(d, k):
            h, v, n = head, head.vec, nc.vector
            inc = lambda ins, *key: ins.then_inc(v.sem, v.step(*key))
            wait = lambda *key: d.wait_ge(v.sem, v.done(k, *key))
            gate = ps[:, GATE, 0:NQ * 8].rearrange("p (q e) -> p q e", e=8)
            d.wait_ge(h.pe.sem, h.pe.done(k, "gate"))
            if bias is None:
                inc(n.tensor_copy(logits[:, :, :], gate), "logits")
            else:
                inc(n.tensor_tensor(logits[:, :, :], gate, bias_sb[:, :].unsqueeze(1).to_broadcast([P, NQ, 8]), ALU.add), "logits")
                wait("logits")
                inc(n.tensor_reduce(lmax[:, :], logits[:, :, :], AXX, ALU.max), "lmax")
                wait("lmax")
                inc(n.tensor_tensor(hot1[:, :, :], logits[:, :, :], wide(lmax[:, :]), ALU.subtract), "shifted")
                wait("shifted")
                inc(n.tensor_scalar(hot2[:, :, :], hot1[:, :, :], LOG2E, None, ALU.mult), "shifted2")

        def gate_choice(d, k):
            h, v, n = head, head.vec, nc.vector
            inc = lambda ins, *key: ins.then_inc(v.sem, v.step(*key))
            wait = lambda *key: d.wait_ge(v.sem, v.done(k, *key))
            if bias is None:
                wait("logits")
            else:
                d.wait_ge(h.pool.sem, h.pool.done(k, "ex", NQ - 1))
                inc(n.reduce_sum(lsum[:, :], ex[:, :, :], AXX), "lsum")
                wait("lsum")
                inc(n.reciprocal(den[:, :], lsum[:, :]), "lrec")
                wait("lrec")
                inc(n.tensor_tensor(logits[:, :, :], ex[:, :, :], wide(den[:, :]), ALU.mult), "rw")
                wait("rw")
            settle(core, d)
            for q in range(NQ):
                inc(n.max(top[:, q, :], logits[:, q, :]), "top", q)
            wait("top", NQ - 1)
            settle(core, d)
            inc(n.tensor_tensor(diff[:, :], top[:, :, 1], top[:, :, 0], ALU.subtract), "diff")
            for q in range(NQ):
                inc(n.max_index(idx[:, q, :], top[:, q, :], logits[:, q, :]), "idx", q)
            wait("diff")
            inc(n.tensor_scalar(p1[:, :], diff[:, :], LOG2E, None, ALU.mult), "diff2")
            wait("idx", NQ - 1)
            inc(n.tensor_copy(idxf[:, :, :], idx[:, :, 0:2]), "idxf")
            wait("idxf")
            it = core.iota[:, :].unsqueeze(1).to_broadcast([P, NQ, 8])
            inc(n.tensor_tensor(hot1[:, :, :], idxf[:, :, 0:1].to_broadcast([P, NQ, 8]), it, ALU.is_equal), "hot1")
            inc(n.tensor_tensor(hot2[:, :, :], idxf[:, :, 1:2].to_broadcast([P, NQ, 8]), it, ALU.is_equal), "hot2")

        def gate_weights(d, k, par):
            h, v, n = head, head.vec, nc.vector
            inc = lambda ins, *key: ins.then_inc(v.sem, v.step(*key))
            wait = lambda *key: d.wait_ge(v.sem, v.done(k, *key))
            d.wait_ge(h.pool.sem, h.pool.done(k, "e2"))
            inc(n.tensor_scalar(den[:, :], e2[:, :], 1.0, None, ALU.add), "den")
            wait("den")
            inc(n.reciprocal(p1[:, :], den[:, :]), "p1")
            wait("p1")
            inc(n.tensor_tensor(p2[:, :], p1[:, :], e2[:, :], ALU.mult), "p2")
            inc(n.tensor_tensor(hot1[:, :, :], hot1[:, :, :], wide(p1[:, :]), ALU.mult), "c1")
            wait("p2")
            inc(n.tensor_tensor(hot2[:, :, :], hot2[:, :, :], wide(p2[:, :]), ALU.mult), "c2")
            wait("c2")
            inc(n.tensor_tensor(comb[:, par, :, :], hot1[:, :, :], hot2[:, :, :], ALU.add), "comb")

        def wide(a):
            return a.unsqueeze(2).to_broadcast([P, NQ, 8])

        def gate_exp(p, k, q):
            h, o = head, head.pool
            p.wait_ge(h.vec.sem, h.vec.done(k, "shifted2"))
            nc.gpsimd.tensor_tensor(ex[:, q, :], core.two[:, 0:8], hot2[:, q, :], ALU.pow).then_inc(o.sem, o.step("ex", q))

        def gate_e2(p, k):
            h, o = head, head.pool
            p.wait_ge(h.vec.sem, h.vec.done(k, "diff2"))
            nc.gpsimd.tensor_tensor(e2[:, :], core.two[:, 0:NQ], p1[:, :], ALU.pow).then_inc(o.sem, o.step("e2"))

        E_STATS, E_Z, E_TR, E_GATE, E_CHOICE = 0, 1, 3, 4, NE - 1 if moe.shared else NE - 2
        E_WEIGHTS = 0 if moe.shared else NE - 1

        @block.sync
        def _(sp):
            if bias is not None:
                sp.dma_start(bias_sb[:, :], bias.unsqueeze(0).to_broadcast([P, 8])).then_inc(bias_loaded, 16)
            weights_in.sync_part(sp)
            if store:
                tokens = core.dram["out"].rearrange("b (q p) d -> p (b q) d", p=P)
                with sp.Fori(0, PAIRS) as i:
                    for j in range(2):
                        sp.wait_ge(vec.sem, vec.done(i, "tail", j))
                        at = cut((2 * i + j) * T, T)
                        sp.dma_start(tokens[:, cut((2 * i + j) * NQ, NQ), :], core.x[:, at].rearrange("p (q d) -> p q d", d=P)
                                     ).then_inc(stored, 16)
                sp.wait_ge(stored, 16 * NSEQ)

        @block.tensor
        def _(t):
            pe.credit(t)
            head.pe.credit(t)
            head.pe.start()
            head.tensor_tr(t, 0)
            weights_in.tensor_part(t, first=1)
            gate_tensor(t, 0, 0)
            weights_in.tensor_part(t)

            def up(i, n):
                j, e = divmod(n, NE)
                hi, lo = head.hi[:, j, :], head.lo[:, j, :]
                if e == 0:
                    t.wait_ge(head.low.sem, head.low.done(2 * i + j, "lo"))
                if not is_shared(n) and not late_c(n):
                    broadcast_c(i, n)
                for h in range(HT):
                    up_products(i, n, h, hi, lo)
                if late_c(n):
                    broadcast_c(i, n)

            def broadcast_c(i, n):
                j, e = divmod(n, NE)
                if e == moe.shared:
                    t.wait_ge(head.vec.sem, head.vec.done(2 * i + j, "comb"))
                back, m = prev_scaled(n)
                t.wait_ge(act.sem, act.done(i, "bc", m, back=back))
                for q in range(NQ):
                    ins = nc.tensor.transpose(ps[:, BC, q * P:(q + 1) * P],
                                              comb[:, j, q, e - moe.shared:e - moe.shared + 1].to_broadcast([P, P]),
                                              core.ident[:, :])
                ins.then_inc(pe.sem, pe.step("bc", n))

            def up_products(i, n, h, hi, lo):
                j, e = divmod(n, NE)
                u = n * HT + h
                c = e * HT * P + h * P
                back, m = earlier(u, 2, NS * HT)
                t.wait_ge(act.sem, act.done(i, "silu", m, back=back))
                product(nc, ps[:, H1[u % 2], :], w_hi[:, moe.w1 + c:moe.w1 + c + P], w_lo[:, moe.w1 + c:moe.w1 + c + P],
                        hi, lo).then_inc(pe.sem, pe.step("h1", u))
                t.wait_ge(vec.sem, vec.done(i, "g", m, back=back))
                product(nc, ps[:, H3[u % 2], :], w_hi[:, moe.w3 + c:moe.w3 + c + P], w_lo[:, moe.w3 + c:moe.w3 + c + P],
                        hi, lo).then_inc(pe.sem, pe.step("h3", u))

            def down(i, n):
                j, e = divmod(n, NE)
                if e == 0:
                    back, m = earlier(j, 1, 2)
                    t.wait_ge(act.sem, act.done(i, "out", m, back=back))
                for h in range(HT):
                    u = n * HT + h
                    c = moe.w2 + e * HT * P + h * P
                    t.wait_ge(vec.sem, vec.done(i, "g_lo", u))
                    ins = product(nc, ps[:, OUT, :], w_hi[:, c:c + P], w_lo[:, c:c + P], g_hi[:, n % RING, h, :],
                                  g_lo[:, n % RING, h, :], start=(e == 0 and h == 0), stop=(e == NE - 1 and h == HT - 1))
                ins.then_inc(pe.sem, pe.step("down", n))

            def tail(i, j):
                t.wait_ge(act.sem, act.done(i, "out", j))
                t.wait_ge(head.low.sem, head.low.done(2 * i + j + 1, "lo"))
                for q in range(NQ):
                    ins = nc.tensor.transpose(ps[:, TR, q * P:(q + 1) * P], out_sb[:, q * P:(q + 1) * P], core.ident[:, :])
                ins.then_inc(pe.sem, pe.step("tail", j))

            with t.Fori(0, PAIRS) as i:
                pe.start()
                for n in range(NS):
                    j, e = divmod(n, NE)
                    up(i, n)
                    if n >= LAG:
                        down(i, n - LAG)
                    if j == 1 and e == LAG:
                        tail(i, 0)
                    if e == E_TR:
                        head.pe.start()
                        t.wait_ge(vec.sem, vec.done(i, "tail", 0) if j else vec.done(i, "tail", 1, back=1))
                        head.tensor_tr(t, 2 * i + j + 1)
                    if e == E_GATE:
                        gate_tensor(t, 2 * i + j + 1, 1 - j)
                for n in range(NS - LAG, NS):
                    down(i, n)
                tail(i, 1)

        @block.scalar
        def _(a):
            act.credit(a)
            head.act.credit(a)
            head.act.start()
            head.scalar_hi(a, 0, 0)
            weights_in.scalar_part(a)

            def g_part(i, n, h):
                u = n * HT + h
                back, m = earlier(n, RING, NS)
                a.wait_ge(vec.sem, vec.done(i, "g", u))
                a.wait_ge(pe.sem, pe.done(i, "down", m, back=back))
                nc.scalar.activation(g_hi[:, n % RING, h, :], g[:, n % 2, h, :], ACT.Copy).then_inc(act.sem, act.step("g_hi", u))

            def out(i, j):
                a.wait_ge(pe.sem, pe.done(i, "down", (j + 1) * NE - 1))
                back, m = earlier(j, 1, 2)
                a.wait_ge(pe.sem, pe.done(i, "tail", m, back=back))
                nc.scalar.activation(out_sb[:, :], ps[:, OUT, :], ACT.Copy).then_inc(act.sem, act.step("out", j))

            def broadcast_c(i, n):
                a.wait_ge(pe.sem, pe.done(i, "bc", n))
                back, m = prev_scaled(n, 2)
                a.wait_ge(*scaled(i, m, HT - 1, back))
                nc.scalar.activation(bcs[:, n % 2, :], ps[:, BC, :], ACT.Copy).then_inc(act.sem, act.step("bc", n))

            with a.Fori(0, PAIRS) as i:
                act.start()
                for n in range(NS):
                    j, e = divmod(n, NE)
                    if not is_shared(n) and not late_c(n):
                        broadcast_c(i, n)
                    for h in range(HT):
                        u = n * HT + h
                        a.wait_ge(pe.sem, pe.done(i, "h1", u))
                        back, m = earlier(n, 2, NS)
                        if is_shared(m):
                            a.wait_ge(vec.sem, vec.done(i, "g", m * HT + h, back=back))
                        else:
                            a.wait_ge(*scaled(i, m, h, back))
                        nc.scalar.activation(s[:, n % 2, h, :], ps[:, H1[u % 2], :], ACT.Silu).then_inc(act.sem, act.step("silu", u))
                        if n > 0:
                            g_part(i, n - 1, h)
                    if late_c(n):
                        broadcast_c(i, n)
                    if j == 1 and e == LAG - 1:
                        out(i, 0)
                    if e == E_TR:
                        head.act.start()
                        head.scalar_hi(a, 2 * i + j + 1, 1 - j)
                for h in range(HT):
                    g_part(i, NS - 1, h)
                out(i, 1)

        @block.gpsimd
        def _(p):
            pool.credit(p)
            head.pool.credit(p)

            head.pool.start()
            head.pool_scale(p, 0, 0)
            for q in range(NQ if bias is not None else 0):
                gate_exp(p, 0, q)
            gate_e2(p, 0)
            with p.Fori(0, PAIRS) as i:
                pool.start()
                for n in range(NS):
                    j, e = divmod(n, NE)
                    if not is_shared(n) and not on_vector(n):
                        for h in range(HT):
                            u = n * HT + h
                            p.wait_ge(act.sem, act.done(i, "bc", n) if late_c(n) else act.done(i, "silu", u))
                            back, m = earlier(n, 2, NS)
                            p.wait_ge(vec.sem, vec.done(i, "g", m * HT + h, back=back))
                            nc.gpsimd.tensor_tensor(sc[:, n % 2, h, :], s[:, n % 2, h, :], bcs[:, n % 2, :],
                                                    ALU.mult).then_inc(pool.sem, pool.step("sc", u))
                    if e == 1 and add_to is not None:
                        at = cut((2 * i + j) * T, T)
                        nc.gpsimd.tensor_tensor(add_to[:, at], add_to[:, at], src[:, at], ALU.add).then_inc(pool.sem, pool.step("added", j))
                    if e == E_STATS:
                        head.pool.start()
                        head.pool_scale(p, 2 * i + j + 1, 1 - j)
                    if bias is not None and e == E_GATE + 1:
                        for q in range(NQ):
                            gate_exp(p, 2 * i + j + 1, q)
                    if e == E_CHOICE:
                        gate_e2(p, 2 * i + j + 1)

        @block.vector
        def _(d):
            vec.credit(d)
            head.vec.credit(d)
            head.low.credit(d)
            head.start()
            head.vector_stats(d, 0, 0, 0)
            head.vector_z(d, 0, 0, 0)
            head.vector_lo(d, 0, 0)
            weights_in.vector_part(d, slice(0, 1))
            if bias is not None:
                d.wait_ge(bias_loaded, 16)
            gate_logits(d, 0)
            weights_in.vector_part(d, slice(1, None))
            gate_choice(d, 0)
            if not moe.shared:
                gate_weights(d, 0, 0)

            def g_lo_part(i, n, h):
                u = n * HT + h
                d.wait_ge(act.sem, act.done(i, "g_hi", u))
                nc.vector.tensor_tensor(g_lo[:, n % RING, h, :], g[:, n % 2, h, :], g_hi[:, n % RING, h, :],
                                        ALU.subtract).then_inc(vec.sem, vec.step("g_lo", u))

            def tail(i, j):
                d.wait_ge(pe.sem, pe.done(i, "tail", j))
                if add_to is not None:
                    d.wait_ge(pool.sem, pool.done(i, "added", j))
                seq = 2 * i + j
                nc.vector.tensor_tensor(core.x[:, cut(seq * T, T)], core.x[:, cut(seq * T, T)], ps[:, TR, :],
                                        ALU.add).then_inc(vec.sem, vec.step("tail", j))

            with d.Fori(0, PAIRS) as i:
                vec.start()
                for n in range(NS):
                    j, e = divmod(n, NE)
                    for h in range(HT):
                        u = n * HT + h
                        if is_shared(n):
                            d.wait_ge(act.sem, act.done(i, "silu", u))
                        elif on_vector(n):
                            d.wait_ge(act.sem, act.done(i, "bc", n) if late_c(n) else act.done(i, "silu", u))
                            nc.vector.tensor_tensor(sc[:, n % 2, h, :], s[:, n % 2, h, :], bcs[:, n % 2, :],
                                                    ALU.mult).then_inc(vec.sem, vec.step("sc", u))
                            d.wait_ge(*scaled(i, n, h))
                        else:
                            d.wait_ge(*scaled(i, n, h))
                        d.wait_ge(pe.sem, pe.done(i, "h3", u))
                        back, m = earlier(n, 2, NS)
                        d.wait_ge(vec.sem, vec.done(i, "g_lo", m * HT + h, back=back))
                        nc.vector.tensor_tensor(g[:, n % 2, h, :], (s if is_shared(n) else sc)[:, n % 2, h, :],
                                                ps[:, H3[u % 2], :], ALU.mult).then_inc(vec.sem, vec.step("g", u))
                        if n > 0:
                            g_lo_part(i, n - 1, h)
                    if j == 1 and e == LAG:
                        tail(i, 0)
                    seq = 2 * i + 1 if j == 0 else (2 * i + 2) % NSEQ
                    if moe.shared and e == E_WEIGHTS:
                        gate_weights(d, 2 * i + j, j)
                    if e == E_STATS:
                        head.start()
                        head.vector_stats(d, 2 * i + j + 1, 1 - j, seq)
                    if e == E_Z:
                        head.vector_z(d, 2 * i + j + 1, 1 - j, seq)
                    if e == E_TR:
                        head.vector_lo(d, 2 * i + j + 1, 1 - j)
                    if e == E_GATE:
                        gate_logits(d, 2 * i + j + 1)
                    if e == E_CHOICE:
                        gate_choice(d, 2 * i + j + 1)
                    if not moe.shared and e == E_WEIGHTS:
                        gate_weights(d, 2 * i + j + 1, 1 - j)
                for h in range(HT):
                    g_lo_part(i, NS - 1, h)
                tail(i, 1)


def product3(nc, out, x_hi, x_lo, w_hi, w_lo):
    nc.tensor.matmul(out, x_hi, w_hi, start=True, stop=False)
    nc.tensor.matmul(out, x_lo, w_hi, start=False, stop=False)
    return nc.tensor.matmul(out, x_hi, w_lo, start=False, stop=True)


LAYERS = ['rwkv', 'attn0', 'moe0', 'alibi', 'attn0', 'moe0', 'light', 'moe1', 'diff', 'moe1']


def build(nc, dram, plan):
    with ExitStack() as ctx:
        core = Core(nc, ctx, plan, dram)
        for n, layer in enumerate(LAYERS):
            with ExitStack() as own:
                core.last = n == len(LAYERS) - 1
                LAYER_BLOCKS[layer](core, own, f"l{n}_{layer}")
            clear_semaphores(nc)


def moe1_layer(core, ctx, name):
    moe_block(core, name, MOE1, Weights(core, ctx, name + "w", "moe1_w", MOE1.cols), "ln", core.x, None, None,
              store=core.last)


def moe0_layer(core, ctx, name):
    weights = Weights(core, ctx, name + "w", "moe0_w", MOE0.cols, [(0, MOE0.w2, core.dram["L0_ffn_g2"].unsqueeze(1))])
    moe_block(core, name, MOE0, weights, "rms", core.x2, core.x, core.dram["L0_ffn_expert_bias"])


LAYER_BLOCKS = {"moe1": moe1_layer, "moe0": moe0_layer, "attn0": attn0_layer, "rwkv": rwkv_layer, "alibi": alibi_layer, "light": light_layer, "diff": diff_layer}


VECTORS = ["L0_attn_a_" + n for n in ("time_decay", "time_first", "ln1_g", "ln1_b", "ln2_g", "ln2_b", "mix_k", "mix_v", "mix_r",
                                      "cmix_k", "cmix_r")]
VECTORS += ["L0_attn_b_alibi_slope"]
VECTORS += ["L0_ffn_g1", "L0_ffn_g2", "L0_ffn_expert_bias"]

VECTORS += ["L1_attn_b_" + n for n in ("bv", "bp", "lambda_q1", "lambda_k1", "lambda_q2", "lambda_k2")]


def laid_out(inputs):
    import numpy as np
    f = lambda n: np.asarray(inputs[n])
    cat = lambda *a: np.ascontiguousarray(np.concatenate([x.reshape(P, -1) for x in a], axis=1))
    out = {"x": np.ascontiguousarray(f("L0_attn_a_x"))}
    for n in VECTORS:
        out[n] = np.ascontiguousarray(f(n).reshape(-1))
    w2 = f("L1_ffn_w2").reshape(8, 2, P, P).transpose(2, 0, 1, 3)
    out["moe1_w"] = cat(f("L1_ffn_w_gate"), f("L1_ffn_w1").transpose(1, 0, 2), f("L1_ffn_w3").transpose(1, 0, 2), w2)
    both = lambda s, e: np.concatenate([f(s)[None], f(e)], axis=0).transpose(2, 0, 1)
    out["moe0_w"] = cat(f("L0_ffn_Wr").T, both("L0_ffn_sW1", "L0_ffn_eW1"), both("L0_ffn_sW3", "L0_ffn_eW3"),
                        both("L0_ffn_sW2", "L0_ffn_eW2"))
    twice = lambda n: (f("L0_attn_a_" + n),) * 2
    out["time_w"] = cat(*twice("w_tk"), *twice("w_tv"), *twice("w_tr"))
    ck = f("L0_attn_a_w_ck").reshape(P, 4, 1, P).repeat(2, axis=2)
    out["channel_w"] = cat(ck, *twice("w_cr"), f("L0_attn_a_w_cv").reshape(4, P, P).transpose(1, 0, 2))
    wq = f("L0_ffn_Wq").T.reshape(P, A0_HEADS, 1, DK).repeat(3, axis=2)
    wk = f("L0_ffn_Wkc").T.reshape(P, 1, DK).repeat(3, axis=1)
    out["attn0_w"] = cat(wq, wk, f("L0_ffn_Wvc").T, f("L0_ffn_Wo").T)
    out["alibi_w"] = cat(f("L0_attn_b_W_qk"), f("L0_attn_b_W_v").T)
    lwq = f("L1_attn_a_Wq").T.reshape(P, 2, 2, 4, HD).transpose(0, 1, 3, 2, 4)
    lwk = f("L1_attn_a_Wk").T.reshape(P, 4, HD)
    swapped = (np.arange(HD) + HD // 2) % HD
    lwo = f("L1_attn_a_Wo").T.reshape(2, 2, 4, HD, P).transpose(1, 3, 0, 2, 4)
    out["light_w"] = cat(lwq, lwq[..., swapped], lwk, lwk[..., swapped], f("L1_attn_a_Wv").T, lwo)
    thrice = lambda n: f(n).T.reshape(P, D_GROUPS, 1, 32).repeat(3, axis=2)
    out["diff_w"] = cat(thrice("L1_attn_b_Wq"), thrice("L1_attn_b_Wk"), f("L1_attn_b_Wv").T, f("L1_attn_b_Wp").T)
    rows3 = lambda n: np.ascontiguousarray(np.tile(f(n).reshape(D_GROUPS, 32).T, (3, 1)))
    out["diff_bq"], out["diff_bk"] = rows3("L1_attn_b_bq"), rows3("L1_attn_b_bk")
    row, hh = np.arange(P)[:, None], np.arange(PER_GROUP)
    out["diff_head_rows"] = np.where(row < D_ROWS, row % 32 // DH == hh, row - D_ROWS == hh).astype(np.float32)
    slopes = np.array([2.0 ** (-8.0 / 16 * (h + 1)) for h in range(16)], dtype=np.float32)
    inv = 1.0 / 10000.0 ** (np.arange(0, HD, 2, dtype=np.float64) / HD)
    angle = np.outer(np.concatenate([inv, inv, inv, inv]), np.arange(T, dtype=np.float64))
    sign = np.where(np.arange(P) % HD < HD // 2, -1.0, 1.0)[:, None]
    out["rope_cos"] = np.cos(angle).astype(np.float32)
    out["rope_sin"] = (sign * np.sin(angle)).astype(np.float32)
    t = np.arange(P, dtype=np.float32)
    past = (t[None, :] - t[:, None])[:, None, :]
    out["light_mask"] = np.where(past >= 0, np.exp(-slopes[:, None] * np.maximum(past, 0)), np.float32(0)).astype(np.float32).reshape(P, 4, 4 * P)
    per_row = slopes.reshape(2, 2, 4).transpose(1, 0, 2).reshape(2, 1, 8).repeat(HD, axis=1).reshape(P, 8)
    out["light_q_dec"] = np.exp(-per_row[:, :, None] * (t + 1)).astype(np.float32).reshape(P, 8, 1, P)
    out["light_k_dec"] = np.exp(-slopes[None, :] * (P - 1 - t)[:, None]).astype(np.float32)
    out["light_blk_dec"] = np.exp(-per_row * P).astype(np.float32)
    key, query = np.arange(T, dtype=np.float32), np.arange(P, dtype=np.float32)[:, None]
    out["distance"] = np.concatenate([key - (query + P * q) for q in range(NQ)], axis=1)
    out["causal"] = np.where(key[:P] <= query, np.float32(0), np.float32(-3e38))
    out["ident"] = np.eye(P, dtype=np.float32)
    out["iota"] = np.ascontiguousarray(np.broadcast_to(np.arange(8, dtype=np.float32), (P, 8)))
    return out


def kernel(**inputs):
    import concourse.bacc as bacc
    from concourse.bass_utils import run_bass_kernel_spmd

    arrays = laid_out(inputs)
    plan = {}
    for final in (False, True):
        nc = bacc.Bacc("TRN2", target_bir_lowering=False, num_devices=1)
        dram = {n: nc.dram_tensor("in_" + n, a.shape, mybir.dt.from_np(a.dtype), kind="ExternalInput").ap()
                for n, a in arrays.items()}
        dram["out"] = nc.dram_tensor("out", (NSEQ, T, P), F32, kind="ExternalOutput").ap()
        build(nc, dram, plan)
    r = run_bass_kernel_spmd(nc, [{"in_" + n: a for n, a in arrays.items()}], core_ids=[0])
    return r.results[0]["out"]
```
